# Optimizing a Trainium2 kernel written in Bass

```python
import numpy as np
import jax
import jax.numpy as jnp

def _softmax(x, axis=-1):
    return jax.nn.softmax(x, axis=axis)

def _gelu(x):
    return jax.nn.gelu(x, approximate=True)

def _silu(x):
    return jax.nn.silu(x)

def _sigmoid(x):
    return jax.nn.sigmoid(x)

def _layernorm(x, axis=-1, eps=1e-05):
    m = jnp.mean(x, axis=axis, keepdims=True)
    v = jnp.var(x, axis=axis, keepdims=True)
    return (x - m) / jnp.sqrt(v + eps)

def _scatter_add(tgt, idx, src, axis=0):
    return tgt.at[idx].add(src)

def _segment_sum(src, seg, n):
    return jax.ops.segment_sum(src, seg, n)
kernel_name = 'mk_decoder_postln_d1_seqx_r8_95535d'

def setup_inputs(seed: int=0):
    np.random.seed(seed)
    _w = jnp.asarray

    def _rec_inputs():
        import jax
        import jax.numpy as jnp
        _rk = jax.random.key(seed)
        x = -0.0002928 + 1 * jax.random.normal(jax.random.fold_in(_rk, 1), (32, 64, 256), jnp.float32)
        _lenS = 64 - jax.random.randint(jax.random.fold_in(_rk, 7), (32,), 0, max(1, 64 // 4) + 1, jnp.int32)
        _lenS2 = 64 - jax.random.randint(jax.random.fold_in(_rk, 8), (32,), 0, max(1, 64 // 4) + 1, jnp.int32)
        _ctx_2048P = jax.random.normal(jax.random.fold_in(_rk, 11), (32, 16, 256), jnp.float32)
        _ctx_2048c = jax.random.dirichlet(jax.random.fold_in(_rk, 511), 0.3 * jnp.ones((16,), jnp.float32), (32, 64))
        _ctx_2048t = jnp.einsum('bsk,bkd->bsd', _ctx_2048c, _ctx_2048P)
        _ctx_2048t = _ctx_2048t * jax.lax.rsqrt(jnp.mean(jnp.square(_ctx_2048t)) + 1e-12) * 0.953939
        ctx_2048 = -1.39393e-06 + 0.999914 * (_ctx_2048t + 0.3 * jax.random.normal(jax.random.fold_in(_rk, 611), (32, 64, 256), jnp.float32))
        return (x, ctx_2048)
    x, ctx_2048 = _rec_inputs()

    def _L0_attn_setup():
        import jax, jax.numpy as jnp
        import numpy as np
        D_MODEL = 256
        D_STATE = 128
        B, S = (8, 128)
        SURPRISE_TEMP = 1.0
        SURPRISE_THR = 0.7
        IMPORTANCE_THR = 0.5
        C_DECAY = 8.0
        RMS_EPS = 1e-06

        def _l2norm(x, eps=1e-12):
            n = jnp.sqrt(jnp.sum(x * x, axis=-1, keepdims=True))
            return x / jnp.maximum(n, eps)

        def _forward(x, Wk, Wv, Wq, fast_lambda, slow_lambda, Waf, baf, Was, bas, nm_w1, nm_b1, nm_w2, nm_b2, ir_w1, ir_b1, ir_w2, ir_b2, pw_w, pw_b, Wo, norm_w):
            b, s, _ = x.shape
            d = Wk.shape[1]
            k = _l2norm(x @ Wk)
            v = x @ Wv
            q = _l2norm(x @ Wq)
            r_fast = jax.nn.sigmoid(x @ Waf + baf)
            r_slow = jax.nn.sigmoid(x @ Was + bas)
            log_af = jnp.log(jax.nn.sigmoid(fast_lambda) + 1e-08)
            log_as = jnp.log(jax.nn.sigmoid(slow_lambda) + 1e-08)
            alpha_fast = jnp.exp(C_DECAY * r_fast * log_af)
            alpha_slow = jnp.exp(C_DECAY * r_slow * log_as)
            importance = jax.nn.sigmoid(jax.nn.gelu(x @ ir_w1 + ir_b1, approximate=False) @ ir_w2 + ir_b2)
            path_w = jax.nn.softmax(x @ pw_w + pw_b, axis=-1)
            neural_update = jax.nn.gelu(v @ nm_w1 + nm_b1, approximate=False) @ nm_w2 + nm_b2

            def step(carry, inp):
                fH, sH, nS = carry
                k_t, v_t, q_t, af_t, as_t, imp_t, pw_t, nu_t = inp
                pred_fast = jnp.einsum('bq,bqv->bv', q_t, fH)
                pred_slow = jnp.einsum('bq,bqv->bv', q_t, sH)
                pred = (pred_fast + pred_slow) * 0.5
                err = jnp.sum((v_t - pred) ** 2, axis=-1, keepdims=True)
                surprise = jax.nn.sigmoid(err / (SURPRISE_TEMP + 1e-06))
                sur_e = surprise[:, :, None]
                kv = k_t[:, :, None] * v_t[:, None, :]
                kpf = jnp.einsum('bk,bkv->bv', k_t, fH)
                delta_fast = kv - k_t[:, :, None] * kpf[:, None, :]
                af = af_t[:, :, None]
                fH = af * fH + (1.0 - af) * (sur_e * delta_fast)
                upd_slow = (imp_t > IMPORTANCE_THR).astype(x.dtype)[:, :, None]
                kps = jnp.einsum('bk,bkv->bv', k_t, sH)
                delta_slow = kv - k_t[:, :, None] * kps[:, None, :]
                a_s = as_t[:, :, None]
                sH = a_s * sH + (1.0 - a_s) * upd_slow * (sur_e * delta_slow)
                upd_n = (surprise > SURPRISE_THR).astype(x.dtype)
                nS = nS + upd_n * (nu_t - nS) * 0.1
                out_f = jnp.einsum('bq,bqv->bv', q_t, fH)
                out_s = jnp.einsum('bq,bqv->bv', q_t, sH)
                out_t = pw_t[:, 0:1] * out_f + pw_t[:, 1:2] * out_s + pw_t[:, 2:3] * nS
                return ((fH, sH, nS), out_t)
            init = (jnp.zeros((b, d, d), x.dtype), jnp.zeros((b, d, d), x.dtype), jnp.zeros((b, d), x.dtype))
            xs = tuple((jnp.swapaxes(a, 0, 1) for a in (k, v, q, alpha_fast, alpha_slow, importance, path_w, neural_update)))
            _, outs = jax.lax.scan(step, init, xs)
            out = jnp.swapaxes(outs, 0, 1)
            of = out.astype(jnp.float32)
            of = of * jax.lax.rsqrt(jnp.mean(of * of, axis=-1, keepdims=True) + RMS_EPS)
            out = (of * norm_w).astype(out.dtype)
            return out @ Wo
        key = jax.random.key(seed)
        ks = jax.random.split(key, 24)
        std = 0.02
        p = {}
        p['x'] = jax.random.normal(ks[0], (B, S, D_MODEL), dtype=jnp.float32)
        p['Wk'] = jax.random.normal(ks[1], (D_MODEL, D_STATE)) * std
        p['Wv'] = jax.random.normal(ks[2], (D_MODEL, D_STATE)) * std
        p['Wq'] = jax.random.normal(ks[3], (D_MODEL, D_STATE)) * std
        p['fast_lambda'] = jax.random.uniform(ks[4], (D_STATE,), minval=2.0, maxval=4.0)
        p['slow_lambda'] = jax.random.uniform(ks[5], (D_STATE,), minval=6.0, maxval=10.0)
        p['Waf'] = jax.random.normal(ks[6], (D_MODEL, D_STATE)) * std
        p['baf'] = jnp.zeros((D_STATE,))
        p['Was'] = jax.random.normal(ks[7], (D_MODEL, D_STATE)) * std
        p['bas'] = jnp.zeros((D_STATE,))
        p['nm_w1'] = jax.random.normal(ks[8], (D_STATE, 2 * D_STATE)) * std
        p['nm_b1'] = jnp.zeros((2 * D_STATE,))
        p['nm_w2'] = jax.random.normal(ks[9], (2 * D_STATE, D_STATE)) * std
        p['nm_b2'] = jnp.zeros((D_STATE,))
        p['ir_w1'] = jax.random.normal(ks[10], (D_MODEL, D_STATE)) * std
        p['ir_b1'] = jnp.zeros((D_STATE,))
        p['ir_w2'] = jax.random.normal(ks[11], (D_STATE, 1)) * std
        p['ir_b2'] = jnp.zeros((1,))
        p['pw_w'] = jax.random.normal(ks[12], (D_MODEL, 3)) * std
        p['pw_b'] = jnp.zeros((3,))
        p['Wo'] = jax.random.normal(ks[13], (D_STATE, D_MODEL)) * std
        p['norm_w'] = jnp.ones((D_STATE,))
        return p
    _L0_attn_all = _L0_attn_setup()
    _L0_attn_in = {k: v for k, v in _L0_attn_all.items() if k in ('Wk', 'Wv', 'Wq', 'fast_lambda', 'slow_lambda', 'Waf', 'baf', 'Was', 'bas', 'nm_w1', 'nm_b1', 'nm_w2', 'nm_b2', 'ir_w1', 'ir_b1', 'ir_w2', 'ir_b2', 'pw_w', 'pw_b', 'Wo', 'norm_w')}
    del _L0_attn_all

    def _L0_xattn_setup():
        import jax, jax.numpy as jnp
        import numpy as np
        HEADS = 8
        DIM_HEAD = 64
        HIDDEN = HEADS * DIM_HEAD
        key = jax.random.key(seed)
        ks = jax.random.split(key, 5)
        b, dim, n = (4, 64, 256)
        ctx_dim, m = (64, 256)
        x = jax.random.normal(ks[0], (b, dim, n), dtype=jnp.float32)
        context = jax.random.normal(ks[1], (b, ctx_dim, m), dtype=jnp.float32)
        Wq = jax.random.normal(ks[2], (HIDDEN, dim), dtype=jnp.float32) / np.sqrt(dim).astype(np.float32)
        Wkv = jax.random.normal(ks[3], (2 * HIDDEN, ctx_dim), dtype=jnp.float32) / np.sqrt(ctx_dim).astype(np.float32)
        Wout = jax.random.normal(ks[4], (dim, HIDDEN), dtype=jnp.float32) / np.sqrt(HIDDEN).astype(np.float32)
        bout = jnp.zeros((dim,), dtype=jnp.float32)
        return {'x': x, 'context': context, 'Wq': Wq, 'Wkv': Wkv, 'Wout': Wout, 'bout': bout}
    _L0_xattn_all = _L0_xattn_setup()
    _L0_xattn_in = {k: v for k, v in _L0_xattn_all.items() if k in ('Wq', 'Wkv', 'Wout', 'bout')}
    del _L0_xattn_all

    def _L0_ffn_setup():
        import jax, jax.numpy as jnp
        import numpy as np
        TOPK = 6
        CAP = 128
        ROUTE_SCALE = 1.0
        key = jax.random.key(seed)
        k = jax.random.split(key, 6)
        B, T, C = (2, 256, 256)
        E, H, HS = (64, 32, 64)
        std = 0.01
        return {'x': jax.random.normal(k[0], (B, T, C), jnp.float32), 'w_gate': jax.random.normal(k[1], (C, E), jnp.float32) * std, 'w_shared_up': jax.random.normal(k[2], (C, 2 * HS), jnp.float32) * std, 'w_shared_down': jax.random.normal(k[3], (HS, C), jnp.float32) * std, 'w_up': jax.random.normal(k[4], (E, C, 2 * H), jnp.float32) * std, 'w_down': jax.random.normal(k[5], (E, H, C), jnp.float32) * std}
    _L0_ffn_all = _L0_ffn_setup()
    _L0_ffn_in = {k: v for k, v in _L0_ffn_all.items() if k in ('w_gate', 'w_shared_up', 'w_shared_down', 'w_up', 'w_down')}
    del _L0_ffn_all
    return {'x': x, 'ctx_2048': ctx_2048, 'L0_attn_Wk': _L0_attn_in['Wk'], 'L0_attn_Wv': _L0_attn_in['Wv'], 'L0_attn_Wq': _L0_attn_in['Wq'], 'L0_attn_fast_lambda': _L0_attn_in['fast_lambda'], 'L0_attn_slow_lambda': _L0_attn_in['slow_lambda'], 'L0_attn_Waf': _L0_attn_in['Waf'], 'L0_attn_baf': _L0_attn_in['baf'], 'L0_attn_Was': _L0_attn_in['Was'], 'L0_attn_bas': _L0_attn_in['bas'], 'L0_attn_nm_w1': _L0_attn_in['nm_w1'], 'L0_attn_nm_b1': _L0_attn_in['nm_b1'], 'L0_attn_nm_w2': _L0_attn_in['nm_w2'], 'L0_attn_nm_b2': _L0_attn_in['nm_b2'], 'L0_attn_ir_w1': _L0_attn_in['ir_w1'], 'L0_attn_ir_b1': _L0_attn_in['ir_b1'], 'L0_attn_ir_w2': _L0_attn_in['ir_w2'], 'L0_attn_ir_b2': _L0_attn_in['ir_b2'], 'L0_attn_pw_w': _L0_attn_in['pw_w'], 'L0_attn_pw_b': _L0_attn_in['pw_b'], 'L0_attn_Wo': _L0_attn_in['Wo'], 'L0_attn_norm_w': _L0_attn_in['norm_w'], 'L0_xattn_Wq': _L0_xattn_in['Wq'], 'L0_xattn_Wkv': _L0_xattn_in['Wkv'], 'L0_xattn_Wout': _L0_xattn_in['Wout'], 'L0_xattn_bout': _L0_xattn_in['bout'], 'L0_ffn_w_gate': _L0_ffn_in['w_gate'], 'L0_ffn_w_shared_up': _L0_ffn_in['w_shared_up'], 'L0_ffn_w_shared_down': _L0_ffn_in['w_shared_down'], 'L0_ffn_w_up': _L0_ffn_in['w_up'], 'L0_ffn_w_down': _L0_ffn_in['w_down']}

def reference(x, ctx_2048, L0_attn_Wk, L0_attn_Wv, L0_attn_Wq, L0_attn_fast_lambda, L0_attn_slow_lambda, L0_attn_Waf, L0_attn_baf, L0_attn_Was, L0_attn_bas, L0_attn_nm_w1, L0_attn_nm_b1, L0_attn_nm_w2, L0_attn_nm_b2, L0_attn_ir_w1, L0_attn_ir_b1, L0_attn_ir_w2, L0_attn_ir_b2, L0_attn_pw_w, L0_attn_pw_b, L0_attn_Wo, L0_attn_norm_w, L0_xattn_Wq, L0_xattn_Wkv, L0_xattn_Wout, L0_xattn_bout, L0_ffn_w_gate, L0_ffn_w_shared_up, L0_ffn_w_shared_down, L0_ffn_w_up, L0_ffn_w_down):
    import jax
    import jax.numpy as jnp

    def _L0_attn_ref(x, Wk, Wv, Wq, fast_lambda, slow_lambda, Waf, baf, Was, bas, nm_w1, nm_b1, nm_w2, nm_b2, ir_w1, ir_b1, ir_w2, ir_b2, pw_w, pw_b, Wo, norm_w):
        import jax, jax.numpy as jnp
        import numpy as np
        D_MODEL = 256
        D_STATE = 128
        B, S = (8, 128)
        SURPRISE_TEMP = 1.0
        SURPRISE_THR = 0.7
        IMPORTANCE_THR = 0.5
        C_DECAY = 8.0
        RMS_EPS = 1e-06

        def _l2norm(x, eps=1e-12):
            n = jnp.sqrt(jnp.sum(x * x, axis=-1, keepdims=True))
            return x / jnp.maximum(n, eps)

        def _forward(x, Wk, Wv, Wq, fast_lambda, slow_lambda, Waf, baf, Was, bas, nm_w1, nm_b1, nm_w2, nm_b2, ir_w1, ir_b1, ir_w2, ir_b2, pw_w, pw_b, Wo, norm_w):
            b, s, _ = x.shape
            d = Wk.shape[1]
            k = _l2norm(x @ Wk)
            v = x @ Wv
            q = _l2norm(x @ Wq)
            r_fast = jax.nn.sigmoid(x @ Waf + baf)
            r_slow = jax.nn.sigmoid(x @ Was + bas)
            log_af = jnp.log(jax.nn.sigmoid(fast_lambda) + 1e-08)
            log_as = jnp.log(jax.nn.sigmoid(slow_lambda) + 1e-08)
            alpha_fast = jnp.exp(C_DECAY * r_fast * log_af)
            alpha_slow = jnp.exp(C_DECAY * r_slow * log_as)
            importance = jax.nn.sigmoid(jax.nn.gelu(x @ ir_w1 + ir_b1, approximate=False) @ ir_w2 + ir_b2)
            path_w = jax.nn.softmax(x @ pw_w + pw_b, axis=-1)
            neural_update = jax.nn.gelu(v @ nm_w1 + nm_b1, approximate=False) @ nm_w2 + nm_b2

            def step(carry, inp):
                fH, sH, nS = carry
                k_t, v_t, q_t, af_t, as_t, imp_t, pw_t, nu_t = inp
                pred_fast = jnp.einsum('bq,bqv->bv', q_t, fH)
                pred_slow = jnp.einsum('bq,bqv->bv', q_t, sH)
                pred = (pred_fast + pred_slow) * 0.5
                err = jnp.sum((v_t - pred) ** 2, axis=-1, keepdims=True)
                surprise = jax.nn.sigmoid(err / (SURPRISE_TEMP + 1e-06))
                sur_e = surprise[:, :, None]
                kv = k_t[:, :, None] * v_t[:, None, :]
                kpf = jnp.einsum('bk,bkv->bv', k_t, fH)
                delta_fast = kv - k_t[:, :, None] * kpf[:, None, :]
                af = af_t[:, :, None]
                fH = af * fH + (1.0 - af) * (sur_e * delta_fast)
                upd_slow = (imp_t > IMPORTANCE_THR).astype(x.dtype)[:, :, None]
                kps = jnp.einsum('bk,bkv->bv', k_t, sH)
                delta_slow = kv - k_t[:, :, None] * kps[:, None, :]
                a_s = as_t[:, :, None]
                sH = a_s * sH + (1.0 - a_s) * upd_slow * (sur_e * delta_slow)
                upd_n = (surprise > SURPRISE_THR).astype(x.dtype)
                nS = nS + upd_n * (nu_t - nS) * 0.1
                out_f = jnp.einsum('bq,bqv->bv', q_t, fH)
                out_s = jnp.einsum('bq,bqv->bv', q_t, sH)
                out_t = pw_t[:, 0:1] * out_f + pw_t[:, 1:2] * out_s + pw_t[:, 2:3] * nS
                return ((fH, sH, nS), out_t)
            init = (jnp.zeros((b, d, d), x.dtype), jnp.zeros((b, d, d), x.dtype), jnp.zeros((b, d), x.dtype))
            xs = tuple((jnp.swapaxes(a, 0, 1) for a in (k, v, q, alpha_fast, alpha_slow, importance, path_w, neural_update)))
            _, outs = jax.lax.scan(step, init, xs)
            out = jnp.swapaxes(outs, 0, 1)
            of = out.astype(jnp.float32)
            of = of * jax.lax.rsqrt(jnp.mean(of * of, axis=-1, keepdims=True) + RMS_EPS)
            out = (of * norm_w).astype(out.dtype)
            return out @ Wo
        return _forward(x, Wk, Wv, Wq, fast_lambda, slow_lambda, Waf, baf, Was, bas, nm_w1, nm_b1, nm_w2, nm_b2, ir_w1, ir_b1, ir_w2, ir_b2, pw_w, pw_b, Wo, norm_w)

    def _L0_xattn_ref(x, context, Wq, Wkv, Wout, bout):
        import jax, jax.numpy as jnp
        import numpy as np
        HEADS = 8
        DIM_HEAD = 64
        HIDDEN = HEADS * DIM_HEAD
        b = x.shape[0]
        q = jnp.einsum('oc,bcn->bon', Wq, x)
        kv = jnp.einsum('oc,bcm->bom', Wkv, context)
        k, v = jnp.split(kv, 2, axis=1)
        split_heads = lambda t: t.reshape(b, HEADS, DIM_HEAD, t.shape[-1])
        q, k, v = (split_heads(q), split_heads(k), split_heads(v))
        sim = jnp.einsum('bhdi,bhdj->bhij', q, k)
        attn = jax.nn.softmax(sim, axis=-1)
        out = jnp.einsum('bhij,bhdj->bhid', attn, v)
        out = jnp.transpose(out, (0, 1, 3, 2)).reshape(b, HIDDEN, -1)
        return jnp.einsum('oc,bcn->bon', Wout, out) + bout[None, :, None]

    def _L0_ffn_ref(x, w_gate, w_shared_up, w_shared_down, w_up, w_down):
        import jax, jax.numpy as jnp
        import numpy as np
        TOPK = 6
        CAP = 128
        ROUTE_SCALE = 1.0
        B, T, C = x.shape
        E = w_gate.shape[1]
        x_flat = x.reshape(-1, C)
        N = x_flat.shape[0]
        su = x_flat @ w_shared_up
        y_s, g_s = jnp.split(su, 2, axis=-1)
        shared = jax.nn.silu(g_s) * y_s @ w_shared_down
        scores = jax.nn.sigmoid(x_flat @ w_gate)
        _, topk_idx = jax.lax.top_k(scores, TOPK)
        w = jnp.take_along_axis(scores, topk_idx, axis=-1)
        w = w / w.sum(-1, keepdims=True) * ROUTE_SCALE
        flat_e = topk_idx.reshape(-1)
        oh = jax.nn.one_hot(flat_e, E, dtype=jnp.int32)
        pos = jnp.take_along_axis(jnp.cumsum(oh, axis=0), flat_e[:, None], axis=1)[:, 0] - 1
        valid = pos < CAP
        pos_c = jnp.where(valid, pos, CAP - 1)
        token_ids = jnp.repeat(jnp.arange(N), TOPK)
        x_disp = jnp.zeros((E, CAP, C), x.dtype).at[flat_e, pos].set(x_flat[token_ids], mode='drop')
        up = jnp.einsum('ecd,edh->ech', x_disp, w_up)
        g_r, v_r = jnp.split(up, 2, axis=-1)
        h_r = jax.nn.silu(g_r) * v_r
        out_r = jnp.einsum('ech,ehd->ecd', h_r, w_down)
        y_ts = out_r[flat_e, pos_c]
        y_ts = jnp.where(valid[:, None], y_ts, 0.0)
        routed = (y_ts.reshape(N, TOPK, C) * w[:, :, None]).sum(axis=1)
        return (shared + routed).reshape(B, T, C)
    x = _layernorm(x + _L0_attn_ref(x, L0_attn_Wk, L0_attn_Wv, L0_attn_Wq, L0_attn_fast_lambda, L0_attn_slow_lambda, L0_attn_Waf, L0_attn_baf, L0_attn_Was, L0_attn_bas, L0_attn_nm_w1, L0_attn_nm_b1, L0_attn_nm_w2, L0_attn_nm_b2, L0_attn_ir_w1, L0_attn_ir_b1, L0_attn_ir_w2, L0_attn_ir_b2, L0_attn_pw_w, L0_attn_pw_b, L0_attn_Wo, L0_attn_norm_w), axis=-1)
    x = _layernorm(x + _L0_xattn_ref(x, ctx_2048, L0_xattn_Wq, L0_xattn_Wkv, L0_xattn_Wout, L0_xattn_bout), axis=-1)
    x = _layernorm(x + _L0_ffn_ref(x, L0_ffn_w_gate, L0_ffn_w_shared_up, L0_ffn_w_shared_down, L0_ffn_w_up, L0_ffn_w_down), axis=-1)
    return x

_drawn_inputs = setup_inputs


def setup_inputs(seed=0):
    import zlib

    import numpy as np

    out = dict(_drawn_inputs(seed))
    spreads = {'L0_attn_baf': (0.0, 2.0),
     'L0_attn_bas': (0.0, 0.8),
     'L0_attn_nm_b1': (0.0, 0.1),
     'L0_attn_nm_b2': (0.0, 0.1),
     'L0_attn_ir_b1': (0.0, 0.8),
     'L0_attn_pw_b': (0.0, 2.0),
     'L0_attn_norm_w': (1.0, 0.2),
     'L0_xattn_bout': (0.0, 2.0)}
    factors = {'L0_attn_fast_lambda': 22.224,
     'L0_attn_slow_lambda': 8.0,
     'L0_attn_Waf': 58.72,
     'L0_attn_Was': 8.0,
     'L0_attn_nm_w1': 3.99,
     'L0_attn_ir_w1': 8.0,
     'L0_attn_ir_w2': 8.0,
     'L0_ffn_w_gate': 8.0,
     'L0_ffn_w_shared_up': 8.0,
     'L0_ffn_w_shared_down': 8.0,
     'L0_ffn_w_up': 8.0,
     'L0_ffn_w_down': 8.0,
     'L0_attn_Wk': 8.0,
     'L0_attn_Wq': 8.0,
     'L0_attn_pw_w': 8.0}
    for name, (base, spread) in spreads.items():
        noise = np.random.default_rng([zlib.crc32(name.encode()), seed]).standard_normal(out[name].shape)
        drawn = base * np.exp(spread * noise) if base else spread * noise
        out[name] = jnp.asarray(drawn.astype(out[name].dtype))
    for name, factor in factors.items():
        out[name] = (out[name] * factor).astype(out[name].dtype)
    return out
```

```python
import numpy as np
from contextlib import ExitStack

import concourse.bass as bass
from concourse import mybir

F32 = mybir.dt.float32
F32R = mybir.dt.float32r
ACT = mybir.ActivationFunctionType
ALU = mybir.AluOpType
AX = mybir.AxisListType

P = 128
NB, NS, DM = 32, 64, 256
NT = NB * NS
KD = DM // P
TT = NT // P
CH = 4
NCH = NS // CH
CW = CH * NB
BW = 512
NBK = NT // BW
LN_EPS, RMS_EPS = 1e-5, 1e-6
PAIRS = [(s, n) for s in range(CH) for n in range(s + 1, CH)]
KQ_AT = [sum(CH - 1 - r for r in range(s)) for s in range(CH)]
O_AT = [sum(CH - r for r in range(s)) for s in range(CH)]
NKQ, NO = len(PAIRS), CH * (CH + 1) // 2


def memory_inputs(nc, ctx, pr, dram):
    sb = lambda n, s: ctx.enter_context(nc.sbuf_tensor(n, s, F32))
    sem = lambda n: ctx.enter_context(nc.semaphore(n))
    x_tok = sb("x_tok", [P, TT, DM])
    xT = sb("xT", [P, KD, NT])
    names = ["Waf", "Was", "ir_w1", "Wk", "Wq", "Wv"]
    w_in = {n: sb("w_" + n, [P, KD, P]) for n in names}
    nm_w1 = sb("nm_w1", [P, 2 * P])
    nm_w2 = sb("nm_w2", [P, 2, P])
    pw_w = sb("pw_w", [P, KD, 3])
    vec = sb("vec", [P, 16])
    BAF, BAS, NB1, NB2, IRB1, IRB2, IRW2, LAM, LOG, TINY = (
        vec[:, 0:1], vec[:, 1:2], vec[:, 2:4], vec[:, 4:5], vec[:, 5:6], vec[:, 6:7], vec[:, 7:8],
        vec[:, 8:10], vec[:, 10:12], vec[:, 12:13])
    pwb = sb("pwb", [P, 3])
    imp_w = sb("imp_w", [P, P])
    hid_i = sb("hid_i", [P, NT])
    hid_n = sb("hid_n", [P, 2, NT])
    sq = sb("sq", [P, 2, BW])
    nrm = sb("nrm", [P, 2, BW])
    upd = sb("upd", [P, NT])
    pwx = sb("pwx", [P, TT, 3])
    pws = sb("pws", [P, TT, 4])
    KQ, A, W, S, NU, pw, ident, ones = (pr[n] for n in ("KQ", "A", "W", "S", "NU", "pw", "ident", "ones"))
    bank = [ctx.enter_context(nc.psum_tensor(f"bank{i}", [P, BW], F32)) for i in range(6)]
    NBANK = len(bank)

    jobs = []
    for c in range(KD):
        for n in range(NBK):
            jobs.append(("xT", c, n, "act" if n % 2 else "dve"))
    for w in ("Waf", "Was", "ir_w1"):
        jobs += [(w, 0, n, "act") for n in range(NBK)]
    for w in ("Wk", "Wq", "Wv"):
        jobs += [(w, 0, n, "dve") for n in range(NBK)]
    jobs += [("norm", w, n, "act") for w in range(2) for n in range(NBK)]
    jobs += [("hid_n", m, n, "act") for n in range(NBK) for m in range(2)]
    jobs += [("imp", 0, n, "act") for n in range(NBK)]
    jobs += [("nu", 0, n, "act") for n in range(NBK)]
    jobs += [("pw", 0, 0, "dve")]
    order = {}
    count = {"act": 0, "dve": 0}
    for j, job in enumerate(jobs):
        count[job[3]] += 1
        order[j] = count[job[3]]
    place = {job[:3]: j for j, job in enumerate(jobs)}

    x_in = sem("x_in")
    w_loaded = sem("w_loaded")
    made = sem("bank_filled")
    freed = {"act": sem("bank_read_act"), "dve": sem("bank_read_dve")}
    consts = sem("consts_ready")
    squares = sem("squares_ready")
    roots = sem("roots_ready")
    act_own = sem("act_own")
    dve_own = sem("dve_own")
    pool_own = sem("pool_own")
    alpha = sem("alpha_ready")
    impw = sem("importance_weights_ready")
    keys = sem("keys_ready")
    vcopy = sem("values_copied")

    def filled(eng, job):
        eng.wait_ge(made, place[job] + 1)

    with nc.Block() as block:
        @block.sync
        def _(sp):
            sp.dma_start(x_tok[:, :, :], dram["x"].rearrange("b s d -> (b s) d")
                         .rearrange("(i p) d -> p i d", p=P)).then_inc(x_in, 16)
            for n in names:
                sp.dma_start(w_in[n][:, :, :], dram[n].rearrange("(c p) m -> p c m", p=P)).then_inc(w_loaded, 16)
            sp.dma_start(nm_w1[:, :], dram["nm_w1"]).then_inc(w_loaded, 16)
            sp.dma_start(nm_w2[:, :, :], dram["nm_w2"].rearrange("(c p) m -> p c m", p=P)).then_inc(w_loaded, 16)
            sp.dma_start(pw_w[:, :, :], dram["pw_w"].rearrange("(c p) m -> p c m", p=P)).then_inc(w_loaded, 16)
            col = lambda a: a.rearrange("(p o) -> p o", o=1)
            for to, a in ((BAF, col(dram["baf"])), (BAS, col(dram["bas"])), (NB2, col(dram["nm_b2"])),
                          (IRB1, col(dram["ir_b1"])), (IRW2, dram["ir_w2"]),
                          (LAM[:, 0:1], col(dram["fast_lambda"])), (LAM[:, 1:2], col(dram["slow_lambda"])),
                          (NB1[:, 0:1], col(dram["nm_b1"][0:P])), (NB1[:, 1:2], col(dram["nm_b1"][P:2 * P])),
                          (IRB2, dram["ir_b2"].partition_broadcast(P)),
                          (pwb[:, :], dram["pw_b"].partition_broadcast(P))):
                sp.dma_start(to, a).then_inc(w_loaded, 16)
        W_ALL = 16 * (len(names) + 3 + 11)

        @block.gpsimd
        def _(pool):
            pool.memset(ident[:, :], 0.0).then_inc(pool_own, 1)
            pool.memset(ones[:, :], 1.0).then_inc(consts, 1)
            pool.memset(TINY, 1e-8).then_inc(consts, 1)
            pool.wait_ge(pool_own, 1)
            pool.affine_select(out=ident[:, :], in_=ident[:, :], compare_op=ALU.not_equal, fill=1.0,
                               base=0, pattern=[[-1, P]], channel_multiplier=1).then_inc(consts, 1)
            for w in range(2):
                for n in range(NBK):
                    i = w * NBK + n
                    pool.wait_ge(freed["dve"], order[place[("Wk" if w == 0 else "Wq", 0, n)]])
                    if i >= 2:
                        pool.wait_ge(made, place[("norm", (i - 2) // NBK, (i - 2) % NBK)] + 1)
                    cols = KQ[:, w, n * BW:(n + 1) * BW]
                    pool.tensor_tensor(sq[:, i % 2, :], cols, cols, ALU.mult).then_inc(squares, 1)
            pool.wait_ge(freed["dve"], order[place[("Wv", 0, NBK - 1)]])
            pool.tensor_copy(S[:, 1, 0, :], S[:, 0, 0, :]).then_inc(vcopy, 1)
            pool.tensor_copy(S[:, 0, 1, :], S[:, 0, 0, :]).then_inc(vcopy, 1)
            pool.memset(S[:, 1, 1, :], 0.0).then_inc(vcopy, 1)
            pool.wait_ge(vcopy, 3)

        @block.tensor
        def _(pe):
            pe.wait_ge(consts, 3)
            for j, (what, c, n, _) in enumerate(jobs):
                ps = bank[j % NBANK]
                if j >= NBANK:
                    last = j - NBANK
                    pe.wait_ge(freed[jobs[last][3]], order[last])
                tok = slice(n * BW, (n + 1) * BW)
                if what == "xT":
                    if j == 0:
                        pe.wait_ge(x_in, 16)
                    for i in range(4):
                        mm = pe.transpose(ps[:, i * P:(i + 1) * P], x_tok[:, 4 * n + i, c * P:(c + 1) * P], ident[:, :])
                elif what in w_in:
                    if (what, n) == ("Waf", 0):
                        pe.wait_ge(w_loaded, W_ALL)
                        for e in ("act", "dve"):
                            pe.wait_ge(freed[e], KD * NBK // 2)
                    for k in range(KD):
                        mm = pe.matmul(ps[:, :], w_in[what][:, k, :], xT[:, k, tok], start=k == 0, stop=k == KD - 1)
                elif what == "norm":
                    pe.wait_ge(squares, c * NBK + n + 1)
                    mm = pe.matmul(ps[:, :], ones[:, :], sq[:, (c * NBK + n) % 2, :], start=True, stop=True)
                elif what == "hid_n":
                    pe.wait_ge(freed["dve"], order[place[("Wv", 0, n)]])
                    mm = pe.matmul(ps[:, :], nm_w1[:, c * P:(c + 1) * P], S[:, 0, 0, tok], start=True, stop=True)
                elif what == "imp":
                    pe.wait_ge(impw, 1)
                    pe.wait_ge(freed["act"], order[place[("ir_w1", 0, n)]])
                    mm = pe.matmul(ps[:, :], imp_w[:, :], hid_i[:, tok], start=True, stop=True)
                elif what == "nu":
                    pe.wait_ge(freed["act"], order[place[("hid_n", 1, n)]])
                    for k in range(2):
                        mm = pe.matmul(ps[:, :], nm_w2[:, k, :], hid_n[:, k, tok], start=k == 0, stop=k == 1)
                elif what == "pw":
                    for i in range(TT):
                        for k in range(KD):
                            mm = pe.matmul(ps[:, 3 * i:3 * i + 3], xT[:, k, i * P:(i + 1) * P], pw_w[:, k, :],
                                           start=k == 0, stop=k == KD - 1)
                mm.then_inc(made, 1)

        def empty_xT(eng, c, n, mine):
            copy = eng.activation if mine == "act" else eng.tensor_copy
            src = bank[place[("xT", c, n)] % NBANK][:, :].rearrange("p (b s) -> p s b", s=NS)
            dst = xT[:, c, :].rearrange("p (s b) -> p s b", b=NB)[:, :, 8 * n:8 * n + 8]
            if mine == "act":
                eng.activation(dst, src, ACT.Copy).then_inc(freed["act"], 1)
            else:
                eng.tensor_copy(dst, src).then_inc(freed["dve"], 1)

        @block.scalar
        def _(act):
            own = 0
            act.wait_ge(consts, 3)
            act.wait_ge(w_loaded, W_ALL)
            act.activation(LOG, LAM, ACT.Sigmoid).then_inc(act_own, 1)
            for (what, c, n, mine) in [j for j in jobs if j[3] == "act"]:
                ps = bank[place[(what, c, n)] % NBANK][:, :]
                tok = slice(n * BW, (n + 1) * BW)
                filled(act, (what, c, n))
                if what == "xT":
                    empty_xT(act, c, n, "act")
                elif what in ("Waf", "Was"):
                    m = 0 if what == "Waf" else 1
                    act.activation(A[:, m, tok], ps, ACT.Sigmoid, bias=(BAF, BAS)[m]).then_inc(freed["act"], 1)
                elif what == "ir_w1":
                    act.activation(hid_i[:, tok], ps, ACT.Gelu, bias=IRB1).then_inc(freed["act"], 1)
                elif what == "norm":
                    i = c * NBK + n
                    if i >= 2:
                        act.wait_ge(keys, i - 1)
                    act.activation(nrm[:, i % 2, :], ps, ACT.Sqrt).then_inc(freed["act"], 1)
                elif what == "hid_n":
                    act.activation(hid_n[:, c, tok], ps, ACT.Gelu, bias=NB1[:, c:c + 1]).then_inc(freed["act"], 1)
                elif what == "imp":
                    act.activation(upd[:, tok], ps, ACT.Sigmoid, bias=IRB2).then_inc(freed["act"], 1)
                elif what == "nu":
                    act.activation(NU[:, tok], ps, ACT.Identity, bias=NB2).then_inc(freed["act"], 1)
            act.wait_ge(act_own, 1)
            act.activation(LOG, LOG, ACT.Ln, bias=TINY).then_inc(act_own, 1)
            act.wait_ge(act_own, 2)
            act.activation(LOG, LOG, ACT.Copy, scale=8.0).then_inc(act_own, 1)
            act.wait_ge(act_own, 3)
            act.wait_ge(freed["act"], order[place[("Was", 0, NBK - 1)]])
            for m in range(2):
                act.activation(A[:, m, :], A[:, m, :], ACT.Exp, scale=LOG[:, m:m + 1]).then_inc(alpha, 1)
            act.wait_ge(roots, 1)
            act.activation(pwx[:, :, :], pwx[:, :, :], ACT.Exp).then_inc(alpha, 1)

        @block.vector
        def _(dve):
            own = 0
            dve.wait_ge(consts, 3)
            dve.wait_ge(w_loaded, W_ALL)
            dve.tensor_scalar(imp_w[:, :], ones[:, :], IRW2, None, ALU.mult).then_inc(impw, 1)
            for (what, c, n, mine) in [j for j in jobs if j[3] == "dve" and j[0] != "pw"]:
                ps = bank[place[(what, c, n)] % NBANK][:, :]
                tok = slice(n * BW, (n + 1) * BW)
                filled(dve, (what, c, n))
                if what == "xT":
                    empty_xT(dve, c, n, "dve")
                elif what == "Wv":
                    dve.tensor_copy(S[:, 0, 0, tok], ps).then_inc(freed["dve"], 1)
                else:
                    dve.tensor_copy(KQ[:, 0 if what == "Wk" else 1, tok], ps).then_inc(freed["dve"], 1)
            for w in range(2):
                for n in range(NBK):
                    i = w * NBK + n
                    part = nrm[:, i % 2, :]
                    dve.wait_ge(freed["act"], order[place[("norm", w, n)]])
                    dve.tensor_scalar(part, part, 1e-12, None, ALU.max).then_inc(dve_own, 1)
                    dve.wait_ge(dve_own, 2 * i + 1)
                    dve.reciprocal(part, part).then_inc(dve_own, 1)
                    dve.wait_ge(dve_own, 2 * i + 2)
                    cols = KQ[:, w, n * BW:(n + 1) * BW]
                    dve.scalar_tensor_tensor(cols, cols, 0.5 if w else 1.0, part, ALU.mult, ALU.mult)\
                       .then_inc(keys, 1)
            own = 4 * NBK
            def link(ins):
                nonlocal own
                own += 1
                ins.then_inc(dve_own, 1)
                dve.wait_ge(dve_own, own)
            filled(dve, ("pw", 0, 0))
            ps = bank[place[("pw", 0, 0)] % NBANK][:, 0:3 * TT].rearrange("p (i j) -> p i j", j=3)
            link(dve.tensor_tensor(pwx[:, :, :], ps, pwb[:, :].unsqueeze(1).broadcast_to((P, TT, 3)), ALU.add))
            link(dve.tensor_reduce(pws[:, :, 0:1], pwx[:, :, :], AX.X, ALU.max))
            dve.tensor_tensor(pwx[:, :, :], pwx[:, :, :], pws[:, :, 0:1].broadcast_to((P, TT, 3)),
                              ALU.subtract).then_inc(roots, 1)
            dve.wait_ge(alpha, 3)
            link(dve.tensor_reduce(pws[:, :, 1:2], pwx[:, :, :], AX.X, ALU.add))
            link(dve.reciprocal(pws[:, :, 2:3], pws[:, :, 1:2]))
            link(dve.tensor_tensor(pw[:, :, :], pwx[:, :, :], pws[:, :, 2:3].broadcast_to((P, TT, 3)), ALU.mult))
            dve.wait_ge(freed["act"], order[place[("imp", 0, NBK - 1)]])
            for m in range(2):
                link(dve.tensor_scalar(W[:, m, :], A[:, m, :], -1.0, 1.0, ALU.mult, ALU.add))
                dve.wait_ge(keys, NBK)
                link(dve.tensor_tensor(W[:, m, :], W[:, m, :], KQ[:, 0, :], ALU.mult))
            link(dve.scalar_tensor_tensor(W[:, 1, :], upd[:, :], 0.5, W[:, 1, :], ALU.is_gt, ALU.mult))


def recurrence(nc, ctx, pr):
    sb = lambda n, s: ctx.enter_context(nc.sbuf_tensor(n, s, F32))
    sem = lambda n: ctx.enter_context(nc.semaphore(n))
    KQ, A, W, S, NU, O, ident, ones = (pr[n] for n in ("KQ", "A", "W", "S", "NU", "O", "ident", "ones"))
    LV = {n: (n & -n) * CH for n in range(1, NCH)}
    HMAX = max(LV.values())
    nblk = lambda n: 2 * LV[n] // CH
    total = lambda n: sum(nblk(m) for m in range(1, n))
    groups = lambda n: -(-nblk(n) // 4)
    turned = lambda n: sum(groups(m) for m in range(1, n))
    gathers = lambda n: sum(2 * groups(m) for m in range(1, n) if LV[m] > CH)
    RING = 8

    Fd = sb("Fd", [P, 2, CH, CH, NB])
    PK = sb("PK", [P, 2, 2, NKQ, NB])
    PO = sb("PO", [P, 2, NO, NB])
    C = sb("C", [P, 2, 2, 2, NKQ, NB])
    CO = sb("CO", [P, 2, 2, NO, NB])
    DEC = sb("DEC", [P, 2, HMAX * NB])
    LW = sb("LW", [P, 2, HMAX * NB])
    LL = sb("LL", [P, 2, 3, HMAX * NB])
    G1 = sb("G1", [P, 2, 3 * P])
    G2 = sb("G2", [P, 2 * HMAX // CH, 3 * P])
    UG = sb("UG", [P, 2, 4, P])
    UT = sb("UT", [P, 2, 4, P])
    sqr = sb("sqr", [P, NB])
    perr = sb("perr", [P, NB])
    sur = sb("sur", [P, RING, NB])
    tk = sb("tk", [P, 2, CH, NB])
    tq = sb("tq", [P, 2, CH, NB])
    tq1 = sb("tq1", [P, 2, NB])
    to = sb("to", [P, 2, CH, NB])
    nst = sb("nst", [P, 3, NB])
    hs = sorted(set(LV.values()))
    sel = DEC[:, 0, 0:len(hs) * P].rearrange("p (i c) -> p i c", c=P)
    mask = {h: sb(f"mask{h}", [P, P]) for h in hs}
    psE = ctx.enter_context(nc.psum_tensor("psE", [P, BW], F32))
    psC = [ctx.enter_context(nc.psum_tensor(f"psC{i}", [P, BW], F32)) for i in range(2)]
    psG = [ctx.enter_context(nc.psum_tensor(f"psG{i}", [P, BW], F32)) for i in range(2)]
    psT = ctx.enter_context(nc.psum_tensor("psT", [P, BW], F32))
    psR = [ctx.enter_context(nc.psum_tensor(f"psR{i}", [P, BW], F32)) for i in range(2)]

    pool_own = sem("pool_own2")
    sel_ok = sem("selectors_ready")
    mask_psum = sem("masks_in_psum")
    masks = sem("masks_ready")
    sq_ready = sem("error_squares_ready")
    err_ready = sem("errors_ready")
    sur_ready = sem("surprises_ready")
    sur_read = sem("surprises_read")
    u_ready = sem("u_ready")
    mul_done = sem("coefficients_read")
    terms = sem("coefficient_terms_ready")
    coef = sem("coefficients_in_psum")
    coef_out = sem("coefficients_ready")
    lw_ready = sem("decayed_ready")
    g_psum = sem("blocks_in_psum")
    g_ready = sem("blocks_ready")
    ug_ready = sem("u_gathered")
    t_psum = sem("transposes_in_psum")
    t_ready = sem("transposes_ready")
    r_psum = sem("reads_in_psum")
    r_done = sem("reads_added")
    dve_own = sem("dve_own2")

    def g_slot(n, i):
        return G1[:, i, :] if LV[n] == CH else G2[:, i, :]

    def slices(n):
        b = nblk(n)
        return [range(b * i // CH, b * (i + 1) // CH) for i in range(CH)]

    cols = lambda t, n=1: slice(t * NB, (t + n) * NB)

    with nc.Block() as block:
        @block.gpsimd
        def _(pool):
            own = 0

            def link(ins):
                nonlocal own
                own += 1
                ins.then_inc(pool_own, 1)
                pool.wait_ge(pool_own, own)

            def terms_of(j):
                part = lambda x, k: x[:, :, cols(j * CH, CH)].rearrange("p m (t b) -> p m t b", b=NB)
                a_, w_, kq = part(A, 2), part(W, 2), part(KQ, 2)
                flat = Fd[:, :, :, :, :].rearrange("p m s t b -> p m (s t) b")
                link(pool.tensor_copy(flat[:, :, 0:CH * CH:CH + 1, :], w_))
                for l in range(1, CH):
                    n = CH - l
                    at = lambda k: slice(k, k + (n - 1) * (CH + 1) + 1, CH + 1)
                    link(pool.tensor_tensor(flat[:, :, at(l), :], flat[:, :, at(l - 1), :], a_[:, :, l:CH, :], ALU.mult))
                if j >= 1:
                    pool.wait_ge(coef, 4 * j)
                for s in range(CH - 1):
                    n = CH - 1 - s
                    for kind in range(2):
                        pool.tensor_tensor(PK[:, :, kind, KQ_AT[s]:KQ_AT[s] + n, :], Fd[:, :, s, s:CH - 1, :],
                                           kq[:, kind, s + 1:CH, :].unsqueeze(1).broadcast_to((P, 2, n, NB)), ALU.mult)
                for s in range(CH):
                    n = CH - s
                    mul = pool.tensor_tensor(PO[:, :, O_AT[s]:O_AT[s] + n, :], Fd[:, :, s, s:CH, :],
                                             kq[:, 1, s:CH, :].unsqueeze(1).broadcast_to((P, 2, n, NB)), ALU.mult)
                mul.then_inc(terms, 1)
                pool.wait_ge(terms, j + 1)

            def decays_of(n):
                h, c = LV[n], n * CH
                g = P // h
                if n >= 2:
                    pool.wait_ge(g_psum, total(n))
                link(pool.memset(DEC[:, :, cols(h - 1)], 1.0))
                for t in range(h - 2, -1, -1):
                    link(pool.tensor_tensor(DEC[:, :, cols(t)], DEC[:, :, cols(t + 1)], A[:, :, cols(c - h + t + 1)], ALU.mult))
                for m in range(2):
                    by_group = lambda x: x.rearrange("p (t g b) -> p t g b", t=h, b=g)
                    pool.tensor_tensor(LW[:, m, 0:h * NB].rearrange("p (g t b) -> p t g b", t=h, b=g),
                                       by_group(W[:, m, cols(c - h, h)]), by_group(DEC[:, m, 0:h * NB]), ALU.mult)
                link(pool.tensor_copy(LL[:, :, 0:2, 0:NB], KQ[:, :, cols(c)].unsqueeze(1).broadcast_to((P, 2, 2, NB))))
                link(pool.tensor_copy(DEC[:, :, cols(0)], A[:, :, cols(c)]))
                for t in range(1, h):
                    link(pool.tensor_tensor(DEC[:, :, cols(t)], DEC[:, :, cols(t - 1)], A[:, :, cols(c + t)], ALU.mult))
                for kind in range(2):
                    pool.tensor_tensor(LL[:, :, kind, NB:h * NB], DEC[:, :, 0:(h - 1) * NB],
                                       KQ[:, kind, cols(c + 1, h - 1)].unsqueeze(1).broadcast_to((P, 2, (h - 1) * NB)), ALU.mult)
                pool.tensor_tensor(LL[:, :, 2, 0:h * NB], DEC[:, :, 0:h * NB],
                                   KQ[:, 1, cols(c, h)].unsqueeze(1).broadcast_to((P, 2, h * NB)), ALU.mult).then_inc(lw_ready, 1)
                pool.wait_ge(lw_ready, n)

            def neural(t):
                nu = NU[:, cols(t)]
                pool.wait_ge(sur_ready, t + 1)
                pool.tensor_scalar(nst[:, 0, :], sur[:, t % RING, :], 0.7, 0.1, ALU.is_gt, ALU.mult).then_inc(sur_read, 1)
                pool.wait_ge(sur_read, t + 1)
                if t:
                    link(pool.tensor_tensor(nst[:, 1, :], nu, NU[:, cols(t - 1)], ALU.subtract))
                    link(pool.tensor_tensor(nst[:, 2, :], nst[:, 1, :], nst[:, 0, :], ALU.mult))
                    link(pool.tensor_tensor(nu, NU[:, cols(t - 1)], nst[:, 2, :], ALU.add))
                else:
                    link(pool.tensor_tensor(nu, nu, nst[:, 0, :], ALU.mult))

            link(pool.memset(O[:, :, :], 0.0))
            link(pool.memset(sel, 0.0))
            for i, h in enumerate(hs):
                g = P // h
                v = sel[0:g, i, :].rearrange("p (t b) -> p t b", b=g)
                pool.affine_select(out=v, in_=v, compare_op=ALU.not_equal, fill=1.0, base=0,
                                   pattern=[[0, h], [-1, g]], channel_multiplier=1).then_inc(sel_ok, 1)
            terms_of(0)
            pool.wait_ge(mask_psum, 1)
            decays_of(1)
            for j in range(NCH):
                if j + 1 < NCH:
                    terms_of(j + 1)
                if j + 2 < NCH:
                    decays_of(j + 2)
                for t in range(j * CH, (j + 1) * CH):
                    neural(t)

        def piece(x):
            j, i = divmod(x, 4)
            m = i % 2
            if i < 2:
                return (PK[:, m, :, :, :].rearrange("p k n b -> p (k n b)"),
                        C[:, j % 2, m, :, :, :].rearrange("p k n b -> p (k n b)"), 2 * NKQ * NB)
            return (PO[:, m, :, :].rearrange("p n b -> p (n b)"),
                    CO[:, j % 2, m, :, :].rearrange("p n b -> p (n b)"), NO * NB)

        @block.tensor
        def _(pe):
            def sum_piece(x):
                src, _, n = piece(x)
                pe.wait_ge(terms, x // 4 + 1)
                if x >= 2:
                    pe.wait_ge(coef_out, x - 1)
                pe.matmul(psC[x % 2][:, 0:n], ones[:, :], src, start=True, stop=True).then_inc(coef, 1)

            def make_block(n, i):
                h = LV[n]
                gi, m = divmod(i, 2)
                g = P // h
                k = total(n) + i
                pe.wait_ge(lw_ready, n)
                if k >= 2:
                    pe.wait_ge(g_ready, k - 1)
                rhs = LL[:, m, :, 0:h * NB].rearrange("p k (t b) -> p k t b", b=NB)[:, :, :, gi * g:(gi + 1) * g]
                pe.matmul(psG[k % 2][:, 0:3 * P], LW[:, m, gi * P:(gi + 1) * P], rhs, start=True, stop=True)\
                  .then_inc(g_psum, 1)

            def turn(n, gr):
                k = turned(n) + gr
                if k >= 1:
                    pe.wait_ge(t_ready, k)
                if LV[n] > CH:
                    pe.wait_ge(ug_ready, gathers(n) + 2 * (gr + 1))
                else:
                    pe.wait_ge(u_ready, n * CH)
                for i in range(min(4, nblk(n))):
                    src = S[:, i, 0, cols((n - 1) * CH, CH)] if LV[n] == CH else UG[:, k % 2, i, :]
                    mm = pe.transpose(psT[:, i * P:(i + 1) * P], src, ident[:, :])
                mm.then_inc(t_psum, 1)

            def read(n, gr):
                for i in range(4 * gr, min(4 * gr + 4, nblk(n))):
                    k = total(n) + i
                    pe.wait_ge(t_ready, turned(n) + gr + 1)
                    pe.wait_ge(g_ready, k + 1)
                    if k >= 2:
                        pe.wait_ge(r_done, k - 1)
                    pe.matmul(psR[k % 2][:, 0:3 * P], UT[:, (turned(n) + gr) % 2, i % 4, :], g_slot(n, i),
                              start=True, stop=True).then_inc(r_psum, 1)

            def boundary(n):
                for gr in range(groups(n)):
                    turn(n, gr)
                    if gr:
                        read(n, gr - 1)
                read(n, groups(n) - 1)

            pe.wait_ge(sel_ok, len(hs))
            for i, h in enumerate(hs):
                g = P // h
                mm = pe.matmul(psT[:, i * P:(i + 1) * P], sel[0:g, i, :], sel[0:g, i, :], start=True, stop=True)
            mm.then_inc(mask_psum, 1)
            pe.wait_ge(masks, len(hs))
            for x in range(4):
                sum_piece(x)
            for i in range(nblk(1)):
                make_block(1, i)
            for t in range(NS):
                j, i = divmod(t, CH)
                pe.wait_ge(sq_ready, t + 1)
                pe.matmul(psE[:, 0:NB], ones[:, :], sqr[:, :], start=True, stop=True).then_inc(err_ready, 1)
                if j + 1 < NCH:
                    sum_piece(4 * (j + 1) + i)
                if j + 2 < NCH:
                    for b in slices(j + 2)[i]:
                        make_block(j + 2, b)
                if i == CH - 1 and j + 1 < NCH:
                    boundary(j + 1)

        @block.scalar
        def _(act):
            def empty_piece(x):
                _, dst, n = piece(x)
                j = x // 4
                act.wait_ge(coef, x + 1)
                if j >= 2:
                    act.wait_ge(mul_done, (j - 1) * CH)
                act.activation(dst, psC[x % 2][:, 0:n], ACT.Copy).then_inc(coef_out, 1)

            for x in range(4):
                empty_piece(x)
            for t in range(NS):
                j, i = divmod(t, CH)
                act.wait_ge(err_ready, t + 1)
                if t >= RING:
                    act.wait_ge(sur_read, t - RING + 1)
                act.activation(sur[:, t % RING, :], psE[:, 0:NB], ACT.Sigmoid, scale=1.0 / (1.0 + 1e-6))\
                   .then_inc(sur_ready, 1)
                if j + 1 < NCH:
                    empty_piece(4 * (j + 1) + i)
                if i == CH - 1 and j + 1 < NCH:
                    n = j + 1
                    h = LV[n]
                    g = P // h
                    for gr in range(groups(n) + 1):
                        k = turned(n) + gr
                        if h > CH and gr < groups(n):
                            act.wait_ge(u_ready, n * CH)
                            if k >= 2:
                                act.wait_ge(t_psum, k - 1)
                            for m in range(2):
                                src = S[:, m, 0, cols(n * CH - h, h)].rearrange("p (t b) -> p t b", b=NB)
                                src = src[:, :, 2 * gr * g:2 * (gr + 1) * g].rearrange("p t (g b) -> p g t b", b=g)
                                act.activation(UG[:, k % 2, m:4:2, :].rearrange("p g (t b) -> p g t b", b=g), src,
                                               ACT.Copy).then_inc(ug_ready, 1)
                        if gr:
                            k -= 1
                            size = min(4, nblk(n))
                            if k >= 2:
                                act.wait_ge(r_psum, [total(x) + min(4 * y + 4, nblk(x)) for x in sorted(LV)
                                                     for y in range(groups(x))][k - 2])
                            act.wait_ge(t_psum, k + 1)
                            act.activation(UT[:, k % 2, 0:size, :], psT[:, 0:size * P], ACT.Copy).then_inc(t_ready, 1)

        @block.vector
        def _(dve):
            own = 0

            def mark(ins):
                nonlocal own
                own += 1
                ins.then_inc(dve_own, 1)
                return own

            def keep_block(n, i):
                k = total(n) + i
                dve.wait_ge(g_psum, k + 1)
                if n >= 3:
                    dve.wait_ge(r_psum, total(n - 1))
                dve.tensor_tensor(g_slot(n, i).rearrange("p (k c) -> p k c", k=3),
                                  psG[k % 2][:, 0:3 * P].rearrange("p (k c) -> p k c", k=3),
                                  mask[LV[n]][:, :].unsqueeze(1).broadcast_to((P, 3, P)), ALU.mult).then_inc(g_ready, 1)

            def square_error(t):
                dve.wait_ge(dve_own, mark(dve.tensor_tensor(perr[:, :], S[:, 0, 1, cols(t)], S[:, 1, 1, cols(t)], ALU.add)))
                dve.tensor_tensor(sqr[:, :], perr[:, :], perr[:, :], ALU.mult).then_inc(sq_ready, 1)

            dve.wait_ge(mask_psum, 1)
            for i, h in enumerate(hs):
                dve.tensor_copy(mask[h][:, :], psT[:, i * P:(i + 1) * P]).then_inc(masks, 1)
            dve.wait_ge(masks, len(hs))
            square_error(0)
            for i in range(nblk(1)):
                keep_block(1, i)
            keys_done = 0
            for t in range(NS):
                j, i = divmod(t, CH)
                c0 = j * CH
                u = S[:, :, 0, cols(t)]
                row = lambda n: u.unsqueeze(2).broadcast_to((P, 2, n, NB))
                dve.wait_ge(sur_ready, t + 1)
                if keys_done:
                    dve.wait_ge(dve_own, keys_done)
                dve.tensor_tensor(u, u, sur[:, t % RING, :].unsqueeze(1).broadcast_to((P, 2, NB)), ALU.mult)\
                   .then_inc(u_ready, 1)
                if i == 0:
                    dve.wait_ge(coef_out, 4 * (j + 1))
                dve.wait_ge(u_ready, t + 1)
                n = CH - 1 - i
                if n:
                    dve.wait_ge(dve_own, mark(dve.tensor_tensor(tq1[:, :, :], C[:, j % 2, :, 1, KQ_AT[i], :], u, ALU.mult)))
                    nxt = S[:, :, 1, cols(t + 1)]
                    dve.wait_ge(dve_own, mark(dve.tensor_tensor(nxt, nxt, tq1[:, :, :], ALU.subtract)))
                    square_error(t + 1)
                if n:
                    dve.tensor_tensor(tk[:, :, 0:n, :], C[:, j % 2, :, 0, KQ_AT[i]:KQ_AT[i] + n, :], row(n), ALU.mult)
                if n > 1:
                    dve.tensor_tensor(tq[:, :, 1:n, :], C[:, j % 2, :, 1, KQ_AT[i] + 1:KQ_AT[i] + n, :], row(n - 1), ALU.mult)
                dve.tensor_tensor(to[:, :, 0:n + 1, :], CO[:, j % 2, :, O_AT[i]:O_AT[i] + n + 1, :], row(n + 1), ALU.mult)\
                   .then_inc(mul_done, 1)
                dve.wait_ge(mul_done, t + 1)
                later = lambda x, a, k: x[:, :, cols(a, k)].rearrange("p m (t b) -> p m t b", b=NB)
                if n:
                    y = later(S[:, :, 0, :], t + 1, n)
                    keys_done = mark(dve.tensor_tensor(y, y, tk[:, :, 0:n, :], ALU.subtract))
                if n > 1:
                    y = later(S[:, :, 1, :], t + 2, n - 1)
                    mark(dve.tensor_tensor(y, y, tq[:, :, 1:n, :], ALU.subtract))
                y = later(O, t, n + 1)
                last = mark(dve.tensor_tensor(y, y, to[:, :, 0:n + 1, :], ALU.add))
                if j + 2 < NCH:
                    for b in slices(j + 2)[i]:
                        keep_block(j + 2, b)
                if i == CH - 1 and j + 1 < NCH:
                    nb, h, c = j + 1, LV[j + 1], (j + 1) * CH
                    g = P // h
                    dve.wait_ge(dve_own, last)
                    for b in range(nblk(nb)):
                        gi, m = divmod(b, 2)
                        k = total(nb) + b
                        ps = psR[k % 2][:, 0:3 * P].rearrange("p (k t b) -> p k t b", k=3, b=g)
                        y = S[:, m, :, cols(c, h)].rearrange("p k (t b) -> p k t b", b=NB)[:, :, :, gi * g:(gi + 1) * g]
                        z = O[:, m, cols(c, h)].rearrange("p (t b) -> p t b", b=NB)[:, :, gi * g:(gi + 1) * g]
                        dve.wait_ge(r_psum, k + 1)
                        dve.tensor_tensor(y, y, ps[:, 0:2], ALU.subtract)
                        dve.tensor_tensor(z, z, ps[:, 2], ALU.add).then_inc(r_done, 1)
                    dve.wait_ge(r_done, total(nb + 1))
                    square_error(t + 1)


def memory_output(nc, ctx, pr, dram, x1):
    sb = lambda n, s: ctx.enter_context(nc.sbuf_tensor(n, s, F32))
    sem = lambda n: ctx.enter_context(nc.semaphore(n))
    NU, O, pw, ident, ones = (pr[n] for n in ("NU", "O", "pw", "ident", "ones"))
    x_tok = sb("x_tok3", [P, TT, DM])
    Wo = sb("Wo", [P, DM])
    nw = sb("nw", [P, 1])
    diag = sb("diag", [P, 2, 3, P])
    mix = sb("mix", [P, NT])
    t1 = sb("t1", [P, 2, BW])
    t2 = sb("t2", [P, 2, BW])
    on = sb("on", [P, NT])
    stats = sb("stats", [P, TT, 6])
    mv = sb("mv", [P, TT, 2])
    eps = sb("eps", [P, 2])
    psB = [ctx.enter_context(nc.psum_tensor(f"psB{i}", [P, 3 * P], F32)) for i in range(2)]
    psS = [ctx.enter_context(nc.psum_tensor(f"psS{i}", [P, BW], F32)) for i in range(2)]
    psO = [ctx.enter_context(nc.psum_tensor(f"psO{i}", [P, DM], F32)) for i in range(3)]
    loaded = sem("loaded3")
    diag_ready = sem("diagonals_ready")
    spread = sem("weights_spread")
    mixed = sem("mixed")
    own_d = sem("dve_own3")
    sq3 = sem("squares3")
    ms = sem("mean_squares")
    root = sem("roots3")
    normed = sem("normed")
    eps_ok = sem("eps_ok")
    out_ps = sem("outputs_in_psum")
    resid = sem("residual_added")
    std = sem("deviations")

    with nc.Block() as block:
        @block.sync
        def _(sp):
            sp.dma_start(x_tok[:, :, :], dram["x"].rearrange("b s d -> (b s) d")
                         .rearrange("(i p) d -> p i d", p=P)).then_inc(loaded, 16)
            sp.dma_start(Wo[:, :], dram["Wo"]).then_inc(loaded, 16)
            sp.dma_start(nw[:, :], dram["norm_w"].rearrange("(p o) -> p o", o=1)).then_inc(loaded, 16)

        @block.gpsimd
        def _(pool):
            pool.memset(eps[:, 0:1], RMS_EPS).then_inc(eps_ok, 1)
            pool.memset(eps[:, 1:2], LN_EPS).then_inc(eps_ok, 1)
            for i in range(TT):
                if i >= 2:
                    pool.wait_ge(spread, i - 1)
                for k in range(3):
                    d = pool.tensor_scalar(diag[:, i % 2, k, :], ident[:, :], pw[:, i, k:k + 1], 2.0 if k < 2 else 1.0,
                                           ALU.mult, ALU.mult)
                d.then_inc(diag_ready, 1)

        @block.tensor
        def _(pe):
            for i in range(TT):
                pe.wait_ge(diag_ready, i + 1)
                if i >= 2:
                    pe.wait_ge(mixed, i - 1)
                pe.matmul(psB[i % 2][:, :], ones[:, :], diag[:, i % 2, :, :].rearrange("p k c -> p (k c)"),
                          start=True, stop=True).then_inc(spread, 1)
                if i % 4 == 3:
                    n = i // 4
                    pe.wait_ge(sq3, n + 1)
                    if n >= 2:
                        pe.wait_ge(root, n - 1)
                    pe.matmul(psS[n % 2][:, :], ones[:, :], t1[:, n % 2, :], start=True, stop=True).then_inc(ms, 1)
            pe.wait_ge(normed, NBK)
            pe.wait_ge(loaded, 48)
            for i in range(TT):
                if i >= 3:
                    pe.wait_ge(resid, i - 2)
                pe.matmul(psO[i % 3][:, :], on[:, i * P:(i + 1) * P], Wo[:, :], start=True, stop=True).then_inc(out_ps, 1)

        @block.scalar
        def _(act):
            act.wait_ge(eps_ok, 2)
            for n in range(NBK):
                act.wait_ge(ms, n + 1)
                if n >= 2:
                    act.wait_ge(normed, n - 1)
                act.activation(t2[:, n % 2, :], psS[n % 2][:, :], ACT.Sqrt, bias=eps[:, 0:1], scale=1.0 / P).then_inc(root, 1)
            act.wait_ge(std, 1)
            act.activation(mv[:, :, 1:2], mv[:, :, 1:2], ACT.Sqrt, bias=eps[:, 1:2]).then_inc(std, 1)

        @block.vector
        def _(dve):
            own = 0

            def link(ins):
                nonlocal own
                own += 1
                ins.then_inc(own_d, 1)
                dve.wait_ge(own_d, own)

            def norm(n):
                dve.wait_ge(root, n + 1)
                r = t2[:, n % 2, :]
                link(dve.reciprocal(r, r))
                dst = on[:, :].rearrange("p (b s) -> p s b", s=NS)[:, n * BW // NB:(n + 1) * BW // NB, :]
                as3 = lambda x: x.rearrange("p (s b) -> p s b", b=NB)
                dve.scalar_tensor_tensor(dst, as3(mix[:, n * BW:(n + 1) * BW]), nw[:, :], as3(r), ALU.mult, ALU.mult)\
                   .then_inc(normed, 1)

            dve.wait_ge(loaded, 48)
            for i in range(TT):
                c = slice(i * P, (i + 1) * P)
                dve.wait_ge(spread, i + 1)
                ps = psB[i % 2]
                link(dve.tensor_tensor(mix[:, c], O[:, 0, c], ps[:, 0:P], ALU.mult))
                link(dve.tensor_tensor(O[:, 1, c], O[:, 1, c], ps[:, P:2 * P], ALU.mult))
                link(dve.tensor_tensor(mix[:, c], mix[:, c], O[:, 1, c], ALU.add))
                dve.tensor_tensor(NU[:, c], NU[:, c], ps[:, 2 * P:], ALU.mult).then_inc(mixed, 1)
                dve.wait_ge(mixed, i + 1)
                link(dve.tensor_tensor(mix[:, c], mix[:, c], NU[:, c], ALU.add))
                if i % 4 == 3:
                    n = i // 4
                    cc = slice(n * BW, (n + 1) * BW)
                    if n >= 2:
                        dve.wait_ge(ms, n - 1)
                    dve.tensor_tensor(t1[:, n % 2, :], mix[:, cc], mix[:, cc], ALU.mult).then_inc(sq3, 1)
                    if n:
                        norm(n - 1)
            norm(NBK - 1)
            for i in range(TT):
                dve.wait_ge(out_ps, i + 1)
                dve.tensor_tensor(x1[:, i, :], x_tok[:, i, :], psO[i % 3][:, :], ALU.add).then_inc(resid, 1)
                dve.wait_ge(resid, i + 1)
                link(dve.bn_stats(stats[:, i, :], x1[:, i, :]))
                link(dve.bn_aggr(mv[:, i, :], stats[:, i, :]))
            dve.nop().then_inc(std, 1)
            dve.wait_ge(std, 2)
            link(dve.reciprocal(mv[:, :, 1:2], mv[:, :, 1:2]))
            for i in range(TT):
                link(dve.tensor_scalar(x1[:, i, :], x1[:, i, :], mv[:, i, 0:1], mv[:, i, 1:2], ALU.subtract, ALU.mult))


def memory(nc, dram, x1, ident, ones):
    with ExitStack() as ctx:
        sb = lambda n, s: ctx.enter_context(nc.sbuf_tensor(n, s, F32))
        pr = {"ident": ident, "ones": ones,
              "KQ": sb("KQ", [P, 2, NT]),
              "W": sb("W", [P, 2, NT]),
              "S": sb("S", [P, 2, 2, NT]),
              "NU": sb("NU", [P, NT]), "O": sb("O", [P, 2, NT]), "pw": sb("pw", [P, TT, 3]),
              "A": x1[:, :, :].rearrange("p i d -> p (i d)").rearrange("p (m c) -> p m c", m=2)}
        with ExitStack() as c:
            memory_inputs(nc, c, pr, dram)
        with ExitStack() as c:
            recurrence(nc, c, pr)
        with ExitStack() as c:
            memory_output(nc, c, pr, dram, x1)


HEADS, HD = 8, 64
NKEY = DM


def cross_attention(nc, ctx, x1, dram, ident, preload):
    sb = lambda n, s: ctx.enter_context(nc.sbuf_tensor(n, s, F32))
    sem = lambda n: ctx.enter_context(nc.semaphore(n))
    r = lambda ap: ap.bitcast(F32R)
    TURN, COPY, ADD = 3, 3, 5
    Y_AT = (2, 4, 5, 7)
    RS_ = 2
    RE = 8
    WQ = sb("WQ", [P, 4, HD])
    WKV = sb("WKV", [P, 8, HD])
    WO = sb("WO", [HD, HEADS * HD])
    WOT = sb("WOT", [P, 4, HD])
    bout = sb("bout", [HD, 1])
    hi_m = sb("hi_m", [P, HEADS * HD])
    MS = sb("MS", [P, HEADS, 2, HD])
    NS_ = sb("NS_", [P, HEADS * HD])
    XX = sb("XX", [P, 2, NKEY])
    XH = sb("XH", [P, 2, NKEY])
    XL = sb("XL", [P, 2, NKEY])
    CC = sb("CC", [P, 2, NKEY])
    CHI = sb("CHI", [P, 2, NKEY])
    CLO = sb("CLO", [P, 2, NKEY])
    Y = sb("Y", [P, 2, HEADS, NKEY])
    Z = sb("Z", [P, 2, 2, HEADS * HD])
    E = sb("E", [P, RE, 2, NKEY])
    AT = sb("AT", [P, 4, 2, NKEY])
    NM = sb("NM", [P, RE, 2])
    RS = sb("RS", [P, RE, 2])
    RI = sb("RI", [P, RE, 2])
    ps = lambda n, w=BW: ctx.enter_context(nc.psum_tensor(n, [P, w], F32))
    psY = [ps("psY0"), ps("psY1"), ps("psY2")]
    psS = [ps(f"psS{i}x") for i in range(RS_)]
    psA = [ps("psA0"), ps("psA1")]
    psU = ps("psU", NKEY)
    psM, psN = (psY[0], psS[1]), (psY[1], psY[2])

    w_in = sem("att_weights")
    wprep_pe = sem("att_products_in_psum")
    wprep = sem("att_weights_ready")
    wot_ready = sem("wout_turned")
    x_in = [sem("x_rows0"), sem("x_rows1")]
    c_in = [sem("ctx_rows0"), sem("ctx_rows1")]
    hi_ready = sem("hi_ready")
    lo_ready = sem("lo_ready")
    y_psum = sem("y_in_psum")
    y_hi = sem("y_hi")
    y_ready = sem("y_ready")
    z_psum = sem("z_in_psum")
    z_ready = sem("z_ready")
    sim_ready = sem("scores_in_psum")
    max_ready = sem("maxima_ready")
    exp_done = sem("exponentials_ready")
    ri_ready = sem("reciprocals_ready")
    norm_done = sem("attention_ready")
    t_psum = sem("attention_turned")
    at_act = sem("turned_by_act")
    at_dve = sem("turned_by_dve")
    av_done = sem("pairs_of_heads_added")
    out_read = sem("outputs_read")
    out_part = sem("outputs_half_read")

    DV = (1, 4, 7)
    by_dve = lambda hh: sum(1 for v in DV if v <= hh)
    ITER = NB // 2
    LAST = 16 * ITER

    def at_wait(eng, it, k):
        q, hh = divmod(k, 8)
        if hh in DV:
            eng.wait_ge(at_dve, it * 2 * len(DV) + (q * len(DV) + by_dve(hh)))
        else:
            eng.wait_ge(at_act, it * 2 * (8 - len(DV)) + (q * (8 - len(DV)) + hh + 1 - by_dve(hh)))

    def rows(x, b2):
        return x[64 * b2:64 * b2 + 64]

    with nc.Block() as block:
        def run(eng, slot, tail):
            for k in range(16):
                slot(0, k, True, False)
            with eng.Fori(1, ITER - 1) as it:
                for k in range(16):
                    slot(it, k, False, False)
            for k in range(16):
                slot(ITER - 1, k, False, True)
            for k in range(16, 16 + tail):
                slot(ITER - 1, k, False, True)

        @block.sync
        def _(sp):
            sp.dma_start(WQ[:, :, :], dram["Wq"].rearrange("(c p) k -> p c k", p=P)).then_inc(w_in, 16)
            sp.dma_start(WKV[:, :, :], dram["Wkv"].rearrange("(c p) k -> p c k", p=P)).then_inc(w_in, 16)
            sp.dma_start(WO[:, :], dram["Wout"]).then_inc(w_in, 16)
            sp.dma_start(bout[:, :], dram["bout"].rearrange("(p o) -> p o", o=1)).then_inc(w_in, 16)

            def load(it, q, wait):
                if wait:
                    sp.wait_ge(lo_ready, it * 2 + (q - 1))
                for half in range(2):
                    sp.dma_start(rows(XX, half)[:, q, :], rows(x1, q)[:, bass.ds(it, 1), :]
                                 .rearrange("p i d -> p (i d)")).then_inc(x_in[q], 16)
                    sp.dma_start(rows(CC, half)[:, q, :], dram["ctx"][bass.ds(it * 2 + q, 1), :, :]
                                 .rearrange("b s d -> (b s) d")).then_inc(c_in[q], 16)
            load(0, 0, False)
            load(0, 1, False)
            preload(sp)
            with sp.Fori(1, ITER) as it:
                load(it, 0, True)
                load(it, 1, True)

        @block.tensor
        def _(pe):
            pe.wait_ge(w_in, 64)
            for i in range(4):
                mm = pe.transpose(psS[0][:, i * HD:(i + 1) * HD], WO[:, i * P:(i + 1) * P], ident[0:HD, 0:HD])
            mm.then_inc(wprep_pe, 1)
            for half in range(2):
                for h in range(HEADS):
                    a = rows(WQ, h % 2)[:, h // 2, :]
                    mm = pe.matmul(rows(psM[h % 2], half)[:, h // 2 * HD:(h // 2 + 1) * HD], a, rows(WKV, h % 2)[:, h // 2, :],
                                   start=True, stop=True)
            mm.then_inc(wprep_pe, 1)
            pe.wait_ge(wot_ready, 1)
            for half in range(2):
                for h in range(HEADS):
                    mm = pe.matmul(rows(psN[h % 2], half)[:, h // 2 * HD:(h // 2 + 1) * HD], rows(WKV, h % 2)[:, 4 + h // 2, :],
                                   rows(WOT, h % 2)[:, h // 2, :], start=True, stop=True)
            mm.then_inc(wprep_pe, 1)
            pe.wait_ge(wprep, 14)

            def y_piece(it, q, p, wait):
                if p == 0:
                    pe.wait_ge(hi_ready, it * 4 + (2 * q + 2))
                    pe.wait_ge(lo_ready, it * 2 + (q + 1))
                if p == 0 and wait:
                    pe.wait_ge(y_ready, it * 8 + 4 * q)
                elif p in (1, 2) and wait:
                    pe.wait_ge(z_ready, it * 4 + (2 * q - 2 + p))
                elif p == 3:
                    pe.wait_ge(y_ready, it * 8 + (4 * q + 1))
                for d in range(2):
                    for n, x in enumerate((XH, XL)):
                        mm = pe.matmul(psY[(2 + p) % 3][:, d * NKEY:(d + 1) * NKEY],
                                       r(MS[:, 2 * p + d, :, :].rearrange("p a c -> p (a c)")), r(x[:, q, :]),
                                       start=n == 0, stop=n == 1)
                mm.then_inc(y_psum, 1)

            def slot(it, k, first, last):
                q, hh = divmod(k, 8)
                if k < 16:
                    pe.wait_ge(y_ready, it * 8 + (4 * q + hh // 2 + 1))
                    if not first or k >= RS_:
                        pe.wait_ge(exp_done, it * 16 + (k - RS_ + 1))
                    for ib in range(2):
                        for n, c in enumerate((CHI, CLO)):
                            mm = pe.matmul(psS[k % RS_][:, ib * NKEY:(ib + 1) * NKEY],
                                           r(Y[:, q, hh, ib * P:(ib + 1) * P]), r(c[:, q, :]), start=n == 0, stop=n == 1)
                    mm.then_inc(sim_ready, 1)
                    if hh in (0, 1):
                        pe.wait_ge(y_ready, it * 8 + (4 * q + 2 + hh))
                        for n, c in enumerate((CHI, CLO)):
                            mm = pe.matmul(psY[hh][:, :], r(c[:, q, hh * P:(hh + 1) * P]), r(NS_[:, :]),
                                           start=n == 0, stop=n == 1)
                        mm.then_inc(z_psum, 1)
                    if hh in Y_AT and not (last and q == 1):
                        y_piece(it + q, 1 - q, Y_AT.index(hh), True)
                t = k - TURN
                if (not first or t >= 0) and t < 16:
                    pe.wait_ge(norm_done, it * 16 + (t + 1))
                    if not first or t >= 2:
                        at_wait(pe, it, t - 2)
                    for jb in range(2):
                        for ib in range(2):
                            mm = pe.transpose(psA[t % 2][:, jb * NKEY + ib * P:jb * NKEY + (ib + 1) * P],
                                              E[:, t % RE, ib, jb * P:(jb + 1) * P], ident[:, :])
                    mm.then_inc(t_psum, 1)
                a = k - ADD
                if a % 2 == 0 and (not first or a >= 0) and a < 16:
                    at_wait(pe, it, a)
                    at_wait(pe, it, a + 1)
                    qa, ha = divmod(a, 8)
                    pe.wait_ge(z_ready, it * 4 + (2 * qa + 2))
                    if ha == 0 and (not first or qa >= 1):
                        pe.wait_ge(out_read, it * 2 + qa)
                    for jb in range(2):
                        for d in range(2):
                            h = ha + d
                            mm = pe.matmul(rows(psU, d)[:, :], Z[:, qa % 2, jb, h * HD:(h + 1) * HD],
                                           AT[:, (a + d) % 4, jb, :], start=ha == 0 and jb == 0, stop=ha == 6 and jb == 1)
                    mm.then_inc(av_done, 1)

            for p in range(4):
                y_piece(0, 0, p, False)
            run(pe, slot, ADD)

        def turn_out(eng, it, t, engine_sem, copy):
            eng.wait_ge(t_psum, it * 16 + (t + 1))
            copy(AT[:, t % 4, :, :].rearrange("p j i -> p (j i)"), psA[t % 2][:, :]).then_inc(engine_sem, 1)

        @block.scalar
        def _(act):
            act.wait_ge(wprep_pe, 1)
            act.activation(WOT[:, :, :].rearrange("p i o -> p (i o)"), psS[0][:, 0:4 * HD], ACT.Copy).then_inc(wot_ready, 1)

            def split_hi(it, q, wait):
                act.wait_ge(x_in[q], it * 32 + 32)
                act.wait_ge(c_in[q], it * 32 + 32)
                if wait:
                    act.wait_ge(y_psum, it * 8 + (4 * q - 4))
                    act.wait_ge(sim_ready, it * 16 + (8 * q - 8))
                act.activation(r(XH[:, q, :]), XX[:, q, :], ACT.Copy).then_inc(hi_ready, 1)
                act.activation(r(CHI[:, q, :]), CC[:, q, :], ACT.Copy).then_inc(hi_ready, 1)

            def y_high(it, q, p, wait):
                act.wait_ge(y_psum, it * 8 + (4 * q + p + 1))
                if p == 0 and wait:
                    act.wait_ge(sim_ready, it * 16 + (8 * q - 8))
                act.activation(r(Y[:, q, 2 * p:2 * p + 2, :].rearrange("p h n -> p (h n)")), psY[(2 + p) % 3][:, :],
                               ACT.Copy).then_inc(y_hi, 1)

            def slot(it, k, first, last):
                q, hh = divmod(k, 8)
                if k < 16:
                    if hh == 0 and not (last and q == 1):
                        split_hi(it + q, 1 - q, not (first and q == 0))
                    if hh in (1, 2):
                        jb = hh - 1
                        act.wait_ge(z_psum, it * 4 + (2 * q + jb + 1))
                        if jb == 0 and (not first):
                            act.wait_ge(av_done, it * 8 + (4 * q - 4))
                        act.activation(Z[:, q, jb, :], psY[jb][:, :], ACT.Copy).then_inc(z_ready, 1)
                    if hh - 1 in Y_AT and not (last and q == 1):
                        y_high(it + q, 1 - q, Y_AT.index(hh - 1), not (first and q == 0))
                    if hh == 0 and not (first and q == 0):
                        y_high(it, q, 3, True)
                    act.wait_ge(max_ready, it * 16 + (k + 1))
                    if not first or k >= RE:
                        act.wait_ge(t_psum, it * 16 + (k - RE + 1))
                    for ib in range(2):
                        ex = act.activation(E[:, k % RE, ib, :], psS[k % RS_][:, ib * NKEY:(ib + 1) * NKEY], ACT.Exp,
                                            bias=NM[:, k % RE, ib:ib + 1], accum_out=RS[:, k % RE, ib:ib + 1])
                    ex.then_inc(exp_done, 1)
                t = k - COPY
                if (not first or t >= 0) and t < 16 and t % 8 not in DV:
                    if not first or t >= 4:
                        act.wait_ge(av_done, it * 8 + (t - 4) // 2 + 1)
                    turn_out(act, it, t, at_act, lambda o, i: act.activation(o, i, ACT.Copy))

            split_hi(0, 0, False)
            for p in range(4):
                y_high(0, 0, p, False)
            run(act, slot, COPY)

        @block.gpsimd
        def _(pool):
            def slot(it, k, first, last):
                pool.wait_ge(ri_ready, it * 16 + (k + 1))
                pool.tensor_tensor(E[:, k % RE, :, :], E[:, k % RE, :, :],
                                   RI[:, k % RE, :].unsqueeze(2).broadcast_to((P, 2, NKEY)), ALU.mult).then_inc(norm_done, 1)
            run(pool, slot, 0)

        @block.vector
        def _(dve):
            dve.wait_ge(w_in, 64)
            dve.wait_ge(wprep_pe, 2)
            heads = lambda x, e: x.rearrange("p (h e c) -> p h e c", e=2, c=HD)[:, :, e, :]
            half = lambda x: x[:, 0:4 * HD].rearrange("p (h c) -> p h c", c=HD)
            for e in range(2):
                dve.tensor_copy(r(heads(hi_m[:, :], e)), half(psM[e][:, :])).then_inc(wprep, 1)
            dve.wait_ge(wprep, 2)
            for e in range(2):
                for d in range(2):
                    dve.tensor_copy(r(MS[0:HD, e:HEADS:2, d, :]), heads(hi_m[0:HD, :], e)).then_inc(wprep, 1)
                    dve.tensor_tensor(r(MS[HD:P, e:HEADS:2, d, :]), half(psM[e][HD:P, :]), heads(hi_m[HD:P, :], e),
                                      ALU.subtract).then_inc(wprep, 1)
            dve.wait_ge(wprep_pe, 3)
            for e in range(2):
                dve.tensor_copy(r(heads(NS_[:, :], e)), half(psN[e][:, :])).then_inc(wprep, 1)
            dve.wait_ge(wprep, 12)
            for e in range(2):
                lo = heads(NS_[HD:P, :], e)
                dve.tensor_tensor(r(lo), half(psN[e][HD:P, :]), lo, ALU.subtract).then_inc(wprep, 1)

            def split_lo(it, q, wait):
                dve.wait_ge(hi_ready, it * 4 + (2 * q + 2))
                dve.tensor_tensor(r(XL[:, q, :]), XX[:, q, :], XH[:, q, :], ALU.subtract)
                dve.tensor_tensor(r(CLO[:, q, :]), CC[:, q, :], CHI[:, q, :], ALU.subtract).then_inc(lo_ready, 1)

            def y_low(it, q, p):
                dve.wait_ge(y_hi, it * 8 + (4 * q + p + 1))
                y = Y[HD:P, q, 2 * p:2 * p + 2, :].rearrange("p h n -> p (h n)")
                dve.tensor_tensor(r(y), psY[(2 + p) % 3][HD:P, :], y, ALU.subtract).then_inc(y_ready, 1)

            def slot(it, k, first, last):
                q, hh = divmod(k, 8)
                if k < 16:
                    dve.wait_ge(sim_ready, it * 16 + (k + 1))
                    dve.tensor_reduce(NM[:, k % RE, :], psS[k % RS_][:, :].rearrange("p (i j) -> p i j", i=2), AX.X,
                                      ALU.max, negate=True).then_inc(max_ready, 1)
                    if hh - 1 in Y_AT and not (last and q == 1):
                        y_low(it + q, 1 - q, Y_AT.index(hh - 1))
                    if hh == 0 and not (first and q == 0):
                        y_low(it, q, 3)
                t = k - 1
                if (not first or t >= 0) and t < 16:
                    dve.wait_ge(exp_done, it * 16 + (t + 1))
                    dve.reciprocal(RI[:, t % RE, :], RS[:, t % RE, :]).then_inc(ri_ready, 1)
                a = k - (ADD + 7)
                if a in (0, 8) or (a in (-8, -16) and not first):
                    qb = a // 8
                    dve.wait_ge(av_done, it * 8 + (4 * qb + 4))
                    i = it if qb >= 0 else it - 1
                    xr = rows(x1, qb % 2)[:, bass.ds(i, 1), :].rearrange("p i d -> p (i d)")
                    dve.scalar_tensor_tensor(xr, psU[0:HD, :], bout[:, :], xr, ALU.add, ALU.add)\
                       .then_inc(out_part, 1)
                    dve.wait_ge(out_part, it * 2 + (qb + 1))
                    dve.tensor_tensor(xr, xr, psU[HD:P, :], ALU.add).then_inc(out_read, 1)
                if k < 16:
                    if hh == 1 and not (last and q == 1):
                        split_lo(it + q, 1 - q, True)
                t = k - COPY
                if (not first or t >= 0) and t < 16 and t % 8 in DV:
                    if not first or t >= 4:
                        dve.wait_ge(av_done, it * 8 + (t - 4) // 2 + 1)
                    turn_out(dve, it, t, at_dve, dve.tensor_copy)
            split_lo(0, 0, False)
            for p in range(4):
                y_low(0, 0, p)
            run(dve, slot, ADD + 1)


def layernorm(nc, ctx, x, name):
    sb = lambda n, s: ctx.enter_context(nc.sbuf_tensor(name + n, s, F32))
    sem = lambda n: ctx.enter_context(nc.semaphore(name + n))
    stats = sb("stats", [P, TT, 6])
    mv = sb("mv", [P, TT, 2])
    eps = sb("eps", [P, 1])
    own_d, std, ready = sem("own"), sem("std"), sem("eps_ready")
    with nc.Block() as block:
        @block.gpsimd
        def _(pool):
            pool.memset(eps[:, :], LN_EPS).then_inc(ready, 1)

        @block.scalar
        def _(act):
            act.wait_ge(ready, 1)
            act.wait_ge(std, 1)
            act.activation(mv[:, :, 1:2], mv[:, :, 1:2], ACT.Sqrt, bias=eps[:, :]).then_inc(std, 1)

        @block.vector
        def _(dve):
            own = 0
            for i in range(TT):
                dve.bn_stats(stats[:, i, :], x[:, i, :]).then_inc(own_d, 1)
            for i in range(TT):
                dve.wait_ge(own_d, i + 1)
                ag = dve.bn_aggr(mv[:, i, :], stats[:, i, :])
            ag.then_inc(std, 1)
            dve.wait_ge(std, 2)
            dve.reciprocal(mv[:, :, 1:2], mv[:, :, 1:2]).then_inc(own_d, 1)
            dve.wait_ge(own_d, TT + 1)
            for i in range(TT):
                last = dve.tensor_scalar(x[:, i, :], x[:, i, :], mv[:, i, 0:1], mv[:, i, 1:2], ALU.subtract, ALU.mult)
            last.then_inc(own_d, 1)


NE, TOPK, CAP, HE, HSH = 64, 6, 128, 32, 64
EC = P // HE
NC = NE // EC
TB = BW
NTB = NT // TB


def expert_weights(nc, ctx):
    sb = lambda n, s: ctx.enter_context(nc.sbuf_tensor(n, s, F32))
    return {"up": sb("up_raw", [P, KD, NE, 2 * HE]), "down": sb("down", [P, NC, DM]),
            "in": ctx.enter_context(nc.semaphore("expert_weights_in"))}


def load_expert_weights(sp, ew, dram):
    for k in range(KD):
        sp.dma_start(ew["up"][:, k, :, :], dram["w_up"][:, k * P:(k + 1) * P, :].rearrange("e p h -> p e h")).then_inc(ew["in"], 16)
    sp.dma_start(ew["down"][:, :, :], dram["w_down"].rearrange("e h c -> (e h) c").rearrange("(n p) c -> p n c", p=P)).then_inc(ew["in"], 16)


EW_IN = 16 * (KD + 1)


def experts(nc, ctx, x2, ew, dram, ident):
    sb = lambda n, s: ctx.enter_context(nc.sbuf_tensor(n, s, F32))
    sem = lambda n: ctx.enter_context(nc.semaphore(n))
    r = lambda ap: ap.bitcast(F32R)
    UH = sb("UH", [P, KD, 2, NE * HE])
    UL = sb("UL", [P, KD, 2, NE * HE])
    XH = sb("XTH", [P, KD, NT])
    XL = sb("XTL", [P, KD, NT])
    WT = sb("WTT", [P, NT])
    sh_up = sb("sh_up", [P, KD, 2 * HSH])
    sh_h = sb("sh_h", [P, KD, 2 * HSH])
    sh_l = sb("sh_l", [P, KD, 2 * HSH])
    sh_dn = sb("sh_dn", [HSH, DM])
    gate = sb("gate", [P, KD, NE])
    small = ctx.enter_context(ExitStack())
    sbs = lambda n, s: small.enter_context(nc.sbuf_tensor(n, s, F32))
    sc = sbs("sc", [P, TT, NE])
    top = sbs("top", [P, TT, 8])
    gt = sbs("gt", [P, TT, NE])
    eq = sbs("eq", [P, TT, NE])
    rank = sbs("rank", [P, TT, NE])
    seg = sbs("seg", [P, TT, NE])
    cnt = sbs("cnt", [P, TT, 2])
    rcp = sbs("rcp", [P, TT, 1])
    car = sbs("car", [P, TT, NE])
    w2 = sbs("w2", [P, TT, 2, NE])
    tri = sbs("tri", [P, P])
    on1 = sbs("on1", [P, P])

    n3 = lambda n: ctx.enter_context(nc.psum_tensor(n, [P, BW], F32))
    bk = [n3(f"e{i}") for i in range(8)]

    loaded = sem("gate_in")
    consts = sem("route_consts")
    xt_ps = sem("x2_turned")
    xt_hi = sem("x2_hi")
    xt_lo = sem("x2_lo")
    logit = sem("logits_in_psum")
    score = sem("scores_ready")
    own_d = sem("dve_own5")
    sel_ok = sem("selection_ready")
    counts = sem("counts_in_psum")
    wr = sem("routing_weights_ready")
    wt_ps = sem("routing_weights_turned")
    wt_ok = sem("routing_rows_ready")
    up_hi = sem("up_hi")
    sh_hi = sem("shared_hi")
    NT8 = KD * NBK

    with nc.Block() as block:
        @block.sync
        def _(sp):
            sp.dma_start(gate[:, :, :], dram["w_gate"].rearrange("(k p) e -> p k e", p=P)).then_inc(loaded, 16)
            sp.dma_start(sh_up[:, :, :], dram["w_shared_up"].rearrange("(k p) e -> p k e", p=P)).then_inc(loaded, 16)
            sp.dma_start(sh_dn[:, :], dram["w_shared_down"]).then_inc(loaded, 16)

        @block.gpsimd
        def _(pool):
            pool.memset(tri[:, :], 1.0).then_inc(consts, 1)
            pool.memset(seg[:, :, :], 1.0).then_inc(consts, 1)
            pool.memset(on1[:, :], 1.0).then_inc(consts, 1)
            pool.wait_ge(consts, 3)
            pool.affine_select(out=r(tri[:, :]), in_=tri[:, :], compare_op=ALU.is_gt, fill=0.0, base=0,
                               pattern=[[1, P]], channel_multiplier=-1).then_inc(consts, 1)
            pool.memset(seg[:, :, 0:1], 0.0).then_inc(consts, 1)
            pool.wait_ge(consts, 5)

        @block.tensor
        def _(pe):
            pe.wait_ge(consts, 5)
            for j in range(NT8):
                k, n = divmod(j, NBK)
                if j >= 4:
                    pe.wait_ge(xt_lo, j - 3)
                for i in range(4):
                    mm = pe.transpose(bk[j % 4][:, i * P:(i + 1) * P], x2[:, 4 * n + i, k * P:(k + 1) * P], ident[:, :])
                mm.then_inc(xt_ps, 1)
            pe.wait_ge(xt_lo, NT8)
            pe.wait_ge(loaded, 48)
            for i in range(TT):
                for n, (k, x) in enumerate([(k, x) for k in range(KD) for x in (XH, XL)]):
                    mm = pe.matmul(bk[4 + i // 8][:, i % 8 * NE:(i % 8 + 1) * NE], x[:, k, i * P:(i + 1) * P],
                                   gate[:, k, :], start=n == 0, stop=n == 2 * KD - 1)
            mm.then_inc(logit, 1)
            pe.wait_ge(sel_ok, 1)
            flat = gt[:, :, :].rearrange("p i e -> p (i e)")
            for m, a in enumerate((tri, on1)):
                for n in range(2):
                    mm = pe.matmul(bk[2 * m + n][:, :], r(a[:, :]), r(flat[:, n * BW:(n + 1) * BW]), start=True, stop=True)
            mm.then_inc(counts, 1)
            pe.wait_ge(wr, 1)
            for i in range(TT):
                mm = pe.transpose(bk[4 + i // 4][:, i % 4 * P:(i % 4 + 1) * P],
                                  w2[:, i, :, :].rearrange("p a e -> p (a e)"), ident[:, :])
                if i % 4 == 3:
                    mm.then_inc(wt_ps, 1)

        @block.scalar
        def _(act):
            for j in range(NT8):
                k, n = divmod(j, NBK)
                act.wait_ge(xt_ps, j + 1)
                act.activation(r(XH[:, k, n * BW:(n + 1) * BW]), bk[j % 4][:, :], ACT.Copy).then_inc(xt_hi, 1)
            act.wait_ge(logit, 1)
            for n in range(2):
                act.activation(sc[:, 8 * n:8 * n + 8, :].rearrange("p i e -> p (i e)"), bk[4 + n][:, :], ACT.Sigmoid)\
                   .then_inc(score, 1)
            act.wait_ge(loaded, 48)
            act.activation(r(sh_h[:, :, :]), sh_up[:, :, :], ACT.Copy).then_inc(sh_hi, 1)
            act.wait_ge(ew["in"], EW_IN)
            for k in range(KD):
                for v in range(2):
                    act.activation(r(UH[:, k, v, :].rearrange("p (e h) -> p e h", h=HE)),
                                   ew["up"][:, k, :, v * HE:(v + 1) * HE], ACT.Copy).then_inc(up_hi, 1)

        @block.vector
        def _(dve):
            own = 0

            def link(ins):
                nonlocal own
                own += 1
                ins.then_inc(own_d, 1)
                dve.wait_ge(own_d, own)

            for j in range(NT8):
                k, n = divmod(j, NBK)
                dve.wait_ge(xt_hi, j + 1)
                c = slice(n * BW, (n + 1) * BW)
                dve.tensor_tensor(r(XL[:, k, c]), bk[j % 4][:, :], XH[:, k, c], ALU.subtract).then_inc(xt_lo, 1)
            dve.wait_ge(score, 2)
            for i in range(TT):
                mx = dve.max(top[:, i, :], sc[:, i, :])
            link(mx)
            edge = top[:, :, TOPK - 1:TOPK].broadcast_to((P, TT, NE))
            dve.tensor_tensor(r(gt[:, :, :]), sc[:, :, :], edge, ALU.is_gt)
            dve.tensor_reduce(rcp[:, :, :], top[:, :, 0:TOPK], AX.X, ALU.add)
            link(dve.tensor_tensor(eq[:, :, :], sc[:, :, :], edge, ALU.is_equal))
            flat = lambda x: x[:, :, :].rearrange("p i e -> p (i e)")
            dve.wait_ge(consts, 5)
            dve.tensor_tensor_scan(flat(rank), flat(seg), flat(eq), 0.0, ALU.mult, ALU.add)
            link(dve.tensor_reduce(cnt[:, :, 0:1], gt[:, :, :], AX.X, ALU.add))
            link(dve.tensor_tensor(rank[:, :, :], rank[:, :, :], cnt[:, :, 0:1].broadcast_to((P, TT, NE)), ALU.add))
            link(dve.scalar_tensor_tensor(flat(eq), flat(rank), float(TOPK), flat(eq), ALU.is_le, ALU.mult))
            dve.tensor_tensor(r(gt[:, :, :]), gt[:, :, :], eq[:, :, :], ALU.add).then_inc(sel_ok, 1)
            dve.wait_ge(sel_ok, 1)
            link(dve.tensor_tensor(sc[:, :, :], sc[:, :, :], gt[:, :, :], ALU.mult))
            link(dve.reciprocal(rcp[:, :, :], rcp[:, :, :]))
            link(dve.tensor_tensor(sc[:, :, :], sc[:, :, :], rcp[:, :, :].broadcast_to((P, TT, NE)), ALU.mult))
            dve.wait_ge(counts, 1)
            link(dve.memset(car[:, 0, :], 0.0))
            for i in range(1, TT):
                link(dve.tensor_tensor(car[:, i, :], car[:, i - 1, :], bk[2 + (i - 1) // 8][:, (i - 1) % 8 * NE:((i - 1) % 8 + 1) * NE], ALU.add))
            for n in range(2):
                c = car[:, 8 * n:8 * n + 8, :].rearrange("p i e -> p (i e)")
                last = dve.tensor_tensor(c, c, bk[n][:, :], ALU.add)
            link(last)
            link(dve.scalar_tensor_tensor(flat(sc), flat(car), float(CAP), flat(sc), ALU.is_lt, ALU.mult))
            link(dve.tensor_copy(r(w2[:, :, 0, :]), sc[:, :, :]))
            dve.tensor_tensor(r(w2[:, :, 1, :]), sc[:, :, :], w2[:, :, 0, :], ALU.subtract).then_inc(wr, 1)
            for n in range(4):
                dve.wait_ge(wt_ps, n + 1)
                dve.tensor_copy(r(WT[:, n * BW:(n + 1) * BW]), bk[4 + n][:, :]).then_inc(wt_ok, 1)
            dve.wait_ge(sh_hi, 1)
            dve.tensor_tensor(r(sh_l[:, :, :]), sh_up[:, :, :], sh_h[:, :, :], ALU.subtract)
            for k in range(KD):
                for v in range(2):
                    dve.wait_ge(up_hi, 2 * k + v + 1)
                    last = dve.tensor_tensor(r(UL[:, k, v, :].rearrange("p (e h) -> p e h", h=HE)),
                                             ew["up"][:, k, :, v * HE:(v + 1) * HE],
                                             UH[:, k, v, :].rearrange("p (e h) -> p e h", h=HE), ALU.subtract)
            link(last)
    small.close()

    SP_ = sb("spread", [P, NC, P])
    SG = sb("SG", [P, 2, TB])
    HT = sb("HT", [P, 2, TB])
    sp_ok = sem("spread_ready")
    g_ps = sem("gates_in_psum")
    v_ps = sem("values_in_psum")
    w_ps = sem("weights_in_psum")
    sg_ok = sem("silu_ready")
    hv = sem("hidden_unweighted")
    h_ok = sem("hidden_ready")
    dn = sem("chunks_added")
    o_read = sem("block_outputs_read")
    N1 = NC + 1

    with nc.Block() as block:
        @block.gpsimd
        def _(pool):
            pool.memset(SP_[:, :, :], 0.0).then_inc(sp_ok, 1)
            for n, base in enumerate((0, -NE)):
                pool.wait_ge(sp_ok, n + 1)
                v = SP_[:, :, :].rearrange("p c (e h) -> p c e h", h=HE)
                pool.affine_select(out=r(v), in_=v, compare_op=ALU.not_equal, fill=1.0, base=base,
                                   pattern=[[-EC, NC], [-1, EC], [0, HE]], channel_multiplier=1).then_inc(sp_ok, 1)

        def before(c):
            return c - 2 if c >= 2 else (NC - 1 if c else NC) - N1

        def blocks(eng, body):
            body(0, True)
            with eng.Fori(1, NTB) as tb:
                body(tb, False)

        @block.tensor
        def _(pe):
            pe.wait_ge(sp_ok, 3)

            def up(tb, c, first):
                tok = bass.ds(tb * TB, TB)
                rhs = [x[:, k, tok] for k in range(KD) for x in (XH, XH, XL)]
                for v, s in ((0, g_ps), (1, v_ps)) if c < NC else ((0, g_ps),):
                    if not first or c >= 2:
                        pe.wait_ge((sg_ok, hv)[v or c == 0], tb * N1 + (before(c) + 1))
                    if c < NC:
                        lhs = [x[:, k, v, c * P:(c + 1) * P] for k in range(KD) for x in (UH, UL, UH)]
                    else:
                        lhs = [x[:, k, :] for k in range(KD) for x in (sh_h, sh_l, sh_h)]
                    for n, (a, b) in enumerate(zip(lhs, rhs)):
                        mm = pe.matmul(bk[2 * (c % 2) + v][:, :], r(a), r(b), start=n == 0, stop=n == 3 * KD - 1)
                    mm.then_inc(s, 1)
                if c < NC:
                    if not first or c >= 2:
                        pe.wait_ge(h_ok, tb * N1 + (before(c) + 1))
                    pe.matmul(bk[4 + c % 2][:, :], r(SP_[:, c, :]), r(WT[:, tok]), start=True, stop=True).then_inc(w_ps, 1)

            def down(tb, c, first):
                pe.wait_ge(h_ok, tb * N1 + (c + 1))
                if c == 0 and not first:
                    pe.wait_ge(o_read, tb)
                rows = P if c < NC else HSH
                for i in range(TB // P):
                    mm = pe.matmul(bk[6 + i // 2][:, i % 2 * DM:(i % 2 + 1) * DM], HT[0:rows, c % 2, i * P:(i + 1) * P],
                                   ew["down"][:, c, :] if c < NC else sh_dn[:, :], start=c == 0 and i % 2 == 0,
                                   stop=c == NC and i % 2 == 1)
                mm.then_inc(dn, 1)

            def body(tb, first):
                for c in range(N1):
                    up(tb, c, first)
                    if c:
                        down(tb, c - 1, first)
                down(tb, NC, first)
            blocks(pe, body)

        @block.scalar
        def _(act):
            def body(tb, first):
                for c in range(N1):
                    rows = P if c < NC else HSH
                    act.wait_ge(g_ps, tb * N1 + (c + 1))
                    if not first or c >= 2:
                        act.wait_ge(hv, tb * N1 + (before(c) + 1))
                    act.activation(SG[0:rows, c % 2, :], bk[2 * (c % 2)][P - rows:P, :], ACT.Silu).then_inc(sg_ok, 1)
            blocks(act, body)

        @block.vector
        def _(dve):
            def body(tb, first):
                for c in range(N1):
                    rows = P if c < NC else HSH
                    dve.wait_ge(sg_ok, tb * N1 + (c + 1))
                    if c < NC:
                        dve.wait_ge(v_ps, tb * NC + (c + 1))
                    if not first or c >= 2:
                        dve.wait_ge(dn, tb * N1 + (before(c) + 1))
                    h = HT[0:rows, c % 2, :]
                    dve.tensor_tensor(h, SG[0:rows, c % 2, :], bk[2 * (c % 2) + (c < NC)][0:rows, :], ALU.mult).then_inc(hv, 1)
                    dve.wait_ge(hv, tb * N1 + (c + 1))
                    if c < NC:
                        dve.wait_ge(w_ps, tb * NC + (c + 1))
                        dve.tensor_tensor(h, h, bk[4 + c % 2][:, :], ALU.mult).then_inc(h_ok, 1)
                    else:
                        dve.nop().then_inc(h_ok, 1)
                dve.wait_ge(dn, tb * N1 + N1)
                for b in range(2):
                    x = x2[:, bass.ds(tb * 4 + 2 * b, 2), :].rearrange("p i d -> p (i d)")
                    o = dve.tensor_tensor(x, x, bk[6 + b][:, :], ALU.add)
                o.then_inc(o_read, 1)
            blocks(dve, body)


def decoder_layer(nc, tensors, out):
    of = lambda prefix: {n[len(prefix):]: a for n, a in tensors.items() if n.startswith(prefix)}
    with ExitStack() as ctx:
        ident = ctx.enter_context(nc.sbuf_tensor("ident", [P, P], F32))
        ones = ctx.enter_context(nc.sbuf_tensor("ones", [P, P], F32))
        x1 = ctx.enter_context(nc.sbuf_tensor("x1", [P, TT, DM], F32))
        memory(nc, dict(of("L0_attn_"), x=tensors["x"]), x1, ident, ones)
        ew = expert_weights(nc, ctx)
        with ExitStack() as c:
            cross_attention(nc, c, x1, dict(of("L0_xattn_"), ctx=tensors["ctx_2048"]), ident,
                            lambda sp: load_expert_weights(sp, ew, of("L0_ffn_")))
        with ExitStack() as c:
            layernorm(nc, c, x1, "ln2")
        with ExitStack() as c:
            experts(nc, c, x1, ew, of("L0_ffn_"), ident)
        with ExitStack() as c:
            layernorm(nc, c, x1, "ln3")
        stored = ctx.enter_context(nc.semaphore("stored"))
        with nc.Block() as block:
            @block.sync
            def _(sp):
                sp.dma_start(out.rearrange("b s d -> (b s) d").rearrange("(i p) d -> p i d", p=P), x1[:, :, :])\
                  .then_inc(stored, 16)
                sp.wait_ge(stored, 16)


_INS = ["x", "ctx_2048", "L0_attn_Wk", "L0_attn_Wv", "L0_attn_Wq", "L0_attn_fast_lambda", "L0_attn_slow_lambda",
        "L0_attn_Waf", "L0_attn_baf", "L0_attn_Was", "L0_attn_bas", "L0_attn_nm_w1", "L0_attn_nm_b1",
        "L0_attn_nm_w2", "L0_attn_nm_b2", "L0_attn_ir_w1", "L0_attn_ir_b1", "L0_attn_ir_w2", "L0_attn_ir_b2",
        "L0_attn_pw_w", "L0_attn_pw_b", "L0_attn_Wo", "L0_attn_norm_w", "L0_xattn_Wq", "L0_xattn_Wkv",
        "L0_xattn_Wout", "L0_xattn_bout", "L0_ffn_w_gate", "L0_ffn_w_shared_up", "L0_ffn_w_shared_down",
        "L0_ffn_w_up", "L0_ffn_w_down"]


def kernel(**inputs):
    import numpy as _np
    import concourse.bacc as _bacc
    from concourse import mybir as _mybir
    from concourse.bass_utils import run_bass_kernel_spmd as _run

    nc = _bacc.Bacc("TRN2", target_bir_lowering=False, num_devices=1)
    arrays, tensors = {}, {}
    for name in _INS:
        a = _np.ascontiguousarray(inputs[name])
        arrays[f"in_{name}_dram"] = a
        tensors[name] = nc.dram_tensor(f"in_{name}_dram", a.shape, _mybir.dt.from_np(a.dtype), kind="ExternalInput").ap()
    out = nc.dram_tensor("out_0_dram", (NB, NS, DM), _mybir.dt.float32, kind="ExternalOutput").ap()
    decoder_layer(nc, tensors, out)
    r = _run(nc, [arrays], core_ids=[0])
    return r.results[0]["out_0_dram"]
```

```python
import numpy as np
from contextlib import ExitStack

import concourse.bass as bass
from concourse import mybir

F32 = mybir.dt.float32
F32R = mybir.dt.float32r
ACT = mybir.ActivationFunctionType
ALU = mybir.AluOpType
AX = mybir.AxisListType

P = 128
NB, NS, DM = 32, 64, 256
NT = NB * NS
KD = DM // P
TT = NT // P
CH = 4
NCH = NS // CH
CW = CH * NB
BW = 512
NBK = NT // BW
LN_EPS, RMS_EPS = 1e-5, 1e-6
PAIRS = [(s, n) for s in range(CH) for n in range(s + 1, CH)]
KQ_AT = [sum(CH - 1 - r for r in range(s)) for s in range(CH)]
O_AT = [sum(CH - r for r in range(s)) for s in range(CH)]
NKQ, NO = len(PAIRS), CH * (CH + 1) // 2


def memory_inputs(nc, ctx, pr, dram):
    sb = lambda n, s: ctx.enter_context(nc.sbuf_tensor(n, s, F32))
    sem = lambda n: ctx.enter_context(nc.semaphore(n))
    x_tok = sb("x_tok", [P, TT, DM])
    xT = sb("xT", [P, KD, NT])
    names = ["Waf", "Was", "ir_w1", "Wk", "Wq", "Wv"]
    w_in = {n: sb("w_" + n, [P, KD, P]) for n in names}
    nm_w1 = sb("nm_w1", [P, 2 * P])
    nm_w2 = sb("nm_w2", [P, 2, P])
    pw_w = sb("pw_w", [P, KD, 3])
    vec = sb("vec", [P, 16])
    BAF, BAS, NB1, NB2, IRB1, IRB2, IRW2, LAM, LOG, TINY = (
        vec[:, 0:1], vec[:, 1:2], vec[:, 2:4], vec[:, 4:5], vec[:, 5:6], vec[:, 6:7], vec[:, 7:8],
        vec[:, 8:10], vec[:, 10:12], vec[:, 12:13])
    pwb = sb("pwb", [P, 3])
    imp_w = sb("imp_w", [P, P])
    hid_i = sb("hid_i", [P, NT])
    hid_n = sb("hid_n", [P, 2, NT])
    sq = sb("sq", [P, 2, BW])
    upd = sb("upd", [P, NT])
    pwx = sb("pwx", [P, TT, 3])
    pws = sb("pws", [P, TT, 4])
    KQ, A, F4, W, S, NU, O, pw, ident, ones = (
        pr[n] for n in ("KQ", "A", "F4", "W", "S", "NU", "O", "pw", "ident", "ones"))
    bank = [ctx.enter_context(nc.psum_tensor(f"bank{i}", [P, BW], F32)) for i in range(6)]
    NBANK = len(bank)

    jobs = []
    for c in range(KD):
        for n in range(NBK):
            jobs.append(("xT", c, n, "act" if n % 2 else "dve"))
    jobs += [(w, 0, n, "dve") for w in ("Wk", "Wq") for n in range(NBK)]
    jobs += [(w, 0, n, "act") for w in ("Waf", "Was") for n in range(NBK)]
    jobs += [("norm", w, n, "act") for w in range(2) for n in range(NBK)]
    jobs += [("pw", 0, 0, "dve")]
    jobs += [("Wv", 0, n, "dve") for n in range(NBK)]
    jobs += [("ir_w1", 0, n, "act") for n in range(NBK)]
    jobs += [("hid_n", m, n, "act") for n in range(NBK) for m in range(2)]
    jobs += [("imp", 0, n, "act") for n in range(NBK)]
    jobs += [("nu", 0, n, "act") for n in range(NBK)]
    order = {}
    count = {"act": 0, "dve": 0}
    for j, job in enumerate(jobs):
        count[job[3]] += 1
        order[j] = count[job[3]]
    place = {job[:3]: j for j, job in enumerate(jobs)}

    x_in = sem("x_in")
    w_loaded = sem("w_loaded")
    made = sem("bank_filled")
    freed = {"act": sem("bank_read_act"), "dve": sem("bank_read_dve")}
    consts = sem("consts_ready")
    squares = sem("squares_ready")
    logits = sem("path_logits_ready")
    act_own = sem("act_own")
    dve_own = sem("dve_own")
    pool_own = sem("pool_own")
    alpha = sem("alpha_ready")
    impw = sem("importance_weights_ready")
    keys = sem("keys_ready")
    vcopy = sem("values_copied")

    def filled(eng, job):
        eng.wait_ge(made, place[job] + 1)

    with nc.Block() as block:
        @block.sync
        def _(sp):
            sp.dma_start(x_tok[:, :, :], dram["x"].rearrange("b s d -> (b s) d")
                         .rearrange("(i p) d -> p i d", p=P)).then_inc(x_in, 16)
            for n in names:
                sp.dma_start(w_in[n][:, :, :], dram[n].rearrange("(c p) m -> p c m", p=P)).then_inc(w_loaded, 16)
            sp.dma_start(nm_w1[:, :], dram["nm_w1"]).then_inc(w_loaded, 16)
            sp.dma_start(nm_w2[:, :, :], dram["nm_w2"].rearrange("(c p) m -> p c m", p=P)).then_inc(w_loaded, 16)
            sp.dma_start(pw_w[:, :, :], dram["pw_w"].rearrange("(c p) m -> p c m", p=P)).then_inc(w_loaded, 16)
            col = lambda a: a.rearrange("(p o) -> p o", o=1)
            for to, a in ((BAF, col(dram["baf"])), (BAS, col(dram["bas"])), (NB2, col(dram["nm_b2"])),
                          (IRB1, col(dram["ir_b1"])), (IRW2, dram["ir_w2"]),
                          (LAM[:, 0:1], col(dram["fast_lambda"])), (LAM[:, 1:2], col(dram["slow_lambda"])),
                          (NB1[:, 0:1], col(dram["nm_b1"][0:P])), (NB1[:, 1:2], col(dram["nm_b1"][P:2 * P])),
                          (IRB2, dram["ir_b2"].partition_broadcast(P)),
                          (pwb[:, :], dram["pw_b"].partition_broadcast(P))):
                sp.dma_start(to, a).then_inc(w_loaded, 16)
        W_ALL = 16 * (len(names) + 3 + 11)

        @block.gpsimd
        def _(pool):
            pool.memset(ident[:, :], 0.0).then_inc(pool_own, 1)
            pool.memset(ones[:, :], 1.0).then_inc(consts, 1)
            pool.memset(TINY, 1e-8).then_inc(consts, 1)
            pool.wait_ge(pool_own, 1)
            pool.affine_select(out=ident[:, :], in_=ident[:, :], compare_op=ALU.not_equal, fill=1.0,
                               base=0, pattern=[[-1, P]], channel_multiplier=1).then_inc(consts, 1)
            pool.memset(O[:, :, :], 0.0)
            for w in range(2):
                for n in range(NBK):
                    i = w * NBK + n
                    pool.wait_ge(freed["dve"], order[place[("Wk" if w == 0 else "Wq", 0, n)]])
                    if i >= 2:
                        pool.wait_ge(made, place[("norm", (i - 2) // NBK, (i - 2) % NBK)] + 1)
                    cols = KQ[:, w, n * BW:(n + 1) * BW]
                    pool.tensor_tensor(sq[:, i % 2, :], cols, cols, ALU.mult).then_inc(squares, 1)
            pool.wait_ge(freed["dve"], order[place[("Wv", 0, NBK - 1)]])
            pool.tensor_copy(S[:, 1, 0, :], S[:, 0, 0, :]).then_inc(vcopy, 1)
            pool.tensor_copy(S[:, 0, 1, :], S[:, 0, 0, :]).then_inc(vcopy, 1)
            pool.memset(S[:, 1, 1, :], 0.0).then_inc(vcopy, 1)
            pool.wait_ge(alpha, 2)
            own = 1

            def link(ins):
                nonlocal own
                own += 1
                ins.then_inc(pool_own, 1)
                pool.wait_ge(pool_own, own)

            chunks = lambda x, t: x.rearrange("p m (j t b) -> p m j t b", t=CH, b=NB)[:, :, :, t, :]
            link(pool.tensor_copy(chunks(F4[:, :, :], 0), chunks(A[:, :, :], 0)))
            for t in range(1, CH):
                link(pool.tensor_tensor(chunks(F4[:, :, :], t), chunks(F4[:, :, :], t - 1), chunks(A[:, :, :], t), ALU.mult))
            pool.wait_ge(vcopy, 3)

        @block.tensor
        def _(pe):
            pe.wait_ge(consts, 3)
            for j, (what, c, n, _) in enumerate(jobs):
                ps = bank[j % NBANK]
                if j >= NBANK:
                    last = j - NBANK
                    pe.wait_ge(freed[jobs[last][3]], order[last])
                tok = slice(n * BW, (n + 1) * BW)
                if what == "xT":
                    if j == 0:
                        pe.wait_ge(x_in, 16)
                    for i in range(4):
                        mm = pe.transpose(ps[:, i * P:(i + 1) * P], x_tok[:, 4 * n + i, c * P:(c + 1) * P], ident[:, :])
                elif what in w_in:
                    if (what, n) == ("Wk", 0):
                        pe.wait_ge(w_loaded, W_ALL)
                        for e in ("act", "dve"):
                            pe.wait_ge(freed[e], KD * NBK // 2)
                    for k in range(KD):
                        mm = pe.matmul(ps[:, :], w_in[what][:, k, :], xT[:, k, tok], start=k == 0, stop=k == KD - 1)
                elif what == "norm":
                    pe.wait_ge(squares, c * NBK + n + 1)
                    mm = pe.matmul(ps[:, :], ones[:, :], sq[:, (c * NBK + n) % 2, :], start=True, stop=True)
                elif what == "hid_n":
                    pe.wait_ge(freed["dve"], order[place[("Wv", 0, n)]])
                    mm = pe.matmul(ps[:, :], nm_w1[:, c * P:(c + 1) * P], S[:, 0, 0, tok], start=True, stop=True)
                elif what == "imp":
                    pe.wait_ge(impw, 1)
                    pe.wait_ge(freed["act"], order[place[("ir_w1", 0, n)]])
                    mm = pe.matmul(ps[:, :], imp_w[:, :], hid_i[:, tok], start=True, stop=True)
                elif what == "nu":
                    pe.wait_ge(freed["act"], order[place[("hid_n", 1, n)]])
                    for k in range(2):
                        mm = pe.matmul(ps[:, :], nm_w2[:, k, :], hid_n[:, k, tok], start=k == 0, stop=k == 1)
                elif what == "pw":
                    for i in range(TT):
                        for k in range(KD):
                            mm = pe.matmul(ps[:, 3 * i:3 * i + 3], xT[:, k, i * P:(i + 1) * P], pw_w[:, k, :],
                                           start=k == 0, stop=k == KD - 1)
                mm.then_inc(made, 1)

        def empty_xT(eng, c, n, mine):
            copy = eng.activation if mine == "act" else eng.tensor_copy
            src = bank[place[("xT", c, n)] % NBANK][:, :].rearrange("p (b s) -> p s b", s=NS)
            dst = xT[:, c, :].rearrange("p (s b) -> p s b", b=NB)[:, :, 8 * n:8 * n + 8]
            if mine == "act":
                eng.activation(dst, src, ACT.Copy).then_inc(freed["act"], 1)
            else:
                eng.tensor_copy(dst, src).then_inc(freed["dve"], 1)

        @block.scalar
        def _(act):
            def alphas():
                act.activation(LOG, LOG, ACT.Ln, bias=TINY).then_inc(act_own, 1)
                act.wait_ge(act_own, 2)
                act.activation(LOG, LOG, ACT.Copy, scale=8.0).then_inc(act_own, 1)
                act.wait_ge(act_own, 3)
                act.wait_ge(freed["act"], order[place[("Was", 0, NBK - 1)]])
                for m in range(2):
                    act.activation(A[:, m, :], A[:, m, :], ACT.Exp, scale=LOG[:, m:m + 1]).then_inc(alpha, 1)
                act.wait_ge(logits, 1)
                act.activation(pwx[:, :, :], pwx[:, :, :], ACT.Exp).then_inc(alpha, 1)

            act.wait_ge(consts, 3)
            act.wait_ge(w_loaded, W_ALL)
            act.activation(LOG, LAM, ACT.Sigmoid).then_inc(act_own, 1)
            act.wait_ge(act_own, 1)
            for (what, c, n, mine) in [j for j in jobs if j[3] == "act"]:
                ps = bank[place[(what, c, n)] % NBANK][:, :]
                tok = slice(n * BW, (n + 1) * BW)
                filled(act, (what, c, n))
                if what == "xT":
                    empty_xT(act, c, n, "act")
                elif what in ("Waf", "Was"):
                    m = 0 if what == "Waf" else 1
                    act.activation(A[:, m, tok], ps, ACT.Sigmoid, bias=(BAF, BAS)[m]).then_inc(freed["act"], 1)
                elif what == "ir_w1":
                    act.activation(hid_i[:, tok], ps, ACT.Gelu, bias=IRB1).then_inc(freed["act"], 1)
                elif what == "norm":
                    act.activation(W[:, c, tok], ps, ACT.Sqrt).then_inc(freed["act"], 1)
                    if (c, n) == (1, NBK - 1):
                        alphas()
                elif what == "hid_n":
                    act.activation(hid_n[:, c, tok], ps, ACT.Gelu, bias=NB1[:, c:c + 1]).then_inc(freed["act"], 1)
                elif what == "imp":
                    act.activation(upd[:, tok], ps, ACT.Sigmoid, bias=IRB2).then_inc(freed["act"], 1)
                elif what == "nu":
                    act.activation(NU[:, tok], ps, ACT.Identity, bias=NB2).then_inc(freed["act"], 1)
        @block.vector
        def _(dve):
            own = 0
            dve.wait_ge(consts, 3)
            dve.wait_ge(w_loaded, W_ALL)
            dve.tensor_scalar(imp_w[:, :], ones[:, :], IRW2, None, ALU.mult).then_inc(impw, 1)
            def link(ins):
                nonlocal own
                own += 1
                ins.then_inc(dve_own, 1)
                dve.wait_ge(dve_own, own)

            def unit_length(i):
                w, n = divmod(i, NBK)
                dve.wait_ge(freed["act"], order[place[("norm", w, n)]])
                part = W[:, w, n * BW:(n + 1) * BW]
                link(dve.tensor_scalar(part, part, 1e-12, None, ALU.max))
                link(dve.reciprocal(part, part))
                cols = KQ[:, w, n * BW:(n + 1) * BW]
                dve.scalar_tensor_tensor(cols, cols, 0.5 if w else 1.0, part, ALU.mult, ALU.mult).then_inc(keys, 1)

            for (what, c, n, mine) in [j for j in jobs if j[3] == "dve"]:
                ps = bank[place[(what, c, n)] % NBANK][:, :]
                tok = slice(n * BW, (n + 1) * BW)
                if what == "pw":
                    unit_length(0)
                    unit_length(1)
                    filled(dve, ("pw", 0, 0))
                    ps = ps[:, 0:3 * TT].rearrange("p (i j) -> p i j", j=3)
                    dve.tensor_tensor(pwx[:, :, :], ps, pwb[:, :].unsqueeze(1).broadcast_to((P, TT, 3)),
                                      ALU.add).then_inc(freed["dve"], 1)
                    dve.wait_ge(freed["dve"], order[place[("pw", 0, 0)]])
                    link(dve.tensor_reduce(pws[:, :, 0:1], pwx[:, :, :], AX.X, ALU.max))
                    dve.tensor_tensor(pwx[:, :, :], pwx[:, :, :], pws[:, :, 0:1].broadcast_to((P, TT, 3)),
                                      ALU.subtract).then_inc(logits, 1)
                    continue
                filled(dve, (what, c, n))
                if what == "xT":
                    empty_xT(dve, c, n, "dve")
                elif what == "Wv":
                    dve.tensor_copy(S[:, 0, 0, tok], ps).then_inc(freed["dve"], 1)
                    if n == 0:
                        unit_length(2)
                else:
                    dve.tensor_copy(KQ[:, 0 if what == "Wk" else 1, tok], ps).then_inc(freed["dve"], 1)
            for i in range(3, 2 * NBK):
                unit_length(i)
            dve.wait_ge(alpha, 3)
            link(dve.tensor_reduce(pws[:, :, 1:2], pwx[:, :, :], AX.X, ALU.add))
            link(dve.reciprocal(pws[:, :, 2:3], pws[:, :, 1:2]))
            link(dve.tensor_tensor(pw[:, :, :], pwx[:, :, :], pws[:, :, 2:3].broadcast_to((P, TT, 3)), ALU.mult))
            dve.wait_ge(keys, 2 * NBK)
            for m in range(2):
                link(dve.tensor_scalar(W[:, m, :], A[:, m, :], -1.0, 1.0, ALU.mult, ALU.add))
                link(dve.tensor_tensor(W[:, m, :], W[:, m, :], KQ[:, 0, :], ALU.mult))
            dve.wait_ge(freed["act"], order[place[("imp", 0, NBK - 1)]])
            link(dve.scalar_tensor_tensor(W[:, 1, :], upd[:, :], 0.5, W[:, 1, :], ALU.is_gt, ALU.mult))


def recurrence(nc, ctx, pr):
    sb = lambda n, s: ctx.enter_context(nc.sbuf_tensor(n, s, F32))
    sem = lambda n: ctx.enter_context(nc.semaphore(n))
    KQ, A, F4, W, S, O, ident, ones = (pr[n] for n in ("KQ", "A", "F4", "W", "S", "O", "ident", "ones"))
    LV = {n: (n & -n) * CH for n in range(1, NCH)}
    HMAX = max(LV.values())
    nblk = lambda n: 2 * LV[n] // CH
    total = lambda n: sum(nblk(m) for m in range(1, n))
    groups = lambda n: -(-nblk(n) // 4)
    turned = lambda n: sum(groups(m) for m in range(1, n))
    gathers = lambda n: sum(2 * groups(m) for m in range(1, n) if LV[m] > CH)
    both = lambda n: LV[n] * NB * 2 <= HMAX * NB
    block_order = lambda n: list(range(nblk(n))) if both(n) else [*range(0, nblk(n), 2), *range(1, nblk(n), 2)]
    parts = lambda n: [sum(1 if both(m) else 2 for m in range(1, n)) + (1 if both(n) else 1 + i) for i in range(2)]

    Fd = sb("Fd", [P, 2, CH, CH, NB])
    PK = sb("PK", [P, 2, 2, 2, NKQ, NB])
    PO = sb("PO", [P, 2, 2, NO, NB])
    C = sb("C", [P, 2, 2, 2, NKQ, NB])
    CO = sb("CO", [P, 2, 2, NO, NB])
    DD = sb("DD", [P, 2, HMAX // CH - 2, NB])
    LW = sb("LW", [P, HMAX * NB])
    LL = sb("LL", [P, 3 * HMAX * NB])
    LL4 = sb("LL4", [P, 2 * 3 * CW])
    G1 = sb("G1", [P, 2, 3 * P])
    G2 = sb("G2", [P, 2 * HMAX // CH, 3 * P])
    UG = sb("UG", [P, 2, 4, P])
    UT = sb("UT", [P, 2, 4, P])
    sqr = sb("sqr", [P, NB])
    perr = sb("perr", [P, NB])
    tk = sb("tk", [P, 2, CH - 1, NB])
    tq = sb("tq", [P, 2, CH - 1, NB])
    tq1 = sb("tq1", [P, 2, NB])
    to = sb("to", [P, 2, CH, NB])
    hs = sorted(set(LV.values()))
    sel = LL[:, 0:len(hs) * P].rearrange("p (i c) -> p i c", c=P)
    mask = {h: sb(f"mask{h}", [P, P]) for h in hs}
    psE = ctx.enter_context(nc.psum_tensor("psE", [P, BW], F32))
    psC = [ctx.enter_context(nc.psum_tensor(f"psC{i}", [P, BW], F32)) for i in range(2)]
    psG = [ctx.enter_context(nc.psum_tensor(f"psG{i}", [P, BW], F32)) for i in range(2)]
    psT = ctx.enter_context(nc.psum_tensor("psT", [P, BW], F32))
    psR = [ctx.enter_context(nc.psum_tensor(f"psR{i}", [P, BW], F32)) for i in range(2)]

    pool_own = sem("pool_own2")
    sel_ok = sem("selectors_ready")
    mask_psum = sem("masks_in_psum")
    masks = sem("masks_ready")
    sq_ready = sem("error_squares_ready")
    err_ready = sem("errors_ready")
    sur_ready = sem("surprises_ready")
    u_ready = sem("u_ready")
    mul_done = sem("coefficients_read")
    terms = sem("coefficient_terms_ready")
    coef = sem("coefficients_in_psum")
    coef_out = sem("coefficients_ready")
    lw_ready = sem("decayed_ready")
    g_psum = sem("blocks_in_psum")
    g_ready = sem("blocks_ready")
    ug_ready = sem("u_gathered")
    t_psum = sem("transposes_in_psum")
    t_ready = sem("transposes_ready")
    r_psum = sem("reads_in_psum")
    r_done = sem("reads_added")
    dve_own = sem("dve_own2")

    def g_slot(n, i):
        return G1[:, i, :] if LV[n] == CH else G2[:, i, :]

    def slices(n):
        b = nblk(n)
        return [range(b * i // CH, b * (i + 1) // CH) for i in range(CH)]

    pieces = lambda n, i: [4 * n + x for x in ((0,), (1,), (2, 3), ())[i]] if n < NCH else []
    cols = lambda t, n=1: slice(t * NB, (t + n) * NB)

    with nc.Block() as block:
        @block.gpsimd
        def _(pool):
            own = 0

            def link(ins):
                nonlocal own
                own += 1
                ins.then_inc(pool_own, 1)
                pool.wait_ge(pool_own, own)

            def terms_of(j):
                part = lambda x, k: x[:, :, cols(j * CH, CH)].rearrange("p m (t b) -> p m t b", b=NB)
                a_, w_, kq = part(A, 2), part(W, 2), part(KQ, 2)
                flat = Fd[:, :, :, :, :].rearrange("p m s t b -> p m (s t) b")
                link(pool.tensor_copy(flat[:, :, 0:CH * CH:CH + 1, :], w_))
                for l in range(1, CH):
                    n = CH - l
                    at = lambda k: slice(k, k + (n - 1) * (CH + 1) + 1, CH + 1)
                    link(pool.tensor_tensor(flat[:, :, at(l), :], flat[:, :, at(l - 1), :], a_[:, :, l:CH, :], ALU.mult))
                if j >= 2:
                    pool.wait_ge(coef, 4 * (j - 1))
                for s in range(CH - 1):
                    n = CH - 1 - s
                    for kind in range(2):
                        pool.tensor_tensor(PK[:, j % 2, :, kind, KQ_AT[s]:KQ_AT[s] + n, :], Fd[:, :, s, s:CH - 1, :],
                                           kq[:, kind, s + 1:CH, :].unsqueeze(1).broadcast_to((P, 2, n, NB)), ALU.mult)
                for s in range(CH):
                    n = CH - s
                    mul = pool.tensor_tensor(PO[:, j % 2, :, O_AT[s]:O_AT[s] + n, :], Fd[:, :, s, s:CH, :],
                                             kq[:, 1, s:CH, :].unsqueeze(1).broadcast_to((P, 2, n, NB)), ALU.mult)
                mul.then_inc(terms, 1)
                link(pool.tensor_copy(w_, flat[:, :, CH - 1:CH * CH:CH, :]))
                pool.wait_ge(terms, j + 1)

            def decays_of(n):
                h, c = LV[n], n * CH
                g, q = P // h, h // CH
                whole = lambda j: F4[:, :, cols(j * CH + CH - 1)]
                over = lambda d, i: whole((n, n - 1)[d]) if i == 1 else DD[:, :, i - 2, :]

                def over_chunks(d):
                    for i in range(2, q):
                        link(pool.tensor_tensor(DD[:, :, i - 2, :], over(d, i - 1), whole(n - i if d else n + i - 1), ALU.mult))
                for ms in ([(0, 1)] if both(n) else [(0,), (1,)]):
                    if ms == (1,):
                        pool.wait_ge(g_psum, total(n) + nblk(n) // 2)
                    elif n >= 3:
                        pool.wait_ge(g_psum, total(n - 1))
                    m0, nm = ms[0], len(ms)
                    mm = slice(m0, m0 + nm)
                    ll = (LL if h > CH else LL4)[:, 0:nm * 3 * h * NB].rearrange("p (m k c) -> p m k c", m=nm, k=3)
                    if h > CH:
                        over_chunks(1)
                        for m in ms:
                            dst = LW[:, (m - m0) * h * NB:(m - m0 + 1) * h * NB].rearrange("p (g t b) -> p g t b", t=h, b=g)
                            for i in range(q):
                                t0 = h - CH * (i + 1)
                                src = W[:, m, cols(c - h + t0, CH)].rearrange("p (t g b) -> p g t b", t=CH, b=g)
                                out = dst[:, :, t0:t0 + CH, :]
                                if i:
                                    e = over(1, i)[:, m, :].rearrange("p (g b) -> p g b", b=g).unsqueeze(2)\
                                        .broadcast_to((P, NB // g, CH, g))
                                    last = pool.tensor_tensor(out, src, e, ALU.mult)
                                else:
                                    pool.tensor_copy(out, src)
                        link(last)
                        over_chunks(0)
                        pool.tensor_copy(ll[:, :, 2, 0:CW], F4[:, mm, cols(c, CH)])
                        for i in range(1, q):
                            dec = pool.tensor_tensor(
                                ll[:, :, 2, i * CW:(i + 1) * CW].rearrange("p m (t b) -> p m t b", b=NB),
                                F4[:, mm, cols(c + i * CH, CH)].rearrange("p m (t b) -> p m t b", b=NB),
                                over(0, i)[:, mm, :].unsqueeze(2).broadcast_to((P, nm, CH, NB)), ALU.mult)
                        link(dec)
                    dec = ll[:, :, 2, :] if h > CH else F4[:, mm, cols(c, CH)]
                    pool.tensor_copy(ll[:, :, 0:2, 0:NB], KQ[:, :, cols(c)].unsqueeze(1).broadcast_to((P, nm, 2, NB)))
                    for kind in range(2):
                        mul = pool.tensor_tensor(ll[:, :, kind, NB:h * NB], dec[:, :, 0:(h - 1) * NB],
                                                 KQ[:, kind, cols(c + 1, h - 1)].unsqueeze(1).broadcast_to((P, nm, (h - 1) * NB)), ALU.mult)
                    link(mul)
                    pool.tensor_tensor(ll[:, :, 2, :], dec, KQ[:, 1, cols(c, h)].unsqueeze(1).broadcast_to((P, nm, h * NB)),
                                       ALU.mult).then_inc(lw_ready, 1)
                    pool.wait_ge(lw_ready, parts(n)[m0])

            link(pool.memset(sel, 0.0))
            for i, h in enumerate(hs):
                g = P // h
                v = sel[0:g, i, :].rearrange("p (t b) -> p t b", b=g)
                pool.affine_select(out=v, in_=v, compare_op=ALU.not_equal, fill=1.0, base=0,
                                   pattern=[[0, h], [-1, g]], channel_multiplier=1).then_inc(sel_ok, 1)
            terms_of(0)
            pool.wait_ge(mask_psum, 1)
            decays_of(1)
            for j in range(1, NCH):
                terms_of(j)
                if j + 1 < NCH:
                    decays_of(j + 1)

        def piece(x):
            j, i = divmod(x, 4)
            m = i % 2
            if i < 2:
                return (PK[:, j % 2, m, :, :, :].rearrange("p k n b -> p (k n b)"),
                        C[:, j % 2, m, :, :, :].rearrange("p k n b -> p (k n b)"), 2 * NKQ * NB)
            return (PO[:, j % 2, m, :, :].rearrange("p n b -> p (n b)"),
                    CO[:, j % 2, m, :, :].rearrange("p n b -> p (n b)"), NO * NB)

        @block.tensor
        def _(pe):
            def sum_piece(x):
                src, _, n = piece(x)
                pe.wait_ge(terms, x // 4 + 1)
                if x >= 2:
                    pe.wait_ge(coef_out, x - 1)
                pe.matmul(psC[x % 2][:, 0:n], ones[:, :], src, start=True, stop=True).then_inc(coef, 1)

            def make_block(n, at):
                h, i = LV[n], block_order(n)[at]
                gi, m = divmod(i, 2)
                g = P // h
                k = total(n) + at
                pe.wait_ge(lw_ready, parts(n)[m])
                if k >= 2:
                    pe.wait_ge(g_ready, k - 1)
                off = m if both(n) else 0
                rhs = (LL if h > CH else LL4)[:, off * 3 * h * NB:(off + 1) * 3 * h * NB].rearrange("p (k t b) -> p k t b", k=3, b=NB)
                lhs = W[:, m, cols((n - 1) * CH, CH)] if h == CH else LW[:, off * h * NB + gi * P:off * h * NB + (gi + 1) * P]
                pe.matmul(psG[k % 2][:, 0:3 * P], lhs, rhs[:, :, :, gi * g:(gi + 1) * g], start=True, stop=True)\
                  .then_inc(g_psum, 1)

            def turn(n, gr):
                k = turned(n) + gr
                if k >= 1:
                    pe.wait_ge(t_ready, k)
                if LV[n] > CH:
                    pe.wait_ge(ug_ready, gathers(n) + 2 * (gr + 1))
                else:
                    pe.wait_ge(u_ready, n * CH)
                for i in range(min(4, nblk(n))):
                    src = S[:, i, 0, cols((n - 1) * CH, CH)] if LV[n] == CH else UG[:, k % 2, i, :]
                    mm = pe.transpose(psT[:, i * P:(i + 1) * P], src, ident[:, :])
                mm.then_inc(t_psum, 1)

            def read(n, gr):
                for i in range(4 * gr, min(4 * gr + 4, nblk(n))):
                    k = total(n) + i
                    pe.wait_ge(t_ready, turned(n) + gr + 1)
                    pe.wait_ge(g_ready, k + 1)
                    if k >= 2:
                        pe.wait_ge(r_done, k - 1)
                    pe.matmul(psR[k % 2][:, 0:3 * P], UT[:, (turned(n) + gr) % 2, i % 4, :], g_slot(n, i),
                              start=True, stop=True).then_inc(r_psum, 1)

            def boundary(n):
                for gr in range(groups(n)):
                    turn(n, gr)
                    if gr:
                        read(n, gr - 1)
                read(n, groups(n) - 1)

            pe.wait_ge(sel_ok, len(hs))
            for i, h in enumerate(hs):
                g = P // h
                mm = pe.matmul(psT[:, i * P:(i + 1) * P], sel[0:g, i, :], sel[0:g, i, :], start=True, stop=True)
            mm.then_inc(mask_psum, 1)
            pe.wait_ge(masks, len(hs))
            for x in range(4):
                sum_piece(x)
            for i in range(nblk(1)):
                make_block(1, i)
            for t in range(NS):
                j, i = divmod(t, CH)
                pe.wait_ge(sq_ready, t + 1)
                pe.matmul(psE[:, 0:NB], ones[:, :], sqr[:, :], start=True, stop=True).then_inc(err_ready, 1)
                if i == CH - 1 and j + 1 < NCH:
                    boundary(j + 1)
                for x in pieces(j + 1, i):
                    sum_piece(x)
                if j + 2 < NCH:
                    for b in slices(j + 2)[i]:
                        make_block(j + 2, b)

        @block.scalar
        def _(act):
            def empty_piece(x):
                _, dst, n = piece(x)
                j = x // 4
                act.wait_ge(coef, x + 1)
                if j >= 2:
                    act.wait_ge(mul_done, (j - 1) * CH)
                act.activation(dst, psC[x % 2][:, 0:n], ACT.Copy).then_inc(coef_out, 1)

            for x in range(4):
                empty_piece(x)
            for t in range(NS):
                j, i = divmod(t, CH)
                act.wait_ge(err_ready, t + 1)
                act.activation(S[:, 1, 1, cols(t)], psE[:, 0:NB], ACT.Sigmoid, scale=1.0 / (1.0 + 1e-6))\
                   .then_inc(sur_ready, 1)
                for x in pieces(j + 1, i):
                    empty_piece(x)
                if i == CH - 1 and j + 1 < NCH:
                    n = j + 1
                    h = LV[n]
                    g = P // h
                    for gr in range(groups(n) + 1):
                        k = turned(n) + gr
                        if h > CH and gr < groups(n):
                            act.wait_ge(u_ready, n * CH)
                            if k >= 2:
                                act.wait_ge(t_psum, k - 1)
                            for m in range(2):
                                src = S[:, m, 0, cols(n * CH - h, h)].rearrange("p (t b) -> p t b", b=NB)
                                src = src[:, :, 2 * gr * g:2 * (gr + 1) * g].rearrange("p t (g b) -> p g t b", b=g)
                                act.activation(UG[:, k % 2, m:4:2, :].rearrange("p g (t b) -> p g t b", b=g), src,
                                               ACT.Copy).then_inc(ug_ready, 1)
                        if gr:
                            k -= 1
                            size = min(4, nblk(n))
                            if k >= 2:
                                act.wait_ge(r_psum, [total(x) + min(4 * y + 4, nblk(x)) for x in sorted(LV)
                                                     for y in range(groups(x))][k - 2])
                            act.wait_ge(t_psum, k + 1)
                            act.activation(UT[:, k % 2, 0:size, :], psT[:, 0:size * P], ACT.Copy).then_inc(t_ready, 1)

        @block.vector
        def _(dve):
            own = 0

            def mark(ins):
                nonlocal own
                own += 1
                ins.then_inc(dve_own, 1)
                return own

            def keep_block(n, at):
                i = block_order(n)[at]
                k = total(n) + at
                dve.wait_ge(g_psum, k + 1)
                if n >= 3:
                    dve.wait_ge(r_psum, total(n - 1))
                dve.tensor_tensor(g_slot(n, i).rearrange("p (k c) -> p k c", k=3),
                                  psG[k % 2][:, 0:3 * P].rearrange("p (k c) -> p k c", k=3),
                                  mask[LV[n]][:, :].unsqueeze(1).broadcast_to((P, 3, P)), ALU.mult).then_inc(g_ready, 1)

            def square_error(t):
                dve.wait_ge(dve_own, mark(dve.tensor_tensor(perr[:, :], S[:, 0, 1, cols(t)], S[:, 1, 1, cols(t)], ALU.add)))
                dve.tensor_tensor(sqr[:, :], perr[:, :], perr[:, :], ALU.mult).then_inc(sq_ready, 1)

            dve.wait_ge(mask_psum, 1)
            for i, h in enumerate(hs):
                dve.tensor_copy(mask[h][:, :], psT[:, i * P:(i + 1) * P]).then_inc(masks, 1)
            dve.wait_ge(masks, len(hs))
            square_error(0)
            for i in range(nblk(1)):
                keep_block(1, i)
            keys_done = 0
            for t in range(NS):
                j, i = divmod(t, CH)
                c0 = j * CH
                u = S[:, :, 0, cols(t)]
                row = lambda n: u.unsqueeze(2).broadcast_to((P, 2, n, NB))
                dve.wait_ge(sur_ready, t + 1)
                if keys_done:
                    dve.wait_ge(dve_own, keys_done)
                dve.tensor_tensor(u, u, S[:, 1, 1, cols(t)].unsqueeze(1).broadcast_to((P, 2, NB)), ALU.mult)\
                   .then_inc(u_ready, 1)
                if i == 0:
                    dve.wait_ge(coef_out, 4 * (j + 1))
                dve.wait_ge(u_ready, t + 1)
                n = CH - 1 - i
                if n:
                    dve.wait_ge(dve_own, mark(dve.tensor_tensor(tq1[:, :, :], C[:, j % 2, :, 1, KQ_AT[i], :], u, ALU.mult)))
                    nxt = S[:, :, 1, cols(t + 1)]
                    dve.wait_ge(dve_own, mark(dve.tensor_tensor(nxt, nxt, tq1[:, :, :], ALU.subtract)))
                    square_error(t + 1)
                if n:
                    dve.tensor_tensor(tk[:, :, 0:n, :], C[:, j % 2, :, 0, KQ_AT[i]:KQ_AT[i] + n, :], row(n), ALU.mult)
                if n > 1:
                    dve.tensor_tensor(tq[:, :, 1:n, :], C[:, j % 2, :, 1, KQ_AT[i] + 1:KQ_AT[i] + n, :], row(n - 1), ALU.mult)
                dve.tensor_tensor(to[:, :, 0:n + 1, :], CO[:, j % 2, :, O_AT[i]:O_AT[i] + n + 1, :], row(n + 1), ALU.mult)\
                   .then_inc(mul_done, 1)
                dve.wait_ge(mul_done, t + 1)
                later = lambda x, a, k: x[:, :, cols(a, k)].rearrange("p m (t b) -> p m t b", b=NB)
                if n:
                    y = later(S[:, :, 0, :], t + 1, n)
                    keys_done = mark(dve.tensor_tensor(y, y, tk[:, :, 0:n, :], ALU.subtract))
                if n > 1:
                    y = later(S[:, :, 1, :], t + 2, n - 1)
                    mark(dve.tensor_tensor(y, y, tq[:, :, 1:n, :], ALU.subtract))
                y = later(O, t, n + 1)
                last = mark(dve.tensor_tensor(y, y, to[:, :, 0:n + 1, :], ALU.add))
                if i == CH - 1 and j + 1 < NCH:
                    nb, h, c = j + 1, LV[j + 1], (j + 1) * CH
                    g = P // h
                    dve.wait_ge(dve_own, last)
                    for b in range(nblk(nb)):
                        gi, m = divmod(b, 2)
                        k = total(nb) + b
                        ps = psR[k % 2][:, 0:3 * P].rearrange("p (k t b) -> p k t b", k=3, b=g)
                        y = S[:, m, :, cols(c, h)].rearrange("p k (t b) -> p k t b", b=NB)[:, :, :, gi * g:(gi + 1) * g]
                        z = O[:, m, cols(c, h)].rearrange("p (t b) -> p t b", b=NB)[:, :, gi * g:(gi + 1) * g]
                        dve.wait_ge(r_psum, k + 1)
                        dve.tensor_tensor(y, y, ps[:, 0:2], ALU.subtract)
                        dve.tensor_tensor(z, z, ps[:, 2], ALU.add).then_inc(r_done, 1)
                    dve.wait_ge(r_done, total(nb + 1))
                    square_error(t + 1)
                if j + 2 < NCH:
                    for b in slices(j + 2)[i]:
                        keep_block(j + 2, b)


def memory_output(nc, ctx, pr, dram, x1):
    sb = lambda n, s: ctx.enter_context(nc.sbuf_tensor(n, s, F32))
    sem = lambda n: ctx.enter_context(nc.semaphore(n))
    S, NU, O, pw, ident, ones = (pr[n] for n in ("S", "NU", "O", "pw", "ident", "ones"))
    x_tok = sb("x_tok3", [P, TT, DM])
    Wo = sb("Wo", [P, DM])
    nw = sb("nw", [P, 1])
    diag = sb("diag", [P, 3, BW])
    mixed = [sb(f"mixed{k}", [P, 2, BW]) for k in range(3)]
    on = sb("on", [P, NT])
    keep = sb("keep", [P, NT])
    gain = sb("gain", [P, NT])
    neural = sb("neural", [P, NT])
    stats = sb("stats", [P, TT, 6])
    mv = sb("mv", [P, TT, 2])
    inv = sb("inv", [P, TT])
    eps = sb("eps", [P, 2])
    bank = [ctx.enter_context(nc.psum_tensor(f"psB{i}", [P, BW], F32)) for i in range(8)]
    psQ = bank[6]
    psO = [bank[0], bank[1], bank[2], bank[3]]
    loaded = sem("loaded3")
    diag_ready = sem("diagonals_ready")
    spread = sem("weights_spread")
    weighted = sem("paths_weighted")
    summed = sem("paths_summed")
    own_d = sem("dve_own3")
    sq3 = sem("squares3")
    ms = sem("mean_squares")
    root = sem("roots3")
    wo_ok = sem("wo_scaled")
    eps_ok = sem("eps_ok")
    out_ps = sem("outputs_in_psum")
    resid = sem("residual_added")
    std = sem("deviations")
    QT = TT // NBK

    with nc.Block() as block:
        @block.sync
        def _(sp):
            sp.dma_start(x_tok[:, :, :], dram["x"].rearrange("b s d -> (b s) d")
                         .rearrange("(i p) d -> p i d", p=P)).then_inc(loaded, 16)
            sp.dma_start(Wo[:, :], dram["Wo"]).then_inc(loaded, 16)
            sp.dma_start(nw[:, :], dram["norm_w"].rearrange("(p o) -> p o", o=1)).then_inc(loaded, 16)

        @block.gpsimd
        def _(pool):
            pool.memset(eps[:, 0:1], RMS_EPS).then_inc(eps_ok, 1)
            pool.memset(eps[:, 1:2], LN_EPS).then_inc(eps_ok, 1)
            for n in range(NBK):
                for k in range(3):
                    if n:
                        pool.wait_ge(spread, 3 * n - 2 + k)
                    for i in range(QT):
                        d = pool.tensor_scalar(diag[:, k, i * P:(i + 1) * P], ident[:, :], pw[:, n * QT + i, k:k + 1],
                                               2.0 if k < 2 else 1.0, ALU.mult, ALU.mult)
                    d.then_inc(diag_ready, 1)

        @block.tensor
        def _(pe):
            for n in range(NBK):
                for k in range(3):
                    pe.wait_ge(diag_ready, 3 * n + k + 1)
                    if n >= 2:
                        pe.wait_ge(weighted, 3 * (n - 2) + k + 1)
                    pe.matmul(bank[3 * (n % 2) + k][:, :], ones[:, :], diag[:, k, :], start=True, stop=True).then_inc(spread, 1)
            pe.wait_ge(weighted, 3 * NBK)
            pe.wait_ge(wo_ok, 1)
            pe.wait_ge(sq3, NBK)
            for i in range(TT):
                mm = pe.matmul(psQ[:, i:i + 1], keep[:, i * P:(i + 1) * P], ones[:, 0:1], start=True, stop=True)
            mm.then_inc(ms, 1)
            for i in range(TT):
                if i >= 8 and i % 2 == 0:
                    pe.wait_ge(resid, i - 6)
                mm = pe.matmul(psO[i // 2 % 4][:, i % 2 * DM:(i % 2 + 1) * DM], on[:, i * P:(i + 1) * P], Wo[:, :],
                               start=True, stop=True)
                if i % 2:
                    mm.then_inc(out_ps, 1)

        @block.scalar
        def _(act):
            act.wait_ge(summed, NBK)
            for n in range(NBK):
                c = slice(n * BW, (n + 1) * BW)
                act.activation(keep[:, c], on[:, c], ACT.Square).then_inc(sq3, 1)
            act.wait_ge(eps_ok, 2)
            act.wait_ge(ms, 1)
            act.activation(inv[:, :], psQ[:, 0:TT], ACT.Sqrt, bias=eps[:, 0:1], scale=1.0 / P).then_inc(root, 1)
            act.wait_ge(std, 1)
            act.activation(mv[:, :, 1:2], mv[:, :, 1:2], ACT.Sqrt, bias=eps[:, 1:2]).then_inc(std, 1)

        @block.vector
        def _(dve):
            own = 0

            def link(ins):
                nonlocal own
                own += 1
                ins.then_inc(own_d, 1)
                dve.wait_ge(own_d, own)

            turned = lambda x: x.rearrange("p (s b) -> p b s", b=NB)
            own_order = lambda x: x[:, :].rearrange("p (b s) -> p b s", s=NS)
            link(dve.tensor_scalar(own_order(gain), turned(S[:, 1, 1, :]), 0.7, 0.1, ALU.is_gt, ALU.mult))
            link(dve.tensor_scalar(keep[:, :], gain[:, :], -1.0, 1.0, ALU.mult, ALU.add))
            dve.memset(own_order(keep)[:, :, 0:1], 0.0)
            link(dve.tensor_tensor(own_order(gain), own_order(gain), turned(NU[:, :]), ALU.mult))
            link(dve.tensor_tensor_scan(neural[:, :], keep[:, :], gain[:, :], 0.0, ALU.mult, ALU.add))
            dve.wait_ge(loaded, 48)
            dve.tensor_scalar(Wo[:, :], Wo[:, :], nw[:, :], None, ALU.mult).then_inc(wo_ok, 1)
            steps = lambda x: x.rearrange("p (s b) -> p s b", b=NB)
            turn = lambda x, n: x[:, :].rearrange("p (b s) -> p s b", s=NS)[:, n * BW // NB:(n + 1) * BW // NB, :]
            def total(n):
                a, b, c = (m[:, n % 2, :] for m in mixed)
                dve.wait_ge(weighted, 3 * n + 3)
                link(dve.tensor_tensor(a, a, b, ALU.add))
                dve.tensor_tensor(turn(on, n), steps(a), steps(c), ALU.add).then_inc(summed, 1)
            for n in range(NBK):
                c = slice(n * BW, (n + 1) * BW)
                for k in range(3):
                    src = turn(neural, n) if k == 2 else steps(O[:, k, c])
                    dve.wait_ge(spread, 3 * n + k + 1)
                    dve.tensor_tensor(steps(mixed[k][:, n % 2, :]), src, steps(bank[3 * (n % 2) + k][:, :]), ALU.mult)\
                       .then_inc(weighted, 1)
                if n:
                    total(n - 1)
                if n:
                    dve.wait_ge(summed, n)
            total(NBK - 1)
            dve.wait_ge(root, 1)
            link(dve.reciprocal(inv[:, :], inv[:, :]))
            for i in range(TT + 2):
                if i < TT:
                    if i % 2 == 0:
                        dve.wait_ge(out_ps, i // 2 + 1)
                    dve.scalar_tensor_tensor(x1[:, i, :], psO[i // 2 % 4][:, i % 2 * DM:(i % 2 + 1) * DM], inv[:, i:i + 1],
                                             x_tok[:, i, :], ALU.mult, ALU.add).then_inc(resid, 1)
                if 1 <= i <= TT:
                    dve.wait_ge(resid, i)
                    dve.bn_stats(stats[:, i - 1, :], x1[:, i - 1, :]).then_inc(own_d, 1)
                if i >= 2:
                    dve.wait_ge(own_d, own + i - 1)
                    last = dve.bn_aggr(mv[:, i - 2, :], stats[:, i - 2, :])
            own += TT
            last.then_inc(std, 1)
            dve.wait_ge(std, 2)
            link(dve.reciprocal(mv[:, :, 1:2], mv[:, :, 1:2]))
            for i in range(TT):
                last = dve.tensor_scalar(x1[:, i, :], x1[:, i, :], mv[:, i, 0:1], mv[:, i, 1:2], ALU.subtract, ALU.mult)
            link(last)


def memory(nc, dram, x1, ident, ones):
    with ExitStack() as ctx:
        sb = lambda n, s: ctx.enter_context(nc.sbuf_tensor(n, s, F32))
        pr = {"ident": ident, "ones": ones,
              "KQ": sb("KQ", [P, 2, NT]),
              "W": sb("W", [P, 2, NT]),
              "S": sb("S", [P, 2, 2, NT]),
              "F4": sb("F4", [P, 2, NT]),
              "NU": sb("NU", [P, NT]), "O": sb("O", [P, 2, NT]), "pw": sb("pw", [P, TT, 3]),
              "A": x1[:, :, :].rearrange("p i d -> p (i d)").rearrange("p (m c) -> p m c", m=2)}
        with ExitStack() as c:
            memory_inputs(nc, c, pr, dram)
        with ExitStack() as c:
            recurrence(nc, c, pr)
        with ExitStack() as c:
            memory_output(nc, c, pr, dram, x1)


HEADS, HD = 8, 64
NKEY = DM


def cross_attention(nc, ctx, x1, dram, ident, preload):
    sb = lambda n, s: ctx.enter_context(nc.sbuf_tensor(n, s, F32))
    sem = lambda n: ctx.enter_context(nc.semaphore(n))
    r = lambda ap: ap.bitcast(F32R)
    TURN, COPY, ADD = 3, 3, 5
    Y_AT = (2, 4, 5, 7)
    RS_ = 2
    RE = 8
    WQ = sb("WQ", [P, 4, HD])
    WKV = sb("WKV", [P, 8, HD])
    WO = sb("WO", [HD, HEADS * HD])
    WOT = sb("WOT", [P, 4, HD])
    bout = sb("bout", [HD, 1])
    hi_m = sb("hi_m", [P, HEADS * HD])
    MS = sb("MS", [P, HEADS, 2, HD])
    NS_ = sb("NS_", [P, HEADS * HD])
    XX = sb("XX", [P, 2, NKEY])
    XH = sb("XH", [P, 2, NKEY])
    XL = sb("XL", [P, 2, NKEY])
    CC = sb("CC", [P, 2, NKEY])
    CHI = sb("CHI", [P, 2, NKEY])
    CLO = sb("CLO", [P, 2, NKEY])
    Y = sb("Y", [P, 2, HEADS, NKEY])
    Z = sb("Z", [P, 2, 2, HEADS * HD])
    E = sb("E", [P, RE, 2, NKEY])
    AT = sb("AT", [P, 4, 2, NKEY])
    NM = sb("NM", [P, RE, 2])
    RS = sb("RS", [P, RE, 2])
    RI = sb("RI", [P, RE, 2])
    ps = lambda n, w=BW: ctx.enter_context(nc.psum_tensor(n, [P, w], F32))
    psY = [ps("psY0"), ps("psY1"), ps("psY2")]
    psS = [ps(f"psS{i}x") for i in range(RS_)]
    psA = [ps("psA0"), ps("psA1")]
    psU = ps("psU", NKEY)
    psM, psN = (psY[0], psS[1]), (psY[1], psY[2])

    w_in = sem("att_weights")
    wprep_pe = sem("att_products_in_psum")
    wprep = sem("att_weights_ready")
    wot_ready = sem("wout_turned")
    x_in = [sem("x_rows0"), sem("x_rows1")]
    c_in = [sem("ctx_rows0"), sem("ctx_rows1")]
    hi_ready = sem("hi_ready")
    lo_ready = sem("lo_ready")
    y_psum = sem("y_in_psum")
    y_hi = sem("y_hi")
    y_ready = sem("y_ready")
    z_psum = sem("z_in_psum")
    z_ready = sem("z_ready")
    sim_ready = sem("scores_in_psum")
    max_ready = sem("maxima_ready")
    exp_done = sem("exponentials_ready")
    ri_ready = sem("reciprocals_ready")
    norm_done = sem("attention_ready")
    t_psum = sem("attention_turned")
    at_act = sem("turned_by_act")
    at_dve = sem("turned_by_dve")
    av_done = sem("pairs_of_heads_added")
    out_read = sem("outputs_read")
    out_part = sem("outputs_half_read")

    DV = (1, 4, 7)
    by_dve = lambda hh: sum(1 for v in DV if v <= hh)
    ITER = NB // 2
    LAST = 16 * ITER

    def at_wait(eng, it, k):
        q, hh = divmod(k, 8)
        if hh in DV:
            eng.wait_ge(at_dve, it * 2 * len(DV) + (q * len(DV) + by_dve(hh)))
        else:
            eng.wait_ge(at_act, it * 2 * (8 - len(DV)) + (q * (8 - len(DV)) + hh + 1 - by_dve(hh)))

    def rows(x, b2):
        return x[64 * b2:64 * b2 + 64]

    with nc.Block() as block:
        def run(eng, slot, tail):
            for k in range(16):
                slot(0, k, True, False)
            with eng.Fori(1, ITER - 1) as it:
                for k in range(16):
                    slot(it, k, False, False)
            for k in range(16):
                slot(ITER - 1, k, False, True)
            for k in range(16, 16 + tail):
                slot(ITER - 1, k, False, True)

        @block.sync
        def _(sp):
            sp.dma_start(WQ[:, :, :], dram["Wq"].rearrange("(c p) k -> p c k", p=P)).then_inc(w_in, 16)
            sp.dma_start(WKV[:, :, :], dram["Wkv"].rearrange("(c p) k -> p c k", p=P)).then_inc(w_in, 16)
            sp.dma_start(WO[:, :], dram["Wout"]).then_inc(w_in, 16)
            sp.dma_start(bout[:, :], dram["bout"].rearrange("(p o) -> p o", o=1)).then_inc(w_in, 16)

            def load(it, q, wait):
                if wait:
                    sp.wait_ge(lo_ready, it * 2 + (q - 1))
                for half in range(2):
                    sp.dma_start(rows(XX, half)[:, q, :], rows(x1, q)[:, bass.ds(it, 1), :]
                                 .rearrange("p i d -> p (i d)")).then_inc(x_in[q], 16)
                    sp.dma_start(rows(CC, half)[:, q, :], dram["ctx"][bass.ds(it * 2 + q, 1), :, :]
                                 .rearrange("b s d -> (b s) d")).then_inc(c_in[q], 16)
            load(0, 0, False)
            load(0, 1, False)
            preload(sp)
            with sp.Fori(1, ITER) as it:
                load(it, 0, True)
                load(it, 1, True)

        @block.tensor
        def _(pe):
            pe.wait_ge(w_in, 64)
            for i in range(4):
                mm = pe.transpose(psS[0][:, i * HD:(i + 1) * HD], WO[:, i * P:(i + 1) * P], ident[0:HD, 0:HD])
            mm.then_inc(wprep_pe, 1)
            for half in range(2):
                for h in range(HEADS):
                    a = rows(WQ, h % 2)[:, h // 2, :]
                    mm = pe.matmul(rows(psM[h % 2], half)[:, h // 2 * HD:(h // 2 + 1) * HD], a, rows(WKV, h % 2)[:, h // 2, :],
                                   start=True, stop=True)
            mm.then_inc(wprep_pe, 1)
            pe.wait_ge(wot_ready, 1)
            for half in range(2):
                for h in range(HEADS):
                    mm = pe.matmul(rows(psN[h % 2], half)[:, h // 2 * HD:(h // 2 + 1) * HD], rows(WKV, h % 2)[:, 4 + h // 2, :],
                                   rows(WOT, h % 2)[:, h // 2, :], start=True, stop=True)
            mm.then_inc(wprep_pe, 1)
            pe.wait_ge(wprep, 14)

            def y_piece(it, q, p, wait):
                if p == 0:
                    pe.wait_ge(hi_ready, it * 4 + (2 * q + 2))
                    pe.wait_ge(lo_ready, it * 2 + (q + 1))
                if p == 0 and wait:
                    pe.wait_ge(y_ready, it * 8 + 4 * q)
                elif p in (1, 2) and wait:
                    pe.wait_ge(z_ready, it * 4 + (2 * q - 2 + p))
                elif p == 3:
                    pe.wait_ge(y_ready, it * 8 + (4 * q + 1))
                for d in range(2):
                    for n, x in enumerate((XH, XL)):
                        mm = pe.matmul(psY[(2 + p) % 3][:, d * NKEY:(d + 1) * NKEY],
                                       r(MS[:, 2 * p + d, :, :].rearrange("p a c -> p (a c)")), r(x[:, q, :]),
                                       start=n == 0, stop=n == 1)
                mm.then_inc(y_psum, 1)

            def slot(it, k, first, last):
                q, hh = divmod(k, 8)
                if k < 16:
                    pe.wait_ge(y_ready, it * 8 + (4 * q + hh // 2 + 1))
                    if not first or k >= RS_:
                        pe.wait_ge(exp_done, it * 16 + (k - RS_ + 1))
                    for ib in range(2):
                        for n, c in enumerate((CHI, CLO)):
                            mm = pe.matmul(psS[k % RS_][:, ib * NKEY:(ib + 1) * NKEY],
                                           r(Y[:, q, hh, ib * P:(ib + 1) * P]), r(c[:, q, :]), start=n == 0, stop=n == 1)
                    mm.then_inc(sim_ready, 1)
                    if hh in (0, 1):
                        pe.wait_ge(y_ready, it * 8 + (4 * q + 2 + hh))
                        for n, c in enumerate((CHI, CLO)):
                            mm = pe.matmul(psY[hh][:, :], r(c[:, q, hh * P:(hh + 1) * P]), r(NS_[:, :]),
                                           start=n == 0, stop=n == 1)
                        mm.then_inc(z_psum, 1)
                    if hh in Y_AT and not (last and q == 1):
                        y_piece(it + q, 1 - q, Y_AT.index(hh), True)
                t = k - TURN
                if (not first or t >= 0) and t < 16:
                    pe.wait_ge(norm_done, it * 16 + (t + 1))
                    if not first or t >= 2:
                        at_wait(pe, it, t - 2)
                    for jb in range(2):
                        for ib in range(2):
                            mm = pe.transpose(psA[t % 2][:, jb * NKEY + ib * P:jb * NKEY + (ib + 1) * P],
                                              E[:, t % RE, ib, jb * P:(jb + 1) * P], ident[:, :])
                    mm.then_inc(t_psum, 1)
                a = k - ADD
                if a % 2 == 0 and (not first or a >= 0) and a < 16:
                    at_wait(pe, it, a)
                    at_wait(pe, it, a + 1)
                    qa, ha = divmod(a, 8)
                    pe.wait_ge(z_ready, it * 4 + (2 * qa + 2))
                    if ha == 0 and (not first or qa >= 1):
                        pe.wait_ge(out_read, it * 2 + qa)
                    for jb in range(2):
                        for d in range(2):
                            h = ha + d
                            mm = pe.matmul(rows(psU, d)[:, :], Z[:, qa % 2, jb, h * HD:(h + 1) * HD],
                                           AT[:, (a + d) % 4, jb, :], start=ha == 0 and jb == 0, stop=ha == 6 and jb == 1)
                    mm.then_inc(av_done, 1)

            for p in range(4):
                y_piece(0, 0, p, False)
            run(pe, slot, ADD)

        def turn_out(eng, it, t, engine_sem, copy):
            eng.wait_ge(t_psum, it * 16 + (t + 1))
            copy(AT[:, t % 4, :, :].rearrange("p j i -> p (j i)"), psA[t % 2][:, :]).then_inc(engine_sem, 1)

        @block.scalar
        def _(act):
            act.wait_ge(wprep_pe, 1)
            act.activation(WOT[:, :, :].rearrange("p i o -> p (i o)"), psS[0][:, 0:4 * HD], ACT.Copy).then_inc(wot_ready, 1)

            def split_hi(it, q, wait):
                act.wait_ge(x_in[q], it * 32 + 32)
                act.wait_ge(c_in[q], it * 32 + 32)
                if wait:
                    act.wait_ge(y_psum, it * 8 + (4 * q - 4))
                    act.wait_ge(sim_ready, it * 16 + (8 * q - 8))
                act.activation(r(XH[:, q, :]), XX[:, q, :], ACT.Copy).then_inc(hi_ready, 1)
                act.activation(r(CHI[:, q, :]), CC[:, q, :], ACT.Copy).then_inc(hi_ready, 1)

            def y_high(it, q, p, wait):
                act.wait_ge(y_psum, it * 8 + (4 * q + p + 1))
                if p == 0 and wait:
                    act.wait_ge(sim_ready, it * 16 + (8 * q - 8))
                act.activation(r(Y[:, q, 2 * p:2 * p + 2, :].rearrange("p h n -> p (h n)")), psY[(2 + p) % 3][:, :],
                               ACT.Copy).then_inc(y_hi, 1)

            def slot(it, k, first, last):
                q, hh = divmod(k, 8)
                if k < 16:
                    if hh == 0 and not (last and q == 1):
                        split_hi(it + q, 1 - q, not (first and q == 0))
                    if hh in (1, 2):
                        jb = hh - 1
                        act.wait_ge(z_psum, it * 4 + (2 * q + jb + 1))
                        if jb == 0 and (not first):
                            act.wait_ge(av_done, it * 8 + (4 * q - 4))
                        act.activation(Z[:, q, jb, :], psY[jb][:, :], ACT.Copy).then_inc(z_ready, 1)
                    if hh - 1 in Y_AT and not (last and q == 1):
                        y_high(it + q, 1 - q, Y_AT.index(hh - 1), not (first and q == 0))
                    if hh == 0 and not (first and q == 0):
                        y_high(it, q, 3, True)
                    act.wait_ge(max_ready, it * 16 + (k + 1))
                    if not first or k >= RE:
                        act.wait_ge(t_psum, it * 16 + (k - RE + 1))
                    for ib in range(2):
                        ex = act.activation(E[:, k % RE, ib, :], psS[k % RS_][:, ib * NKEY:(ib + 1) * NKEY], ACT.Exp,
                                            bias=NM[:, k % RE, ib:ib + 1], accum_out=RS[:, k % RE, ib:ib + 1])
                    ex.then_inc(exp_done, 1)
                t = k - COPY
                if (not first or t >= 0) and t < 16 and t % 8 not in DV:
                    if not first or t >= 4:
                        act.wait_ge(av_done, it * 8 + (t - 4) // 2 + 1)
                    turn_out(act, it, t, at_act, lambda o, i: act.activation(o, i, ACT.Copy))

            split_hi(0, 0, False)
            for p in range(4):
                y_high(0, 0, p, False)
            run(act, slot, COPY)

        @block.gpsimd
        def _(pool):
            def slot(it, k, first, last):
                pool.wait_ge(ri_ready, it * 16 + (k + 1))
                pool.tensor_tensor(E[:, k % RE, :, :], E[:, k % RE, :, :],
                                   RI[:, k % RE, :].unsqueeze(2).broadcast_to((P, 2, NKEY)), ALU.mult).then_inc(norm_done, 1)
            run(pool, slot, 0)

        @block.vector
        def _(dve):
            dve.wait_ge(w_in, 64)
            dve.wait_ge(wprep_pe, 2)
            heads = lambda x, e: x.rearrange("p (h e c) -> p h e c", e=2, c=HD)[:, :, e, :]
            half = lambda x: x[:, 0:4 * HD].rearrange("p (h c) -> p h c", c=HD)
            for e in range(2):
                dve.tensor_copy(r(heads(hi_m[:, :], e)), half(psM[e][:, :])).then_inc(wprep, 1)
            dve.wait_ge(wprep, 2)
            for e in range(2):
                for d in range(2):
                    dve.tensor_copy(r(MS[0:HD, e:HEADS:2, d, :]), heads(hi_m[0:HD, :], e)).then_inc(wprep, 1)
                    dve.tensor_tensor(r(MS[HD:P, e:HEADS:2, d, :]), half(psM[e][HD:P, :]), heads(hi_m[HD:P, :], e),
                                      ALU.subtract).then_inc(wprep, 1)
            dve.wait_ge(wprep_pe, 3)
            for e in range(2):
                dve.tensor_copy(r(heads(NS_[:, :], e)), half(psN[e][:, :])).then_inc(wprep, 1)
            dve.wait_ge(wprep, 12)
            for e in range(2):
                lo = heads(NS_[HD:P, :], e)
                dve.tensor_tensor(r(lo), half(psN[e][HD:P, :]), lo, ALU.subtract).then_inc(wprep, 1)

            def split_lo(it, q, wait):
                dve.wait_ge(hi_ready, it * 4 + (2 * q + 2))
                dve.tensor_tensor(r(XL[:, q, :]), XX[:, q, :], XH[:, q, :], ALU.subtract)
                dve.tensor_tensor(r(CLO[:, q, :]), CC[:, q, :], CHI[:, q, :], ALU.subtract).then_inc(lo_ready, 1)

            def y_low(it, q, p):
                dve.wait_ge(y_hi, it * 8 + (4 * q + p + 1))
                y = Y[HD:P, q, 2 * p:2 * p + 2, :].rearrange("p h n -> p (h n)")
                dve.tensor_tensor(r(y), psY[(2 + p) % 3][HD:P, :], y, ALU.subtract).then_inc(y_ready, 1)

            def slot(it, k, first, last):
                q, hh = divmod(k, 8)
                if k < 16:
                    dve.wait_ge(sim_ready, it * 16 + (k + 1))
                    dve.tensor_reduce(NM[:, k % RE, :], psS[k % RS_][:, :].rearrange("p (i j) -> p i j", i=2), AX.X,
                                      ALU.max, negate=True).then_inc(max_ready, 1)
                    if hh - 1 in Y_AT and not (last and q == 1):
                        y_low(it + q, 1 - q, Y_AT.index(hh - 1))
                    if hh == 0 and not (first and q == 0):
                        y_low(it, q, 3)
                t = k - 1
                if (not first or t >= 0) and t < 16:
                    dve.wait_ge(exp_done, it * 16 + (t + 1))
                    dve.reciprocal(RI[:, t % RE, :], RS[:, t % RE, :]).then_inc(ri_ready, 1)
                a = k - (ADD + 7)
                if a in (0, 8) or (a in (-8, -16) and not first):
                    qb = a // 8
                    dve.wait_ge(av_done, it * 8 + (4 * qb + 4))
                    i = it if qb >= 0 else it - 1
                    xr = rows(x1, qb % 2)[:, bass.ds(i, 1), :].rearrange("p i d -> p (i d)")
                    dve.scalar_tensor_tensor(xr, psU[0:HD, :], bout[:, :], xr, ALU.add, ALU.add)\
                       .then_inc(out_part, 1)
                    dve.wait_ge(out_part, it * 2 + (qb + 1))
                    dve.tensor_tensor(xr, xr, psU[HD:P, :], ALU.add).then_inc(out_read, 1)
                if k < 16:
                    if hh == 1 and not (last and q == 1):
                        split_lo(it + q, 1 - q, True)
                t = k - COPY
                if (not first or t >= 0) and t < 16 and t % 8 in DV:
                    if not first or t >= 4:
                        dve.wait_ge(av_done, it * 8 + (t - 4) // 2 + 1)
                    turn_out(dve, it, t, at_dve, dve.tensor_copy)
            split_lo(0, 0, False)
            for p in range(4):
                y_low(0, 0, p)
            run(dve, slot, ADD + 1)


def layernorm(nc, ctx, x, name):
    sb = lambda n, s: ctx.enter_context(nc.sbuf_tensor(name + n, s, F32))
    sem = lambda n: ctx.enter_context(nc.semaphore(name + n))
    stats = sb("stats", [P, TT, 6])
    mv = sb("mv", [P, TT, 2])
    eps = sb("eps", [P, 1])
    own_d, std, ready = sem("own"), sem("std"), sem("eps_ready")
    with nc.Block() as block:
        @block.gpsimd
        def _(pool):
            pool.memset(eps[:, :], LN_EPS).then_inc(ready, 1)

        @block.scalar
        def _(act):
            act.wait_ge(ready, 1)
            act.wait_ge(std, 1)
            act.activation(mv[:, :, 1:2], mv[:, :, 1:2], ACT.Sqrt, bias=eps[:, :]).then_inc(std, 1)

        @block.vector
        def _(dve):
            own = 0
            for i in range(TT):
                dve.bn_stats(stats[:, i, :], x[:, i, :]).then_inc(own_d, 1)
            for i in range(TT):
                dve.wait_ge(own_d, i + 1)
                ag = dve.bn_aggr(mv[:, i, :], stats[:, i, :])
            ag.then_inc(std, 1)
            dve.wait_ge(std, 2)
            dve.reciprocal(mv[:, :, 1:2], mv[:, :, 1:2]).then_inc(own_d, 1)
            dve.wait_ge(own_d, TT + 1)
            for i in range(TT):
                last = dve.tensor_scalar(x[:, i, :], x[:, i, :], mv[:, i, 0:1], mv[:, i, 1:2], ALU.subtract, ALU.mult)
            last.then_inc(own_d, 1)


NE, TOPK, CAP, HE, HSH = 64, 6, 128, 32, 64
EC = P // HE
NC = NE // EC
TB = BW
NTB = NT // TB


def expert_weights(nc, ctx):
    sb = lambda n, s: ctx.enter_context(nc.sbuf_tensor(n, s, F32))
    return {"up": sb("up_raw", [P, KD, NE, 2 * HE]), "down": sb("down", [P, NC, DM]),
            "in": ctx.enter_context(nc.semaphore("expert_weights_in"))}


def load_expert_weights(sp, ew, dram):
    for k in range(KD):
        sp.dma_start(ew["up"][:, k, :, :], dram["w_up"][:, k * P:(k + 1) * P, :].rearrange("e p h -> p e h")).then_inc(ew["in"], 16)
    sp.dma_start(ew["down"][:, :, :], dram["w_down"].rearrange("e h c -> (e h) c").rearrange("(n p) c -> p n c", p=P)).then_inc(ew["in"], 16)


EW_IN = 16 * (KD + 1)


def experts(nc, ctx, x2, ew, dram, ident):
    sb = lambda n, s: ctx.enter_context(nc.sbuf_tensor(n, s, F32))
    sem = lambda n: ctx.enter_context(nc.semaphore(n))
    r = lambda ap: ap.bitcast(F32R)
    UH = sb("UH", [P, KD, 2, NE * HE])
    UL = sb("UL", [P, KD, 2, NE * HE])
    XH = sb("XTH", [P, KD, NT])
    XL = sb("XTL", [P, KD, NT])
    WT = sb("WTT", [P, NT])
    sh_up = sb("sh_up", [P, KD, 2 * HSH])
    sh_h = sb("sh_h", [P, KD, 2 * HSH])
    sh_l = sb("sh_l", [P, KD, 2 * HSH])
    sh_dn = sb("sh_dn", [HSH, DM])
    gate = sb("gate", [P, KD, NE])
    small = ctx.enter_context(ExitStack())
    sbs = lambda n, s: small.enter_context(nc.sbuf_tensor(n, s, F32))
    sc = sbs("sc", [P, TT, NE])
    top = sbs("top", [P, TT, 8])
    gt = sbs("gt", [P, TT, NE])
    eq = sbs("eq", [P, TT, NE])
    rank = sbs("rank", [P, TT, NE])
    seg = sbs("seg", [P, TT, NE])
    cnt = sbs("cnt", [P, TT, 2])
    rcp = sbs("rcp", [P, TT, 1])
    car = sbs("car", [P, TT, NE])
    w2 = sbs("w2", [P, TT, 2, NE])
    tri = sbs("tri", [P, P])
    on1 = sbs("on1", [P, P])

    n3 = lambda n: ctx.enter_context(nc.psum_tensor(n, [P, BW], F32))
    bk = [n3(f"e{i}") for i in range(8)]

    loaded = sem("gate_in")
    consts = sem("route_consts")
    xt_ps = sem("x2_turned")
    xt_hi = sem("x2_hi")
    xt_lo = sem("x2_lo")
    logit = sem("logits_in_psum")
    score = sem("scores_ready")
    own_d = sem("dve_own5")
    sel_ok = sem("selection_ready")
    counts = sem("counts_in_psum")
    wr = sem("routing_weights_ready")
    wt_ps = sem("routing_weights_turned")
    wt_ok = sem("routing_rows_ready")
    up_hi = sem("up_hi")
    sh_hi = sem("shared_hi")
    NT8 = KD * NBK

    with nc.Block() as block:
        @block.sync
        def _(sp):
            sp.dma_start(gate[:, :, :], dram["w_gate"].rearrange("(k p) e -> p k e", p=P)).then_inc(loaded, 16)
            sp.dma_start(sh_up[:, :, :], dram["w_shared_up"].rearrange("(k p) e -> p k e", p=P)).then_inc(loaded, 16)
            sp.dma_start(sh_dn[:, :], dram["w_shared_down"]).then_inc(loaded, 16)

        @block.gpsimd
        def _(pool):
            pool.memset(tri[:, :], 1.0).then_inc(consts, 1)
            pool.memset(seg[:, :, :], 1.0).then_inc(consts, 1)
            pool.memset(on1[:, :], 1.0).then_inc(consts, 1)
            pool.wait_ge(consts, 3)
            pool.affine_select(out=r(tri[:, :]), in_=tri[:, :], compare_op=ALU.is_gt, fill=0.0, base=0,
                               pattern=[[1, P]], channel_multiplier=-1).then_inc(consts, 1)
            pool.memset(seg[:, :, 0:1], 0.0).then_inc(consts, 1)
            pool.wait_ge(consts, 5)

        @block.tensor
        def _(pe):
            pe.wait_ge(consts, 5)
            for j in range(NT8):
                k, n = divmod(j, NBK)
                if j >= 4:
                    pe.wait_ge(xt_lo, j - 3)
                for i in range(4):
                    mm = pe.transpose(bk[j % 4][:, i * P:(i + 1) * P], x2[:, 4 * n + i, k * P:(k + 1) * P], ident[:, :])
                mm.then_inc(xt_ps, 1)
            pe.wait_ge(xt_lo, NT8)
            pe.wait_ge(loaded, 48)
            for i in range(TT):
                for n, (k, x) in enumerate([(k, x) for k in range(KD) for x in (XH, XL)]):
                    mm = pe.matmul(bk[4 + i // 8][:, i % 8 * NE:(i % 8 + 1) * NE], x[:, k, i * P:(i + 1) * P],
                                   gate[:, k, :], start=n == 0, stop=n == 2 * KD - 1)
            mm.then_inc(logit, 1)
            pe.wait_ge(sel_ok, 1)
            flat = gt[:, :, :].rearrange("p i e -> p (i e)")
            for m, a in enumerate((tri, on1)):
                for n in range(2):
                    mm = pe.matmul(bk[2 * m + n][:, :], r(a[:, :]), r(flat[:, n * BW:(n + 1) * BW]), start=True, stop=True)
            mm.then_inc(counts, 1)
            pe.wait_ge(wr, 1)
            for i in range(TT):
                mm = pe.transpose(bk[4 + i // 4][:, i % 4 * P:(i % 4 + 1) * P],
                                  w2[:, i, :, :].rearrange("p a e -> p (a e)"), ident[:, :])
                if i % 4 == 3:
                    mm.then_inc(wt_ps, 1)

        @block.scalar
        def _(act):
            for j in range(NT8):
                k, n = divmod(j, NBK)
                act.wait_ge(xt_ps, j + 1)
                act.activation(r(XH[:, k, n * BW:(n + 1) * BW]), bk[j % 4][:, :], ACT.Copy).then_inc(xt_hi, 1)
            act.wait_ge(logit, 1)
            for n in range(2):
                act.activation(sc[:, 8 * n:8 * n + 8, :].rearrange("p i e -> p (i e)"), bk[4 + n][:, :], ACT.Sigmoid)\
                   .then_inc(score, 1)
            act.wait_ge(loaded, 48)
            act.activation(r(sh_h[:, :, :]), sh_up[:, :, :], ACT.Copy).then_inc(sh_hi, 1)
            act.wait_ge(ew["in"], EW_IN)
            for k in range(KD):
                for v in range(2):
                    act.activation(r(UH[:, k, v, :].rearrange("p (e h) -> p e h", h=HE)),
                                   ew["up"][:, k, :, v * HE:(v + 1) * HE], ACT.Copy).then_inc(up_hi, 1)

        @block.vector
        def _(dve):
            own = 0

            def link(ins):
                nonlocal own
                own += 1
                ins.then_inc(own_d, 1)
                dve.wait_ge(own_d, own)

            for j in range(NT8):
                k, n = divmod(j, NBK)
                dve.wait_ge(xt_hi, j + 1)
                c = slice(n * BW, (n + 1) * BW)
                dve.tensor_tensor(r(XL[:, k, c]), bk[j % 4][:, :], XH[:, k, c], ALU.subtract).then_inc(xt_lo, 1)
            dve.wait_ge(score, 2)
            for i in range(TT):
                mx = dve.max(top[:, i, :], sc[:, i, :])
            link(mx)
            edge = top[:, :, TOPK - 1:TOPK].broadcast_to((P, TT, NE))
            dve.tensor_tensor(r(gt[:, :, :]), sc[:, :, :], edge, ALU.is_gt)
            dve.tensor_reduce(rcp[:, :, :], top[:, :, 0:TOPK], AX.X, ALU.add)
            link(dve.tensor_tensor(eq[:, :, :], sc[:, :, :], edge, ALU.is_equal))
            flat = lambda x: x[:, :, :].rearrange("p i e -> p (i e)")
            dve.wait_ge(consts, 5)
            dve.tensor_tensor_scan(flat(rank), flat(seg), flat(eq), 0.0, ALU.mult, ALU.add)
            link(dve.tensor_reduce(cnt[:, :, 0:1], gt[:, :, :], AX.X, ALU.add))
            link(dve.tensor_tensor(rank[:, :, :], rank[:, :, :], cnt[:, :, 0:1].broadcast_to((P, TT, NE)), ALU.add))
            link(dve.scalar_tensor_tensor(flat(eq), flat(rank), float(TOPK), flat(eq), ALU.is_le, ALU.mult))
            dve.tensor_tensor(r(gt[:, :, :]), gt[:, :, :], eq[:, :, :], ALU.add).then_inc(sel_ok, 1)
            dve.wait_ge(sel_ok, 1)
            link(dve.tensor_tensor(sc[:, :, :], sc[:, :, :], gt[:, :, :], ALU.mult))
            link(dve.reciprocal(rcp[:, :, :], rcp[:, :, :]))
            link(dve.tensor_tensor(sc[:, :, :], sc[:, :, :], rcp[:, :, :].broadcast_to((P, TT, NE)), ALU.mult))
            dve.wait_ge(counts, 1)
            link(dve.memset(car[:, 0, :], 0.0))
            for i in range(1, TT):
                link(dve.tensor_tensor(car[:, i, :], car[:, i - 1, :], bk[2 + (i - 1) // 8][:, (i - 1) % 8 * NE:((i - 1) % 8 + 1) * NE], ALU.add))
            for n in range(2):
                c = car[:, 8 * n:8 * n + 8, :].rearrange("p i e -> p (i e)")
                last = dve.tensor_tensor(c, c, bk[n][:, :], ALU.add)
            link(last)
            link(dve.scalar_tensor_tensor(flat(sc), flat(car), float(CAP), flat(sc), ALU.is_lt, ALU.mult))
            link(dve.tensor_copy(r(w2[:, :, 0, :]), sc[:, :, :]))
            dve.tensor_tensor(r(w2[:, :, 1, :]), sc[:, :, :], w2[:, :, 0, :], ALU.subtract).then_inc(wr, 1)
            for n in range(4):
                dve.wait_ge(wt_ps, n + 1)
                dve.tensor_copy(r(WT[:, n * BW:(n + 1) * BW]), bk[4 + n][:, :]).then_inc(wt_ok, 1)
            dve.wait_ge(sh_hi, 1)
            dve.tensor_tensor(r(sh_l[:, :, :]), sh_up[:, :, :], sh_h[:, :, :], ALU.subtract)
            for k in range(KD):
                for v in range(2):
                    dve.wait_ge(up_hi, 2 * k + v + 1)
                    last = dve.tensor_tensor(r(UL[:, k, v, :].rearrange("p (e h) -> p e h", h=HE)),
                                             ew["up"][:, k, :, v * HE:(v + 1) * HE],
                                             UH[:, k, v, :].rearrange("p (e h) -> p e h", h=HE), ALU.subtract)
            link(last)
    small.close()

    SP_ = sb("spread", [P, NC, P])
    SG = sb("SG", [P, 2, TB])
    HT = sb("HT", [P, 2, TB])
    sp_ok = sem("spread_ready")
    g_ps = sem("gates_in_psum")
    v_ps = sem("values_in_psum")
    w_ps = sem("weights_in_psum")
    sg_ok = sem("silu_ready")
    hv = sem("hidden_unweighted")
    h_ok = sem("hidden_ready")
    dn = sem("chunks_added")
    o_read = sem("block_outputs_read")
    N1 = NC + 1

    with nc.Block() as block:
        @block.gpsimd
        def _(pool):
            pool.memset(SP_[:, :, :], 0.0).then_inc(sp_ok, 1)
            for n, base in enumerate((0, -NE)):
                pool.wait_ge(sp_ok, n + 1)
                v = SP_[:, :, :].rearrange("p c (e h) -> p c e h", h=HE)
                pool.affine_select(out=r(v), in_=v, compare_op=ALU.not_equal, fill=1.0, base=base,
                                   pattern=[[-EC, NC], [-1, EC], [0, HE]], channel_multiplier=1).then_inc(sp_ok, 1)

        def before(c):
            return c - 2 if c >= 2 else (NC - 1 if c else NC) - N1

        def blocks(eng, body):
            body(0, True)
            with eng.Fori(1, NTB) as tb:
                body(tb, False)

        @block.tensor
        def _(pe):
            pe.wait_ge(sp_ok, 3)

            def up(tb, c, first):
                tok = bass.ds(tb * TB, TB)
                rhs = [x[:, k, tok] for k in range(KD) for x in (XH, XH, XL)]
                for v, s in ((0, g_ps), (1, v_ps)) if c < NC else ((0, g_ps),):
                    if not first or c >= 2:
                        pe.wait_ge((sg_ok, hv)[v or c == 0], tb * N1 + (before(c) + 1))
                    if c < NC:
                        lhs = [x[:, k, v, c * P:(c + 1) * P] for k in range(KD) for x in (UH, UL, UH)]
                    else:
                        lhs = [x[:, k, :] for k in range(KD) for x in (sh_h, sh_l, sh_h)]
                    for n, (a, b) in enumerate(zip(lhs, rhs)):
                        mm = pe.matmul(bk[2 * (c % 2) + v][:, :], r(a), r(b), start=n == 0, stop=n == 3 * KD - 1)
                    mm.then_inc(s, 1)
                if c < NC:
                    if not first or c >= 2:
                        pe.wait_ge(h_ok, tb * N1 + (before(c) + 1))
                    pe.matmul(bk[4 + c % 2][:, :], r(SP_[:, c, :]), r(WT[:, tok]), start=True, stop=True).then_inc(w_ps, 1)

            def down(tb, c, first):
                pe.wait_ge(h_ok, tb * N1 + (c + 1))
                if c == 0 and not first:
                    pe.wait_ge(o_read, tb)
                rows = P if c < NC else HSH
                for i in range(TB // P):
                    mm = pe.matmul(bk[6 + i // 2][:, i % 2 * DM:(i % 2 + 1) * DM], HT[0:rows, c % 2, i * P:(i + 1) * P],
                                   ew["down"][:, c, :] if c < NC else sh_dn[:, :], start=c == 0 and i % 2 == 0,
                                   stop=c == NC and i % 2 == 1)
                mm.then_inc(dn, 1)

            def body(tb, first):
                for c in range(N1):
                    up(tb, c, first)
                    if c:
                        down(tb, c - 1, first)
                down(tb, NC, first)
            blocks(pe, body)

        @block.scalar
        def _(act):
            def body(tb, first):
                for c in range(N1):
                    rows = P if c < NC else HSH
                    act.wait_ge(g_ps, tb * N1 + (c + 1))
                    if not first or c >= 2:
                        act.wait_ge(hv, tb * N1 + (before(c) + 1))
                    act.activation(SG[0:rows, c % 2, :], bk[2 * (c % 2)][P - rows:P, :], ACT.Silu).then_inc(sg_ok, 1)
            blocks(act, body)

        @block.vector
        def _(dve):
            def body(tb, first):
                for c in range(N1):
                    rows = P if c < NC else HSH
                    dve.wait_ge(sg_ok, tb * N1 + (c + 1))
                    if c < NC:
                        dve.wait_ge(v_ps, tb * NC + (c + 1))
                    if not first or c >= 2:
                        dve.wait_ge(dn, tb * N1 + (before(c) + 1))
                    h = HT[0:rows, c % 2, :]
                    dve.tensor_tensor(h, SG[0:rows, c % 2, :], bk[2 * (c % 2) + (c < NC)][0:rows, :], ALU.mult).then_inc(hv, 1)
                    dve.wait_ge(hv, tb * N1 + (c + 1))
                    if c < NC:
                        dve.wait_ge(w_ps, tb * NC + (c + 1))
                        dve.tensor_tensor(h, h, bk[4 + c % 2][:, :], ALU.mult).then_inc(h_ok, 1)
                    else:
                        dve.nop().then_inc(h_ok, 1)
                dve.wait_ge(dn, tb * N1 + N1)
                for b in range(2):
                    x = x2[:, bass.ds(tb * 4 + 2 * b, 2), :].rearrange("p i d -> p (i d)")
                    o = dve.tensor_tensor(x, x, bk[6 + b][:, :], ALU.add)
                o.then_inc(o_read, 1)
            blocks(dve, body)


def decoder_layer(nc, tensors, out):
    of = lambda prefix: {n[len(prefix):]: a for n, a in tensors.items() if n.startswith(prefix)}
    with ExitStack() as ctx:
        ident = ctx.enter_context(nc.sbuf_tensor("ident", [P, P], F32))
        ones = ctx.enter_context(nc.sbuf_tensor("ones", [P, P], F32))
        x1 = ctx.enter_context(nc.sbuf_tensor("x1", [P, TT, DM], F32))
        memory(nc, dict(of("L0_attn_"), x=tensors["x"]), x1, ident, ones)
        ew = expert_weights(nc, ctx)
        with ExitStack() as c:
            cross_attention(nc, c, x1, dict(of("L0_xattn_"), ctx=tensors["ctx_2048"]), ident,
                            lambda sp: load_expert_weights(sp, ew, of("L0_ffn_")))
        with ExitStack() as c:
            layernorm(nc, c, x1, "ln2")
        with ExitStack() as c:
            experts(nc, c, x1, ew, of("L0_ffn_"), ident)
        with ExitStack() as c:
            layernorm(nc, c, x1, "ln3")
        stored = ctx.enter_context(nc.semaphore("stored"))
        with nc.Block() as block:
            @block.sync
            def _(sp):
                sp.dma_start(out.rearrange("b s d -> (b s) d").rearrange("(i p) d -> p i d", p=P), x1[:, :, :])\
                  .then_inc(stored, 16)
                sp.wait_ge(stored, 16)


_INS = ["x", "ctx_2048", "L0_attn_Wk", "L0_attn_Wv", "L0_attn_Wq", "L0_attn_fast_lambda", "L0_attn_slow_lambda",
        "L0_attn_Waf", "L0_attn_baf", "L0_attn_Was", "L0_attn_bas", "L0_attn_nm_w1", "L0_attn_nm_b1",
        "L0_attn_nm_w2", "L0_attn_nm_b2", "L0_attn_ir_w1", "L0_attn_ir_b1", "L0_attn_ir_w2", "L0_attn_ir_b2",
        "L0_attn_pw_w", "L0_attn_pw_b", "L0_attn_Wo", "L0_attn_norm_w", "L0_xattn_Wq", "L0_xattn_Wkv",
        "L0_xattn_Wout", "L0_xattn_bout", "L0_ffn_w_gate", "L0_ffn_w_shared_up", "L0_ffn_w_shared_down",
        "L0_ffn_w_up", "L0_ffn_w_down"]


def kernel(**inputs):
    import numpy as _np
    import concourse.bacc as _bacc
    from concourse import mybir as _mybir
    from concourse.bass_utils import run_bass_kernel_spmd as _run

    nc = _bacc.Bacc("TRN2", target_bir_lowering=False, num_devices=1)
    arrays, tensors = {}, {}
    for name in _INS:
        a = _np.ascontiguousarray(inputs[name])
        arrays[f"in_{name}_dram"] = a
        tensors[name] = nc.dram_tensor(f"in_{name}_dram", a.shape, _mybir.dt.from_np(a.dtype), kind="ExternalInput").ap()
    out = nc.dram_tensor("out_0_dram", (NB, NS, DM), _mybir.dt.float32, kind="ExternalOutput").ap()
    decoder_layer(nc, tensors, out)
    r = _run(nc, [arrays], core_ids=[0])
    return r.results[0]["out_0_dram"]
```

```python
import numpy as np
from contextlib import ExitStack

import concourse.bass as bass
from concourse import mybir

F32 = mybir.dt.float32
F32R = mybir.dt.float32r
ACT = mybir.ActivationFunctionType
ALU = mybir.AluOpType
AX = mybir.AxisListType

P = 128
NB, NS, DM = 32, 64, 256
NT = NB * NS
KD = DM // P
TT = NT // P
CH = 4
NCH = NS // CH
CW = CH * NB
BW = 512
NBK = NT // BW
LN_EPS, RMS_EPS = 1e-5, 1e-6
PAIRS = [(s, n) for s in range(CH) for n in range(s + 1, CH)]
KQ_AT = [sum(CH - 1 - r for r in range(s)) for s in range(CH)]
O_AT = [sum(CH - r for r in range(s)) for s in range(CH)]
NKQ, NO = len(PAIRS), CH * (CH + 1) // 2


def memory_inputs(nc, ctx, pr, dram):
    sb = lambda n, s: ctx.enter_context(nc.sbuf_tensor(n, s, F32))
    sem = lambda n: ctx.enter_context(nc.semaphore(n))
    x_tok = sb("x_tok", [P, TT, DM])
    xT = sb("xT", [P, KD, NT])
    names = ["Waf", "Was", "ir_w1", "Wk", "Wq", "Wv"]
    w_in = {n: sb("w_" + n, [P, KD, P]) for n in names}
    nm_w1 = sb("nm_w1", [P, 2 * P])
    nm_w2 = sb("nm_w2", [P, 2, P])
    pw_w = sb("pw_w", [P, KD, 3])
    vec = sb("vec", [P, 16])
    BAF, BAS, NB1, NB2, IRB1, IRB2, IRW2, LAM, LOG, TINY = (
        vec[:, 0:1], vec[:, 1:2], vec[:, 2:4], vec[:, 4:5], vec[:, 5:6], vec[:, 6:7], vec[:, 7:8],
        vec[:, 8:10], vec[:, 10:12], vec[:, 12:13])
    pwb = sb("pwb", [P, 3])
    imp_w = sb("imp_w", [P, P])
    hid_i = sb("hid_i", [P, NT])
    hid_n = sb("hid_n", [P, 2, NT])
    sq = sb("sq", [P, 2, BW])
    upd = sb("upd", [P, NT])
    pwx = sb("pwx", [P, TT, 3])
    pws = sb("pws", [P, TT, 4])
    KQ, A, F4, W, S, NU, O, pw, ident, ones = (
        pr[n] for n in ("KQ", "A", "F4", "W", "S", "NU", "O", "pw", "ident", "ones"))
    bank = [ctx.enter_context(nc.psum_tensor(f"bank{i}", [P, BW], F32)) for i in range(6)]
    NBANK = len(bank)

    jobs = []
    for c in range(KD):
        for n in range(NBK):
            jobs.append(("xT", c, n, "act" if n % 2 else "dve"))
    jobs += [(w, 0, n, "dve") for w in ("Wk", "Wq") for n in range(NBK)]
    jobs += [(w, 0, n, "act") for w in ("Waf", "Was") for n in range(NBK)]
    jobs += [("norm", w, n, "act") for w in range(2) for n in range(NBK)]
    jobs += [("pw", 0, 0, "dve")]
    jobs += [("Wv", 0, n, "dve") for n in range(NBK)]
    jobs += [("ir_w1", 0, n, "act") for n in range(NBK)]
    jobs += [("hid_n", m, n, "act") for n in range(NBK) for m in range(2)]
    jobs += [("imp", 0, n, "act") for n in range(NBK)]
    jobs += [("nu", 0, n, "act") for n in range(NBK)]
    order = {}
    count = {"act": 0, "dve": 0}
    for j, job in enumerate(jobs):
        count[job[3]] += 1
        order[j] = count[job[3]]
    place = {job[:3]: j for j, job in enumerate(jobs)}

    x_in = sem("x_in")
    w_loaded = sem("w_loaded")
    made = sem("bank_filled")
    freed = {"act": sem("bank_read_act"), "dve": sem("bank_read_dve")}
    consts = sem("consts_ready")
    squares = sem("squares_ready")
    logits = sem("path_logits_ready")
    act_own = sem("act_own")
    dve_own = sem("dve_own")
    pool_own = sem("pool_own")
    alpha = sem("alpha_ready")
    impw = sem("importance_weights_ready")
    keys = sem("keys_ready")
    vcopy = sem("values_copied")

    def filled(eng, job):
        eng.wait_ge(made, place[job] + 1)

    with nc.Block() as block:
        @block.sync
        def _(sp):
            sp.dma_start(x_tok[:, :, :], dram["x"].rearrange("b s d -> (b s) d")
                         .rearrange("(i p) d -> p i d", p=P)).then_inc(x_in, 16)
            for n in names:
                sp.dma_start(w_in[n][:, :, :], dram[n].rearrange("(c p) m -> p c m", p=P)).then_inc(w_loaded, 16)
            sp.dma_start(nm_w1[:, :], dram["nm_w1"]).then_inc(w_loaded, 16)
            sp.dma_start(nm_w2[:, :, :], dram["nm_w2"].rearrange("(c p) m -> p c m", p=P)).then_inc(w_loaded, 16)
            sp.dma_start(pw_w[:, :, :], dram["pw_w"].rearrange("(c p) m -> p c m", p=P)).then_inc(w_loaded, 16)
            col = lambda a: a.rearrange("(p o) -> p o", o=1)
            for to, a in ((BAF, col(dram["baf"])), (BAS, col(dram["bas"])), (NB2, col(dram["nm_b2"])),
                          (IRB1, col(dram["ir_b1"])), (IRW2, dram["ir_w2"]),
                          (LAM[:, 0:1], col(dram["fast_lambda"])), (LAM[:, 1:2], col(dram["slow_lambda"])),
                          (NB1[:, 0:1], col(dram["nm_b1"][0:P])), (NB1[:, 1:2], col(dram["nm_b1"][P:2 * P])),
                          (IRB2, dram["ir_b2"].partition_broadcast(P)),
                          (pwb[:, :], dram["pw_b"].partition_broadcast(P))):
                sp.dma_start(to, a).then_inc(w_loaded, 16)
        W_ALL = 16 * (len(names) + 3 + 11)

        @block.gpsimd
        def _(pool):
            pool.memset(ident[:, :], 0.0).then_inc(pool_own, 1)
            pool.memset(ones[:, :], 1.0).then_inc(consts, 1)
            pool.memset(TINY, 1e-8).then_inc(consts, 1)
            pool.wait_ge(pool_own, 1)
            pool.affine_select(out=ident[:, :], in_=ident[:, :], compare_op=ALU.not_equal, fill=1.0,
                               base=0, pattern=[[-1, P]], channel_multiplier=1).then_inc(consts, 1)
            pool.memset(O[:, :, :], 0.0)
            for w in range(2):
                for n in range(NBK):
                    i = w * NBK + n
                    pool.wait_ge(freed["dve"], order[place[("Wk" if w == 0 else "Wq", 0, n)]])
                    if i >= 2:
                        pool.wait_ge(made, place[("norm", (i - 2) // NBK, (i - 2) % NBK)] + 1)
                    cols = KQ[:, w, n * BW:(n + 1) * BW]
                    pool.tensor_tensor(sq[:, i % 2, :], cols, cols, ALU.mult).then_inc(squares, 1)
            pool.wait_ge(freed["dve"], order[place[("Wv", 0, NBK - 1)]])
            pool.tensor_copy(S[:, 1, 0, :], S[:, 0, 0, :]).then_inc(vcopy, 1)
            pool.tensor_copy(S[:, 0, 1, :], S[:, 0, 0, :]).then_inc(vcopy, 1)
            pool.memset(S[:, 1, 1, :], 0.0).then_inc(vcopy, 1)
            pool.wait_ge(alpha, 2)
            own = 1

            def link(ins):
                nonlocal own
                own += 1
                ins.then_inc(pool_own, 1)
                pool.wait_ge(pool_own, own)

            chunks = lambda x, t: x.rearrange("p m (j t b) -> p m j t b", t=CH, b=NB)[:, :, :, t, :]
            link(pool.tensor_copy(chunks(F4[:, :, :], 0), chunks(A[:, :, :], 0)))
            for t in range(1, CH):
                link(pool.tensor_tensor(chunks(F4[:, :, :], t), chunks(F4[:, :, :], t - 1), chunks(A[:, :, :], t), ALU.mult))
            pool.wait_ge(vcopy, 3)

        @block.tensor
        def _(pe):
            pe.wait_ge(consts, 3)
            for j, (what, c, n, _) in enumerate(jobs):
                ps = bank[j % NBANK]
                if j >= NBANK:
                    last = j - NBANK
                    pe.wait_ge(freed[jobs[last][3]], order[last])
                tok = slice(n * BW, (n + 1) * BW)
                if what == "xT":
                    if j == 0:
                        pe.wait_ge(x_in, 16)
                    for i in range(4):
                        mm = pe.transpose(ps[:, i * P:(i + 1) * P], x_tok[:, 4 * n + i, c * P:(c + 1) * P], ident[:, :])
                elif what in w_in:
                    if (what, n) == ("Wk", 0):
                        pe.wait_ge(w_loaded, W_ALL)
                        for e in ("act", "dve"):
                            pe.wait_ge(freed[e], KD * NBK // 2)
                    for k in range(KD):
                        mm = pe.matmul(ps[:, :], w_in[what][:, k, :], xT[:, k, tok], start=k == 0, stop=k == KD - 1)
                elif what == "norm":
                    pe.wait_ge(squares, c * NBK + n + 1)
                    mm = pe.matmul(ps[:, :], ones[:, :], sq[:, (c * NBK + n) % 2, :], start=True, stop=True)
                elif what == "hid_n":
                    pe.wait_ge(freed["dve"], order[place[("Wv", 0, n)]])
                    mm = pe.matmul(ps[:, :], nm_w1[:, c * P:(c + 1) * P], S[:, 0, 0, tok], start=True, stop=True)
                elif what == "imp":
                    pe.wait_ge(impw, 1)
                    pe.wait_ge(freed["act"], order[place[("ir_w1", 0, n)]])
                    mm = pe.matmul(ps[:, :], imp_w[:, :], hid_i[:, tok], start=True, stop=True)
                elif what == "nu":
                    pe.wait_ge(freed["act"], order[place[("hid_n", 1, n)]])
                    for k in range(2):
                        mm = pe.matmul(ps[:, :], nm_w2[:, k, :], hid_n[:, k, tok], start=k == 0, stop=k == 1)
                elif what == "pw":
                    for i in range(TT):
                        for k in range(KD):
                            mm = pe.matmul(ps[:, 3 * i:3 * i + 3], xT[:, k, i * P:(i + 1) * P], pw_w[:, k, :],
                                           start=k == 0, stop=k == KD - 1)
                mm.then_inc(made, 1)

        def empty_xT(eng, c, n, mine):
            src = bank[place[("xT", c, n)] % NBANK][:, :].rearrange("p (b s) -> p s b", s=NS)
            dst = xT[:, c, :].rearrange("p (s b) -> p s b", b=NB)[:, :, 8 * n:8 * n + 8]
            if mine == "act":
                eng.activation(dst, src, ACT.Copy).then_inc(freed["act"], 1)
            else:
                eng.tensor_copy(dst, src).then_inc(freed["dve"], 1)

        @block.scalar
        def _(act):
            def alphas():
                act.activation(LOG, LOG, ACT.Ln, bias=TINY).then_inc(act_own, 1)
                act.wait_ge(act_own, 2)
                act.activation(LOG, LOG, ACT.Copy, scale=8.0).then_inc(act_own, 1)
                act.wait_ge(act_own, 3)
                act.wait_ge(freed["act"], order[place[("Was", 0, NBK - 1)]])
                for m in range(2):
                    act.activation(A[:, m, :], A[:, m, :], ACT.Exp, scale=LOG[:, m:m + 1]).then_inc(alpha, 1)
                act.wait_ge(logits, 1)
                act.activation(pwx[:, :, :], pwx[:, :, :], ACT.Exp).then_inc(alpha, 1)

            act.wait_ge(consts, 3)
            act.wait_ge(w_loaded, W_ALL)
            act.activation(LOG, LAM, ACT.Sigmoid).then_inc(act_own, 1)
            act.wait_ge(act_own, 1)
            for (what, c, n, mine) in [j for j in jobs if j[3] == "act"]:
                ps = bank[place[(what, c, n)] % NBANK][:, :]
                tok = slice(n * BW, (n + 1) * BW)
                filled(act, (what, c, n))
                if what == "xT":
                    empty_xT(act, c, n, "act")
                elif what in ("Waf", "Was"):
                    m = 0 if what == "Waf" else 1
                    act.activation(A[:, m, tok], ps, ACT.Sigmoid, bias=(BAF, BAS)[m]).then_inc(freed["act"], 1)
                elif what == "ir_w1":
                    act.activation(hid_i[:, tok], ps, ACT.Gelu, bias=IRB1).then_inc(freed["act"], 1)
                elif what == "norm":
                    act.activation(W[:, c, tok], ps, ACT.Sqrt).then_inc(freed["act"], 1)
                    if (c, n) == (1, NBK - 1):
                        alphas()
                elif what == "hid_n":
                    act.activation(hid_n[:, c, tok], ps, ACT.Gelu, bias=NB1[:, c:c + 1]).then_inc(freed["act"], 1)
                elif what == "imp":
                    act.activation(upd[:, tok], ps, ACT.Sigmoid, bias=IRB2).then_inc(freed["act"], 1)
                elif what == "nu":
                    act.activation(NU[:, tok], ps, ACT.Identity, bias=NB2).then_inc(freed["act"], 1)
        @block.vector
        def _(dve):
            own = 0
            dve.wait_ge(consts, 3)
            dve.wait_ge(w_loaded, W_ALL)
            dve.tensor_scalar(imp_w[:, :], ones[:, :], IRW2, None, ALU.mult).then_inc(impw, 1)
            def link(ins):
                nonlocal own
                own += 1
                ins.then_inc(dve_own, 1)
                dve.wait_ge(dve_own, own)

            def unit_length(i):
                w, n = divmod(i, NBK)
                dve.wait_ge(freed["act"], order[place[("norm", w, n)]])
                part = W[:, w, n * BW:(n + 1) * BW]
                link(dve.tensor_scalar(part, part, 1e-12, None, ALU.max))
                link(dve.reciprocal(part, part))
                cols = KQ[:, w, n * BW:(n + 1) * BW]
                dve.scalar_tensor_tensor(cols, cols, 0.5 if w else 1.0, part, ALU.mult, ALU.mult).then_inc(keys, 1)

            for (what, c, n, mine) in [j for j in jobs if j[3] == "dve"]:
                ps = bank[place[(what, c, n)] % NBANK][:, :]
                tok = slice(n * BW, (n + 1) * BW)
                if what == "pw":
                    unit_length(0)
                    unit_length(1)
                    filled(dve, ("pw", 0, 0))
                    ps = ps[:, 0:3 * TT].rearrange("p (i j) -> p i j", j=3)
                    dve.tensor_tensor(pwx[:, :, :], ps, pwb[:, :].unsqueeze(1).broadcast_to((P, TT, 3)),
                                      ALU.add).then_inc(freed["dve"], 1)
                    dve.wait_ge(freed["dve"], order[place[("pw", 0, 0)]])
                    link(dve.tensor_reduce(pws[:, :, 0:1], pwx[:, :, :], AX.X, ALU.max))
                    dve.tensor_tensor(pwx[:, :, :], pwx[:, :, :], pws[:, :, 0:1].broadcast_to((P, TT, 3)),
                                      ALU.subtract).then_inc(logits, 1)
                    continue
                filled(dve, (what, c, n))
                if what == "xT":
                    empty_xT(dve, c, n, "dve")
                elif what == "Wv":
                    dve.tensor_copy(S[:, 0, 0, tok], ps).then_inc(freed["dve"], 1)
                    if n == 0:
                        unit_length(2)
                else:
                    dve.tensor_copy(KQ[:, 0 if what == "Wk" else 1, tok], ps).then_inc(freed["dve"], 1)
            for i in range(3, 2 * NBK):
                unit_length(i)
            dve.wait_ge(alpha, 3)
            link(dve.tensor_reduce(pws[:, :, 1:2], pwx[:, :, :], AX.X, ALU.add))
            link(dve.reciprocal(pws[:, :, 2:3], pws[:, :, 1:2]))
            link(dve.tensor_tensor(pw[:, :, :], pwx[:, :, :], pws[:, :, 2:3].broadcast_to((P, TT, 3)), ALU.mult))
            dve.wait_ge(keys, 2 * NBK)
            for m in range(2):
                link(dve.tensor_scalar(W[:, m, :], A[:, m, :], -1.0, 1.0, ALU.mult, ALU.add))
                link(dve.tensor_tensor(W[:, m, :], W[:, m, :], KQ[:, 0, :], ALU.mult))
            dve.wait_ge(freed["act"], order[place[("imp", 0, NBK - 1)]])
            link(dve.scalar_tensor_tensor(W[:, 1, :], upd[:, :], 0.5, W[:, 1, :], ALU.is_gt, ALU.mult))


def recurrence(nc, ctx, pr):
    sb = lambda n, s: ctx.enter_context(nc.sbuf_tensor(n, s, F32))
    sem = lambda n: ctx.enter_context(nc.semaphore(n))
    KQ, A, F4, W, S, O, ident, ones = (pr[n] for n in ("KQ", "A", "F4", "W", "S", "O", "ident", "ones"))
    LV = {n: (n & -n) * CH for n in range(1, NCH)}
    HMAX = max(LV.values())
    nblk = lambda n: 2 * LV[n] // CH
    total = lambda n: sum(nblk(m) for m in range(1, n))
    groups = lambda n: -(-nblk(n) // 4)
    turned = lambda n: sum(groups(m) for m in range(1, n))
    gathers = lambda n: sum(2 * groups(m) for m in range(1, n) if LV[m] > CH)
    both = lambda n: LV[n] * NB * 2 <= HMAX * NB
    block_order = lambda n: list(range(nblk(n))) if both(n) else [*range(0, nblk(n), 2), *range(1, nblk(n), 2)]
    BY_DVE = {8}
    parts = lambda n, m: sum(1 if both(x) else 2 for x in range(1, n) if (x in BY_DVE) == (n in BY_DVE)) + \
        (1 if both(n) else 1 + m)
    P_AT = (2, 1)
    spread_to = lambda n, y, c: 1 if n == 1 else min(3, 2 + 2 * y // c) if c < 8 else min(3, 1 + 3 * y // c)
    blocks_at, parts_at = {}, {}
    for n in LV:
        runs = [(max(n - 2, 0), range(nblk(n)), 0)] if both(n) else \
            [(n - 3 + m, range(m * nblk(n) // 2, (m + 1) * nblk(n) // 2), m) for m in range(2)]
        for j, places, m in runs:
            if n in BY_DVE:
                parts_at[j, P_AT[m]] = (n, m)
            for y, at in enumerate(places):
                if n in BY_DVE:
                    i = P_AT[m] + 1 + (3 - P_AT[m]) * y // len(places)
                else:
                    i = 0 if n + 1 in BY_DVE else spread_to(n, y, len(places))
                blocks_at.setdefault((j, i), []).append((n, at))

    Fd = sb("Fd", [P, 2, CH, CH, NB])
    PK = sb("PK", [P, 2, 2, 2, NKQ, NB])
    PO = sb("PO", [P, 2, 2, NO, NB])
    C = sb("C", [P, 2, 2, 2, NKQ, NB])
    CO = sb("CO", [P, 2, 2, NO, NB])
    DD = sb("DD", [P, 2, HMAX // CH - 2, NB])
    LW = sb("LW", [P, HMAX * NB])
    LL = sb("LL", [P, 3 * HMAX * NB])
    LL4 = sb("LL4", [P, 2 * 3 * CW])
    G1 = sb("G1", [P, 2, 3 * P])
    G2 = sb("G2", [P, 2 * HMAX // CH, 3 * P])
    UG = sb("UG", [P, 2, 4, P])
    UT = sb("UT", [P, 2, 4, P])
    sqr = sb("sqr", [P, NB])
    perr = sb("perr", [P, NB])
    tk = sb("tk", [P, 2, CH - 1, NB])
    tq = sb("tq", [P, 2, CH - 1, NB])
    tq1 = sb("tq1", [P, 2, NB])
    to = sb("to", [P, 2, CH, NB])
    hs = sorted(set(LV.values()))
    selectors = LL[:, 0:len(hs) * P].rearrange("p (i c) -> p i c", c=P)
    mask = {h: sb(f"mask{h}", [P, P]) for h in hs}
    psE = ctx.enter_context(nc.psum_tensor("psE", [P, BW], F32))
    psC = [ctx.enter_context(nc.psum_tensor(f"psC{i}", [P, BW], F32)) for i in range(2)]
    psG = [ctx.enter_context(nc.psum_tensor(f"psG{i}", [P, BW], F32)) for i in range(2)]
    psT = ctx.enter_context(nc.psum_tensor("psT", [P, BW], F32))
    psR = [ctx.enter_context(nc.psum_tensor(f"psR{i}", [P, BW], F32)) for i in range(2)]

    pool_own = sem("pool_own2")
    sel_ok = sem("selectors_ready")
    mask_psum = sem("masks_in_psum")
    masks = sem("masks_ready")
    sq_ready = sem("error_squares_ready")
    err_ready = sem("errors_ready")
    sur_ready = sem("surprises_ready")
    u_ready = sem("u_ready")
    mul_done = sem("coefficients_read")
    terms = sem("coefficient_terms_ready")
    coef = sem("coefficients_in_psum")
    coef_out = sem("coefficients_ready")
    lw_ready = sem("decays_ready")
    ll_ready = sem("decayed_ready")
    pool_ready = sem("decayed_by_pool")
    g_psum = sem("blocks_in_psum")
    g_ready = sem("blocks_ready")
    ug_ready = sem("u_gathered")
    t_psum = sem("transposes_in_psum")
    t_ready = sem("transposes_ready")
    r_psum = sem("reads_in_psum")
    r_done = sem("reads_added")
    dve_own = sem("dve_own2")

    def g_slot(n, i):
        return G1[:, i, :] if LV[n] == CH else G2[:, 2 * i + 1 if LV[n] == 2 * CH else i, :]

    pieces = lambda n, i: [4 * n + x for x in ((), (0, 1), (2, 3), ())[i]] if n < NCH else []
    cols = lambda t, n=1: slice(t * NB, (t + n) * NB)

    def products(eng, link, n, ms, dec):
        h, c, nm = LV[n], n * CH, len(ms)
        ll = (LL if h > CH else LL4)[:, 0:nm * 3 * h * NB].rearrange("p (m k c) -> p m k c", m=nm, k=3)
        dec = ll[:, :, 2, :] if dec is None else dec
        eng.tensor_copy(ll[:, :, 0:2, 0:NB], KQ[:, :, cols(c)].unsqueeze(1).broadcast_to((P, nm, 2, NB)))
        for kind in range(2):
            mul = eng.tensor_tensor(ll[:, :, kind, NB:h * NB], dec[:, :, 0:(h - 1) * NB],
                                    KQ[:, kind, cols(c + 1, h - 1)].unsqueeze(1).broadcast_to((P, nm, (h - 1) * NB)), ALU.mult)
        link(mul)
        return eng.tensor_tensor(ll[:, :, 2, :], dec, KQ[:, 1, cols(c, h)].unsqueeze(1).broadcast_to((P, nm, h * NB)), ALU.mult)

    with nc.Block() as block:
        @block.gpsimd
        def _(pool):
            own = 0

            def link(ins):
                nonlocal own
                own += 1
                ins.then_inc(pool_own, 1)
                pool.wait_ge(pool_own, own)

            def terms_of(j):
                part = lambda x, k: x[:, :, cols(j * CH, CH)].rearrange("p m (t b) -> p m t b", b=NB)
                a_, w_, kq = part(A, 2), part(W, 2), part(KQ, 2)
                flat = Fd[:, :, :, :, :].rearrange("p m s t b -> p m (s t) b")
                link(pool.tensor_copy(flat[:, :, 0:CH * CH:CH + 1, :], w_))
                for l in range(1, CH):
                    n = CH - l
                    at = lambda k: slice(k, k + (n - 1) * (CH + 1) + 1, CH + 1)
                    link(pool.tensor_tensor(flat[:, :, at(l), :], flat[:, :, at(l - 1), :], a_[:, :, l:CH, :], ALU.mult))
                if j >= 2:
                    pool.wait_ge(coef, 4 * (j - 1))
                for s in range(CH - 1):
                    n = CH - 1 - s
                    for kind in range(2):
                        pool.tensor_tensor(PK[:, j % 2, :, kind, KQ_AT[s]:KQ_AT[s] + n, :], Fd[:, :, s, s:CH - 1, :],
                                           kq[:, kind, s + 1:CH, :].unsqueeze(1).broadcast_to((P, 2, n, NB)), ALU.mult)
                for s in range(CH):
                    n = CH - s
                    mul = pool.tensor_tensor(PO[:, j % 2, :, O_AT[s]:O_AT[s] + n, :], Fd[:, :, s, s:CH, :],
                                             kq[:, 1, s:CH, :].unsqueeze(1).broadcast_to((P, 2, n, NB)), ALU.mult)
                mul.then_inc(terms, 1)
                link(pool.tensor_copy(w_, flat[:, :, CH - 1:CH * CH:CH, :]))
                pool.wait_ge(terms, j + 1)

            def decays_of(n):
                h, c = LV[n], n * CH
                g, q = P // h, h // CH
                whole = lambda j: F4[:, :, cols(j * CH + CH - 1)]
                over = lambda d, i: whole((n, n - 1)[d]) if i == 1 else DD[:, :, i - 2, :]

                def over_chunks(d):
                    for i in range(2, q):
                        link(pool.tensor_tensor(DD[:, :, i - 2, :], over(d, i - 1), whole(n - i if d else n + i - 1), ALU.mult))
                for ms in ([(0, 1)] if both(n) else [(0,), (1,)]):
                    if ms == (1,):
                        pool.wait_ge(g_psum, total(n) + nblk(n) // 2)
                    elif n >= 3:
                        pool.wait_ge(g_psum, total(n - 1))
                    m0, nm = ms[0], len(ms)
                    mm = slice(m0, m0 + nm)
                    ll = (LL if h > CH else LL4)[:, 0:nm * 3 * h * NB].rearrange("p (m k c) -> p m k c", m=nm, k=3)
                    if h > CH:
                        over_chunks(1)
                        for m in ms:
                            dst = LW[:, (m - m0) * h * NB:(m - m0 + 1) * h * NB].rearrange("p (g t b) -> p g t b", t=h, b=g)
                            for i in range(q):
                                t0 = h - CH * (i + 1)
                                src = W[:, m, cols(c - h + t0, CH)].rearrange("p (t g b) -> p g t b", t=CH, b=g)
                                out = dst[:, :, t0:t0 + CH, :]
                                if i:
                                    e = over(1, i)[:, m, :].rearrange("p (g b) -> p g b", b=g).unsqueeze(2)\
                                        .broadcast_to((P, NB // g, CH, g))
                                    last = pool.tensor_tensor(out, src, e, ALU.mult)
                                else:
                                    pool.tensor_copy(out, src)
                        link(last)
                        over_chunks(0)
                        pool.tensor_copy(ll[:, :, 2, 0:CW], F4[:, mm, cols(c, CH)])
                        for i in range(1, q):
                            dec = pool.tensor_tensor(
                                ll[:, :, 2, i * CW:(i + 1) * CW].rearrange("p m (t b) -> p m t b", b=NB),
                                F4[:, mm, cols(c + i * CH, CH)].rearrange("p m (t b) -> p m t b", b=NB),
                                over(0, i)[:, mm, :].unsqueeze(2).broadcast_to((P, nm, CH, NB)), ALU.mult)
                        if n in BY_DVE:
                            dec.then_inc(lw_ready, 1)
                        else:
                            link(dec)
                    if n not in BY_DVE:
                        products(pool, link, n, ms, None if h > CH else F4[:, mm, cols(c, CH)]).then_inc(pool_ready, 1)
                        pool.wait_ge(pool_ready, parts(n, 0))

            link(pool.memset(selectors, 0.0))
            for i, h in enumerate(hs):
                g = P // h
                v = selectors[0:g, i, :].rearrange("p (t b) -> p t b", b=g)
                pool.affine_select(out=v, in_=v, compare_op=ALU.not_equal, fill=1.0, base=0,
                                   pattern=[[0, h], [-1, g]], channel_multiplier=1).then_inc(sel_ok, 1)
            terms_of(0)
            terms_of(1)
            pool.wait_ge(mask_psum, 1)
            decays_of(1)
            for j in range(1, NCH):
                if j > 1:
                    terms_of(j)
                if j + 1 < NCH:
                    decays_of(j + 1)

        def piece(x):
            j, i = divmod(x, 4)
            m = i % 2
            if i < 2:
                return (PK[:, j % 2, m, :, :, :].rearrange("p k n b -> p (k n b)"),
                        C[:, j % 2, m, :, :, :].rearrange("p k n b -> p (k n b)"), 2 * NKQ * NB)
            return (PO[:, j % 2, m, :, :].rearrange("p n b -> p (n b)"),
                    CO[:, j % 2, m, :, :].rearrange("p n b -> p (n b)"), NO * NB)

        @block.tensor
        def _(pe):
            def sum_piece(x):
                src, _, n = piece(x)
                pe.wait_ge(terms, x // 4 + 1)
                if x >= 2:
                    pe.wait_ge(coef_out, x - 1)
                pe.matmul(psC[x % 2][:, 0:n], ones[:, :], src, start=True, stop=True).then_inc(coef, 1)

            def make_block(n, at):
                h, i = LV[n], block_order(n)[at]
                gi, m = divmod(i, 2)
                g = P // h
                k = total(n) + at
                pe.wait_ge(ll_ready if n in BY_DVE else pool_ready, parts(n, m))
                if k >= 2:
                    pe.wait_ge(g_ready, k - 1)
                off = m if both(n) else 0
                rhs = (LL if h > CH else LL4)[:, off * 3 * h * NB:(off + 1) * 3 * h * NB]\
                    .rearrange("p (k t b) -> p k t b", k=3, b=NB)
                lhs = W[:, m, cols((n - 1) * CH, CH)] if h == CH else LW[:, off * h * NB + gi * P:off * h * NB + (gi + 1) * P]
                pe.matmul(psG[k % 2][:, 0:3 * P], lhs, rhs[:, :, :, gi * g:(gi + 1) * g], start=True, stop=True)\
                  .then_inc(g_psum, 1)

            def turn(n, gr):
                k = turned(n) + gr
                if k >= 1:
                    pe.wait_ge(t_ready, k)
                if LV[n] > CH:
                    pe.wait_ge(ug_ready, gathers(n) + 2 * (gr + 1))
                else:
                    pe.wait_ge(u_ready, n * CH)
                for i in range(min(4, nblk(n))):
                    src = S[:, i, 0, cols((n - 1) * CH, CH)] if LV[n] == CH else UG[:, k % 2, i, :]
                    mm = pe.transpose(psT[:, i * P:(i + 1) * P], src, ident[:, :])
                mm.then_inc(t_psum, 1)

            def read(n, gr):
                for i in range(4 * gr, min(4 * gr + 4, nblk(n))):
                    k = total(n) + i
                    pe.wait_ge(t_ready, turned(n) + gr + 1)
                    pe.wait_ge(g_ready, k + 1 if both(n) else total(n + 1))
                    if k >= 2:
                        pe.wait_ge(r_done, k - 1)
                    pe.matmul(psR[k % 2][:, 0:3 * P], UT[:, (turned(n) + gr) % 2, i % 4, :], g_slot(n, i),
                              start=True, stop=True).then_inc(r_psum, 1)

            def boundary(n):
                for gr in range(groups(n)):
                    turn(n, gr)
                    if gr:
                        read(n, gr - 1)
                read(n, groups(n) - 1)

            pe.wait_ge(sel_ok, len(hs))
            for i, h in enumerate(hs):
                g = P // h
                mm = pe.matmul(psT[:, i * P:(i + 1) * P], selectors[0:g, i, :], selectors[0:g, i, :], start=True, stop=True)
            mm.then_inc(mask_psum, 1)
            pe.wait_ge(masks, len(hs))
            for x in range(4):
                sum_piece(x)
            for t in range(NS):
                j, i = divmod(t, CH)
                pe.wait_ge(sq_ready, t + 1)
                pe.matmul(psE[:, 0:NB], ones[:, :], sqr[:, :], start=True, stop=True).then_inc(err_ready, 1)
                if i == CH - 1 and j + 1 < NCH:
                    boundary(j + 1)
                for x in pieces(j + 1, i):
                    sum_piece(x)
                for n, at in blocks_at.get((j, i), []):
                    make_block(n, at)

        @block.scalar
        def _(act):
            def empty_piece(x):
                _, dst, n = piece(x)
                j = x // 4
                act.wait_ge(coef, x + 1)
                if j >= 2:
                    act.wait_ge(mul_done, (j - 1) * CH)
                act.activation(dst, psC[x % 2][:, 0:n], ACT.Copy).then_inc(coef_out, 1)

            for x in range(4):
                empty_piece(x)
            for t in range(NS):
                j, i = divmod(t, CH)
                act.wait_ge(err_ready, t + 1)
                act.activation(S[:, 1, 1, cols(t)], psE[:, 0:NB], ACT.Sigmoid, scale=1.0 / (1.0 + 1e-6))\
                   .then_inc(sur_ready, 1)
                for x in pieces(j + 1, i):
                    empty_piece(x)
                if i == CH - 1 and j + 1 < NCH:
                    n = j + 1
                    h = LV[n]
                    g = P // h
                    for gr in range(groups(n) + 1):
                        k = turned(n) + gr
                        if h > CH and gr < groups(n):
                            act.wait_ge(u_ready, n * CH)
                            if k >= 2:
                                act.wait_ge(t_psum, k - 1)
                            for m in range(2):
                                src = S[:, m, 0, cols(n * CH - h, h)].rearrange("p (t b) -> p t b", b=NB)
                                src = src[:, :, 2 * gr * g:2 * (gr + 1) * g].rearrange("p t (g b) -> p g t b", b=g)
                                act.activation(UG[:, k % 2, m:4:2, :].rearrange("p g (t b) -> p g t b", b=g), src,
                                               ACT.Copy).then_inc(ug_ready, 1)
                        if gr:
                            k -= 1
                            size = min(4, nblk(n))
                            if k >= 2:
                                act.wait_ge(r_psum, [total(x) + min(4 * y + 4, nblk(x)) for x in sorted(LV)
                                                     for y in range(groups(x))][k - 2])
                            act.wait_ge(t_psum, k + 1)
                            act.activation(UT[:, k % 2, 0:size, :], psT[:, 0:size * P], ACT.Copy).then_inc(t_ready, 1)

        @block.vector
        def _(dve):
            own = 0

            def mark(ins):
                nonlocal own
                own += 1
                ins.then_inc(dve_own, 1)
                return own

            def keep_block(n, at):
                i = block_order(n)[at]
                k = total(n) + at
                dve.wait_ge(g_psum, k + 1)
                if n >= 3:
                    dve.wait_ge(r_psum, total(n - 1 if both(n) or at >= nblk(n) // 2 else n - 3))
                dve.tensor_tensor(g_slot(n, i).rearrange("p (k c) -> p k c", k=3),
                                  psG[k % 2][:, 0:3 * P].rearrange("p (k c) -> p k c", k=3),
                                  mask[LV[n]][:, :].unsqueeze(1).broadcast_to((P, 3, P)), ALU.mult).then_inc(g_ready, 1)

            def square_error(t):
                dve.wait_ge(dve_own, mark(dve.tensor_tensor(perr[:, :], S[:, 0, 1, cols(t)], S[:, 1, 1, cols(t)], ALU.add)))
                dve.tensor_tensor(sqr[:, :], perr[:, :], perr[:, :], ALU.mult).then_inc(sq_ready, 1)

            dve.wait_ge(mask_psum, 1)
            for i, h in enumerate(hs):
                dve.tensor_copy(mask[h][:, :], psT[:, i * P:(i + 1) * P]).then_inc(masks, 1)
            dve.wait_ge(masks, len(hs))
            square_error(0)
            keys_done = 0
            for t in range(NS):
                j, i = divmod(t, CH)
                u = S[:, :, 0, cols(t)]
                row = lambda n: u.unsqueeze(2).broadcast_to((P, 2, n, NB))
                dve.wait_ge(sur_ready, t + 1)
                if keys_done:
                    dve.wait_ge(dve_own, keys_done)
                dve.tensor_tensor(u, u, S[:, 1, 1, cols(t)].unsqueeze(1).broadcast_to((P, 2, NB)), ALU.mult)\
                   .then_inc(u_ready, 1)
                if i == 0:
                    dve.wait_ge(coef_out, 4 * (j + 1))
                dve.wait_ge(u_ready, t + 1)
                n = CH - 1 - i
                if n:
                    dve.wait_ge(dve_own, mark(dve.tensor_tensor(tq1[:, :, :], C[:, j % 2, :, 1, KQ_AT[i], :], u, ALU.mult)))
                    nxt = S[:, :, 1, cols(t + 1)]
                    dve.wait_ge(dve_own, mark(dve.tensor_tensor(nxt, nxt, tq1[:, :, :], ALU.subtract)))
                    square_error(t + 1)
                if n:
                    dve.tensor_tensor(tk[:, :, 0:n, :], C[:, j % 2, :, 0, KQ_AT[i]:KQ_AT[i] + n, :], row(n), ALU.mult)
                if n > 1:
                    dve.tensor_tensor(tq[:, :, 1:n, :], C[:, j % 2, :, 1, KQ_AT[i] + 1:KQ_AT[i] + n, :], row(n - 1), ALU.mult)
                dve.tensor_tensor(to[:, :, 0:n + 1, :], CO[:, j % 2, :, O_AT[i]:O_AT[i] + n + 1, :], row(n + 1), ALU.mult)\
                   .then_inc(mul_done, 1)
                dve.wait_ge(mul_done, t + 1)
                later = lambda x, a, k: x[:, :, cols(a, k)].rearrange("p m (t b) -> p m t b", b=NB)
                if n:
                    y = later(S[:, :, 0, :], t + 1, n)
                    keys_done = mark(dve.tensor_tensor(y, y, tk[:, :, 0:n, :], ALU.subtract))
                if n > 1:
                    y = later(S[:, :, 1, :], t + 2, n - 1)
                    mark(dve.tensor_tensor(y, y, tq[:, :, 1:n, :], ALU.subtract))
                y = later(O, t, n + 1)
                last = mark(dve.tensor_tensor(y, y, to[:, :, 0:n + 1, :], ALU.add))
                if i == CH - 1 and j + 1 < NCH:
                    nb, h, c = j + 1, LV[j + 1], (j + 1) * CH
                    g = P // h
                    dve.wait_ge(dve_own, last)
                    for b in range(nblk(nb)):
                        gi, m = divmod(b, 2)
                        k = total(nb) + b
                        ps = psR[k % 2][:, 0:3 * P].rearrange("p (k t b) -> p k t b", k=3, b=g)
                        y = S[:, m, :, cols(c, h)].rearrange("p k (t b) -> p k t b", b=NB)[:, :, :, gi * g:(gi + 1) * g]
                        z = O[:, m, cols(c, h)].rearrange("p (t b) -> p t b", b=NB)[:, :, gi * g:(gi + 1) * g]
                        dve.wait_ge(r_psum, k + 1)
                        dve.tensor_tensor(y, y, ps[:, 0:2], ALU.subtract)
                        dve.tensor_tensor(z, z, ps[:, 2], ALU.add).then_inc(r_done, 1)
                    dve.wait_ge(r_done, total(nb + 1))
                    square_error(t + 1)
                if (j, i) in parts_at:
                    n, m = parts_at[j, i]
                    dve.wait_ge(lw_ready, parts(n, m))
                    products(dve, lambda ins: dve.wait_ge(dve_own, mark(ins)), n, (0, 1) if both(n) else (m,), None)\
                        .then_inc(ll_ready, 1)
                for n, at in blocks_at.get((j, i), []):
                    keep_block(n, at)


def memory_output(nc, ctx, pr, dram, x1):
    sb = lambda n, s: ctx.enter_context(nc.sbuf_tensor(n, s, F32))
    sem = lambda n: ctx.enter_context(nc.semaphore(n))
    S, NU, O, pw, ident, ones = (pr[n] for n in ("S", "NU", "O", "pw", "ident", "ones"))
    x_tok = sb("x_tok3", [P, TT, DM])
    Wo = sb("Wo", [P, DM])
    nw = sb("nw", [P, 1])
    diag = sb("diag", [P, 3, BW])
    mixed = [sb(f"mixed{k}", [P, 2, BW]) for k in range(3)]
    on = sb("on", [P, NT])
    keep = sb("keep", [P, NT])
    gain = sb("gain", [P, NT])
    neural = sb("neural", [P, NT])
    stats = sb("stats", [P, TT, 6])
    mv = sb("mv", [P, TT, 2])
    inv = sb("inv", [P, TT])
    shift = sb("shift", [P, TT, 1])
    shift_ok = sem("shift_ready")
    BY_ACT = range(TT - 6, TT)
    eps = sb("eps", [P, 2])
    bank = [ctx.enter_context(nc.psum_tensor(f"psB{i}", [P, BW], F32)) for i in range(8)]
    psQ = bank[6]
    psO = [bank[0], bank[1], bank[2], bank[3]]
    loaded = sem("loaded3")
    diag_ready = sem("diagonals_ready")
    spread = sem("weights_spread")
    weighted = sem("paths_weighted")
    summed = sem("paths_summed")
    own_d = sem("dve_own3")
    sq3 = sem("squares3")
    ms = sem("mean_squares")
    root = sem("roots3")
    wo_ok = sem("wo_scaled")
    eps_ok = sem("eps_ok")
    out_ps = sem("outputs_in_psum")
    resid = sem("residual_added")
    std = sem("deviations")
    QT = TT // NBK

    with nc.Block() as block:
        @block.sync
        def _(sp):
            sp.dma_start(x_tok[:, :, :], dram["x"].rearrange("b s d -> (b s) d")
                         .rearrange("(i p) d -> p i d", p=P)).then_inc(loaded, 16)
            sp.dma_start(Wo[:, :], dram["Wo"]).then_inc(loaded, 16)
            sp.dma_start(nw[:, :], dram["norm_w"].rearrange("(p o) -> p o", o=1)).then_inc(loaded, 16)

        @block.gpsimd
        def _(pool):
            pool.memset(eps[:, 0:1], RMS_EPS).then_inc(eps_ok, 1)
            pool.memset(eps[:, 1:2], LN_EPS).then_inc(eps_ok, 1)
            for n in range(NBK):
                for k in range(3):
                    if n:
                        pool.wait_ge(spread, 3 * n - 2 + k)
                    for i in range(QT):
                        d = pool.tensor_scalar(diag[:, k, i * P:(i + 1) * P], ident[:, :], pw[:, n * QT + i, k:k + 1],
                                               2.0 if k < 2 else 1.0, ALU.mult, ALU.mult)
                    d.then_inc(diag_ready, 1)

        @block.tensor
        def _(pe):
            for n in range(NBK):
                for k in range(3):
                    pe.wait_ge(diag_ready, 3 * n + k + 1)
                    if n >= 2:
                        pe.wait_ge(weighted, 3 * (n - 2) + k + 1)
                    pe.matmul(bank[3 * (n % 2) + k][:, :], ones[:, :], diag[:, k, :], start=True, stop=True).then_inc(spread, 1)
            pe.wait_ge(weighted, 3 * NBK)
            pe.wait_ge(wo_ok, 1)
            pe.wait_ge(summed, NBK)
            for i in range(TT):
                if i == 8:
                    pe.wait_ge(sq3, NBK)
                    for x in range(TT):
                        mm = pe.matmul(psQ[:, x:x + 1], keep[:, x * P:(x + 1) * P], ones[:, 0:1], start=True, stop=True)
                    mm.then_inc(ms, 1)
                if i >= 8 and i % 2 == 0:
                    pe.wait_ge(resid, i - 6)
                mm = pe.matmul(psO[i // 2 % 4][:, i % 2 * DM:(i % 2 + 1) * DM], on[:, i * P:(i + 1) * P], Wo[:, :],
                               start=True, stop=True)
                if i % 2:
                    mm.then_inc(out_ps, 1)

        @block.scalar
        def _(act):
            act.wait_ge(summed, NBK)
            for n in range(NBK):
                c = slice(n * BW, (n + 1) * BW)
                act.activation(keep[:, c], on[:, c], ACT.Square).then_inc(sq3, 1)
            act.wait_ge(eps_ok, 2)
            act.wait_ge(ms, 1)
            act.activation(inv[:, :], psQ[:, 0:TT], ACT.Sqrt, bias=eps[:, 0:1], scale=1.0 / P).then_inc(root, 1)
            act.wait_ge(std, 1)
            act.activation(mv[:, :, 1:2], mv[:, :, 1:2], ACT.Sqrt, bias=eps[:, 1:2]).then_inc(std, 1)
            act.wait_ge(shift_ok, 1)
            for i in [i for i in range(TT) if i in BY_ACT]:
                act.activation(x1[:, i, :], x1[:, i, :], ACT.Identity, scale=mv[:, i, 1:2], bias=shift[:, i, :])

        @block.vector
        def _(dve):
            own = 0

            def link(ins):
                nonlocal own
                own += 1
                ins.then_inc(own_d, 1)
                dve.wait_ge(own_d, own)

            turned = lambda x: x.rearrange("p (s b) -> p b s", b=NB)
            own_order = lambda x: x[:, :].rearrange("p (b s) -> p b s", s=NS)
            link(dve.tensor_scalar(own_order(gain), turned(S[:, 1, 1, :]), 0.7, 0.1, ALU.is_gt, ALU.mult))
            link(dve.tensor_scalar(keep[:, :], gain[:, :], -1.0, 1.0, ALU.mult, ALU.add))
            dve.memset(own_order(keep)[:, :, 0:1], 0.0)
            link(dve.tensor_tensor(own_order(gain), own_order(gain), turned(NU[:, :]), ALU.mult))
            link(dve.tensor_tensor_scan(neural[:, :], keep[:, :], gain[:, :], 0.0, ALU.mult, ALU.add))
            dve.wait_ge(loaded, 48)
            dve.tensor_scalar(Wo[:, :], Wo[:, :], nw[:, :], None, ALU.mult).then_inc(wo_ok, 1)
            steps = lambda x: x.rearrange("p (s b) -> p s b", b=NB)
            turn = lambda x, n: x[:, :].rearrange("p (b s) -> p s b", s=NS)[:, n * BW // NB:(n + 1) * BW // NB, :]
            def total(n):
                a, b, c = (m[:, n % 2, :] for m in mixed)
                dve.wait_ge(weighted, 3 * n + 3)
                link(dve.tensor_tensor(a, a, b, ALU.add))
                dve.tensor_tensor(turn(on, n), steps(a), steps(c), ALU.add).then_inc(summed, 1)
            for n in range(NBK):
                c = slice(n * BW, (n + 1) * BW)
                for k in range(3):
                    src = turn(neural, n) if k == 2 else steps(O[:, k, c])
                    dve.wait_ge(spread, 3 * n + k + 1)
                    dve.tensor_tensor(steps(mixed[k][:, n % 2, :]), src, steps(bank[3 * (n % 2) + k][:, :]), ALU.mult)\
                       .then_inc(weighted, 1)
                if n:
                    total(n - 1)
                if n:
                    dve.wait_ge(summed, n)
            total(NBK - 1)
            dve.wait_ge(root, 1)
            link(dve.reciprocal(inv[:, :], inv[:, :]))
            for i in range(TT + 2):
                if i < TT:
                    if i % 2 == 0:
                        dve.wait_ge(out_ps, i // 2 + 1)
                    dve.scalar_tensor_tensor(x1[:, i, :], psO[i // 2 % 4][:, i % 2 * DM:(i % 2 + 1) * DM], inv[:, i:i + 1],
                                             x_tok[:, i, :], ALU.mult, ALU.add).then_inc(resid, 1)
                if 1 <= i <= TT:
                    dve.wait_ge(resid, i)
                    dve.bn_stats(stats[:, i - 1, :], x1[:, i - 1, :]).then_inc(own_d, 1)
                if i >= 2:
                    dve.wait_ge(own_d, own + i - 1)
                    last = dve.bn_aggr(mv[:, i - 2, :], stats[:, i - 2, :])
            own += TT
            last.then_inc(std, 1)
            dve.wait_ge(std, 2)
            link(dve.reciprocal(mv[:, :, 1:2], mv[:, :, 1:2]))
            dve.scalar_tensor_tensor(shift[:, :, :], mv[:, :, 0:1], -1.0, mv[:, :, 1:2], ALU.mult, ALU.mult).then_inc(shift_ok, 1)
            for i in [i for i in range(TT) if i not in BY_ACT]:
                last = dve.tensor_scalar(x1[:, i, :], x1[:, i, :], mv[:, i, 0:1], mv[:, i, 1:2], ALU.subtract, ALU.mult)
            link(last)


def memory(nc, dram, x1, ident, ones):
    with ExitStack() as ctx:
        sb = lambda n, s: ctx.enter_context(nc.sbuf_tensor(n, s, F32))
        pr = {"ident": ident, "ones": ones,
              "KQ": sb("KQ", [P, 2, NT]),
              "W": sb("W", [P, 2, NT]),
              "S": sb("S", [P, 2, 2, NT]),
              "F4": sb("F4", [P, 2, NT]),
              "NU": sb("NU", [P, NT]), "O": sb("O", [P, 2, NT]), "pw": sb("pw", [P, TT, 3]),
              "A": x1[:, :, :].rearrange("p i d -> p (i d)").rearrange("p (m c) -> p m c", m=2)}
        with ExitStack() as c:
            memory_inputs(nc, c, pr, dram)
        with ExitStack() as c:
            recurrence(nc, c, pr)
        with ExitStack() as c:
            memory_output(nc, c, pr, dram, x1)


HEADS, HD = 8, 64
NKEY = DM


def cross_attention(nc, ctx, x1, dram, ident, preload):
    sb = lambda n, s: ctx.enter_context(nc.sbuf_tensor(n, s, F32))
    sem = lambda n: ctx.enter_context(nc.semaphore(n))
    r = lambda ap: ap.bitcast(F32R)
    TURN, COPY, ADD = 3, 3, 7
    Y_AT = (2, 3, 6, 7)
    S_RING = 2
    E_RING, T_RING = 8, 8
    WQ = sb("WQ", [P, 4, HD])
    WKV = sb("WKV", [P, 8, HD])
    WO = sb("WO", [HD, HEADS * HD])
    WOT = sb("WOT", [P, 4, HD])
    bout = sb("bout", [HD, 1])
    product_hi = sb("hi_m", [P, HEADS * HD])
    qk_parts = sb("MS", [P, HEADS, 2, HD])
    vo_parts = sb("NS_", [P, HEADS * HD])
    x_rows = sb("XX", [P, 2, NKEY])
    x_hi = sb("XH", [P, 2, NKEY])
    x_lo = sb("XL", [P, 2, NKEY])
    c_rows = sb("CC", [P, 2, NKEY])
    c_hi = sb("CHI", [P, 2, NKEY])
    c_lo = sb("CLO", [P, 2, NKEY])
    Y = sb("Y", [P, 2, HEADS, NKEY])
    Z = sb("Z", [P, 2, 2, HEADS * HD])
    expo = sb("E", [P, E_RING, 2, NKEY])
    attn_t = sb("AT", [P, T_RING, 2, NKEY])
    neg_max = sb("NM", [P, E_RING, 2])
    row_sum = sb("RS", [P, E_RING, 2])
    inv_sum = sb("RI", [P, E_RING, 2])
    ps = lambda n, w=BW: ctx.enter_context(nc.psum_tensor(n, [P, w], F32))
    psY = [ps("psY0"), ps("psY1"), ps("psY2")]
    psS = [ps(f"psS{i}x") for i in range(S_RING)]
    psA = [ps("psA0"), ps("psA1")]
    psU = ps("psU", NKEY)
    psM, psN = (psY[0], psS[1]), (psY[1], psY[2])

    w_in = sem("att_weights")
    wprep_pe = sem("att_products_in_psum")
    wprep = sem("att_weights_ready")
    wot_ready = sem("wout_turned")
    x_in = [sem("x_rows0"), sem("x_rows1")]
    c_in = [sem("ctx_rows0"), sem("ctx_rows1")]
    hi_ready = sem("hi_ready")
    lo_ready = sem("lo_ready")
    y_psum = sem("y_in_psum")
    y_hi = sem("y_hi")
    y_ready = sem("y_ready")
    z_psum = sem("z_in_psum")
    z_ready = sem("z_ready")
    sim_ready = sem("scores_in_psum")
    max_ready = sem("maxima_ready")
    exp_done = sem("exponentials_ready")
    ri_ready = sem("reciprocals_ready")
    norm_done = sem("attention_ready")
    t_psum = sem("attention_turned")
    at_act = sem("turned_by_act")
    at_dve = sem("turned_by_dve")
    av_done = sem("pairs_of_heads_added")
    out_read = sem("outputs_read")
    out_part = sem("outputs_half_read")

    DV = (2, 4, 7)
    by_dve = lambda hh: sum(1 for v in DV if v <= hh)
    ITER = NB // 2

    def at_wait(eng, it, k):
        q, hh = divmod(k, 8)
        if hh in DV:
            eng.wait_ge(at_dve, it * 2 * len(DV) + (q * len(DV) + by_dve(hh)))
        else:
            eng.wait_ge(at_act, it * 2 * (8 - len(DV)) + (q * (8 - len(DV)) + hh + 1 - by_dve(hh)))

    def rows(x, b2):
        return x[64 * b2:64 * b2 + 64]

    with nc.Block() as block:
        def run(eng, slot, tail):
            for k in range(16):
                slot(0, k, True, False)
            with eng.Fori(1, ITER - 1) as it:
                for k in range(16):
                    slot(it, k, False, False)
            for k in range(16):
                slot(ITER - 1, k, False, True)
            for k in range(16, 16 + tail):
                slot(ITER - 1, k, False, True)

        @block.sync
        def _(sp):
            sp.dma_start(WQ[:, :, :], dram["Wq"].rearrange("(c p) k -> p c k", p=P)).then_inc(w_in, 16)
            sp.dma_start(WKV[:, :, :], dram["Wkv"].rearrange("(c p) k -> p c k", p=P)).then_inc(w_in, 16)
            sp.dma_start(WO[:, :], dram["Wout"]).then_inc(w_in, 16)
            sp.dma_start(bout[:, :], dram["bout"].rearrange("(p o) -> p o", o=1)).then_inc(w_in, 16)

            def load(it, q, wait):
                if wait:
                    sp.wait_ge(lo_ready, it * 2 + (q - 1))
                for half in range(2):
                    sp.dma_start(rows(x_rows, half)[:, q, :], rows(x1, q)[:, bass.ds(it, 1), :]
                                 .rearrange("p i d -> p (i d)")).then_inc(x_in[q], 16)
                    sp.dma_start(rows(c_rows, half)[:, q, :], dram["ctx"][bass.ds(it * 2 + q, 1), :, :]
                                 .rearrange("b s d -> (b s) d")).then_inc(c_in[q], 16)
            load(0, 0, False)
            load(0, 1, False)
            preload(sp)
            with sp.Fori(1, ITER) as it:
                load(it, 0, True)
                load(it, 1, True)

        @block.tensor
        def _(pe):
            pe.wait_ge(w_in, 64)
            for i in range(4):
                mm = pe.transpose(psS[0][:, i * HD:(i + 1) * HD], WO[:, i * P:(i + 1) * P], ident[0:HD, 0:HD])
            mm.then_inc(wprep_pe, 1)
            for half in range(2):
                for h in range(HEADS):
                    a = rows(WQ, h % 2)[:, h // 2, :]
                    mm = pe.matmul(rows(psM[h % 2], half)[:, h // 2 * HD:(h // 2 + 1) * HD], a, rows(WKV, h % 2)[:, h // 2, :],
                                   start=True, stop=True)
            mm.then_inc(wprep_pe, 1)
            pe.wait_ge(wot_ready, 1)
            for half in range(2):
                for h in range(HEADS):
                    mm = pe.matmul(rows(psN[h % 2], half)[:, h // 2 * HD:(h // 2 + 1) * HD], rows(WKV, h % 2)[:, 4 + h // 2, :],
                                   rows(WOT, h % 2)[:, h // 2, :], start=True, stop=True)
            mm.then_inc(wprep_pe, 1)
            pe.wait_ge(wprep, 14)

            def y_piece(it, q, p, wait):
                if p == 0:
                    pe.wait_ge(hi_ready, it * 4 + (2 * q + 2))
                    pe.wait_ge(lo_ready, it * 2 + (q + 1))
                if p == 0 and wait:
                    pe.wait_ge(y_ready, it * 8 + 4 * q)
                elif p in (1, 2) and wait:
                    pe.wait_ge(z_ready, it * 4 + (2 * q - 2 + p))
                elif p == 3:
                    pe.wait_ge(y_ready, it * 8 + (4 * q + 1))
                for d in range(2):
                    for n, x in enumerate((x_hi, x_lo)):
                        mm = pe.matmul(psY[(2 + p) % 3][:, d * NKEY:(d + 1) * NKEY],
                                       r(qk_parts[:, 2 * p + d, :, :].rearrange("p a c -> p (a c)")), r(x[:, q, :]),
                                       start=n == 0, stop=n == 1)
                mm.then_inc(y_psum, 1)

            def slot(it, k, first, last):
                q, hh = divmod(k, 8)
                if k < 16:
                    pe.wait_ge(y_ready, it * 8 + (4 * q + hh // 2 + 1))
                    if not first or k >= S_RING:
                        pe.wait_ge(exp_done, it * 16 + (k - S_RING + 1))
                    for ib in range(2):
                        for n, c in enumerate((c_hi, c_lo)):
                            mm = pe.matmul(psS[k % S_RING][:, ib * NKEY:(ib + 1) * NKEY],
                                           r(Y[:, q, hh, ib * P:(ib + 1) * P]), r(c[:, q, :]), start=n == 0, stop=n == 1)
                    mm.then_inc(sim_ready, 1)
                    if hh in (0, 1):
                        pe.wait_ge(y_ready, it * 8 + (4 * q + 2 + hh))
                        for n, c in enumerate((c_hi, c_lo)):
                            mm = pe.matmul(psY[hh][:, :], r(c[:, q, hh * P:(hh + 1) * P]), r(vo_parts[:, :]),
                                           start=n == 0, stop=n == 1)
                        mm.then_inc(z_psum, 1)
                    if hh in Y_AT and not (last and q == 1):
                        y_piece(it + q, 1 - q, Y_AT.index(hh), True)
                t = k - TURN
                if (not first or t >= 0) and t < 16:
                    pe.wait_ge(norm_done, it * 16 + (t + 1))
                    if not first or t >= 2:
                        at_wait(pe, it, t - 2)
                    for jb in range(2):
                        for ib in range(2):
                            mm = pe.transpose(psA[t % 2][:, jb * NKEY + ib * P:jb * NKEY + (ib + 1) * P],
                                              expo[:, t % E_RING, ib, jb * P:(jb + 1) * P], ident[:, :])
                    mm.then_inc(t_psum, 1)
                a = k - ADD
                if a % 2 == 0 and (not first or a >= 0) and a < 16:
                    at_wait(pe, it, a)
                    at_wait(pe, it, a + 1)
                    qa, ha = divmod(a, 8)
                    pe.wait_ge(z_ready, it * 4 + (2 * qa + 2))
                    if ha == 0 and (not first or qa >= 1):
                        pe.wait_ge(out_read, it * 2 + qa)
                    for jb in range(2):
                        for d in range(2):
                            h = ha + d
                            mm = pe.matmul(rows(psU, d)[:, :], Z[:, qa % 2, jb, h * HD:(h + 1) * HD],
                                           attn_t[:, (a + d) % T_RING, jb, :],
                                           start=ha == 0 and jb == 0, stop=ha == 6 and jb == 1)
                    mm.then_inc(av_done, 1)

            for p in range(4):
                y_piece(0, 0, p, False)
            run(pe, slot, ADD)

        def turn_out(eng, it, t, engine_sem, copy):
            eng.wait_ge(t_psum, it * 16 + (t + 1))
            copy(attn_t[:, t % T_RING, :, :].rearrange("p j i -> p (j i)"), psA[t % 2][:, :]).then_inc(engine_sem, 1)

        @block.scalar
        def _(act):
            act.wait_ge(wprep_pe, 1)
            act.activation(WOT[:, :, :].rearrange("p i o -> p (i o)"), psS[0][:, 0:4 * HD], ACT.Copy).then_inc(wot_ready, 1)

            def split_hi(it, q, wait):
                act.wait_ge(x_in[q], it * 32 + 32)
                act.wait_ge(c_in[q], it * 32 + 32)
                if wait:
                    act.wait_ge(y_psum, it * 8 + (4 * q - 4))
                    act.wait_ge(sim_ready, it * 16 + (8 * q - 8))
                act.activation(r(x_hi[:, q, :]), x_rows[:, q, :], ACT.Copy).then_inc(hi_ready, 1)
                act.activation(r(c_hi[:, q, :]), c_rows[:, q, :], ACT.Copy).then_inc(hi_ready, 1)

            def y_high(it, q, p, wait):
                act.wait_ge(y_psum, it * 8 + (4 * q + p + 1))
                if p == 0 and wait:
                    act.wait_ge(sim_ready, it * 16 + (8 * q - 8))
                act.activation(r(Y[:, q, 2 * p:2 * p + 2, :].rearrange("p h n -> p (h n)")), psY[(2 + p) % 3][:, :],
                               ACT.Copy).then_inc(y_hi, 1)

            def slot(it, k, first, last):
                q, hh = divmod(k, 8)
                if k < 16:
                    if hh == 0 and not (last and q == 1):
                        split_hi(it + q, 1 - q, not (first and q == 0))
                    if hh in (1, 2):
                        jb = hh - 1
                        act.wait_ge(z_psum, it * 4 + (2 * q + jb + 1))
                        if jb == 0 and (not first):
                            act.wait_ge(av_done, it * 8 + (4 * q - 4))
                        act.activation(Z[:, q, jb, :], psY[jb][:, :], ACT.Copy).then_inc(z_ready, 1)
                    if hh - 1 in Y_AT and not (last and q == 1):
                        y_high(it + q, 1 - q, Y_AT.index(hh - 1), not (first and q == 0))
                    if hh == 0 and not (first and q == 0):
                        y_high(it, q, 3, True)
                    act.wait_ge(max_ready, it * 16 + (k + 1))
                    if not first or k >= E_RING:
                        act.wait_ge(t_psum, it * 16 + (k - E_RING + 1))
                    for ib in range(2):
                        ex = act.activation(expo[:, k % E_RING, ib, :], psS[k % S_RING][:, ib * NKEY:(ib + 1) * NKEY], ACT.Exp,
                                            bias=neg_max[:, k % E_RING, ib:ib + 1], accum_out=row_sum[:, k % E_RING, ib:ib + 1])
                    ex.then_inc(exp_done, 1)
                t = k - COPY
                if (not first or t >= 0) and t < 16 and t % 8 not in DV:
                    if not first or t >= T_RING:
                        act.wait_ge(av_done, it * 8 + (t - T_RING) // 2 + 1)
                    turn_out(act, it, t, at_act, lambda o, i: act.activation(o, i, ACT.Copy))

            split_hi(0, 0, False)
            for p in range(4):
                y_high(0, 0, p, False)
            run(act, slot, COPY)

        @block.gpsimd
        def _(pool):
            def slot(it, k, first, last):
                pool.wait_ge(ri_ready, it * 16 + (k + 1))
                pool.tensor_tensor(expo[:, k % E_RING, :, :], expo[:, k % E_RING, :, :],
                                   inv_sum[:, k % E_RING, :].unsqueeze(2).broadcast_to((P, 2, NKEY)), ALU.mult)\
                    .then_inc(norm_done, 1)
            run(pool, slot, 0)

        @block.vector
        def _(dve):
            dve.wait_ge(w_in, 64)
            dve.wait_ge(wprep_pe, 2)
            heads = lambda x, e: x.rearrange("p (h e c) -> p h e c", e=2, c=HD)[:, :, e, :]
            half = lambda x: x[:, 0:4 * HD].rearrange("p (h c) -> p h c", c=HD)
            for e in range(2):
                dve.tensor_copy(r(heads(product_hi[:, :], e)), half(psM[e][:, :])).then_inc(wprep, 1)
            dve.wait_ge(wprep, 2)
            for e in range(2):
                for d in range(2):
                    dve.tensor_copy(r(qk_parts[0:HD, e:HEADS:2, d, :]), heads(product_hi[0:HD, :], e)).then_inc(wprep, 1)
                    dve.tensor_tensor(r(qk_parts[HD:P, e:HEADS:2, d, :]), half(psM[e][HD:P, :]), heads(product_hi[HD:P, :], e),
                                      ALU.subtract).then_inc(wprep, 1)
            dve.wait_ge(wprep_pe, 3)
            for e in range(2):
                dve.tensor_copy(r(heads(vo_parts[:, :], e)), half(psN[e][:, :])).then_inc(wprep, 1)
            dve.wait_ge(wprep, 12)
            for e in range(2):
                lo = heads(vo_parts[HD:P, :], e)
                dve.tensor_tensor(r(lo), half(psN[e][HD:P, :]), lo, ALU.subtract).then_inc(wprep, 1)

            def split_lo(it, q, wait):
                dve.wait_ge(hi_ready, it * 4 + (2 * q + 2))
                dve.tensor_tensor(r(x_lo[:, q, :]), x_rows[:, q, :], x_hi[:, q, :], ALU.subtract)
                dve.tensor_tensor(r(c_lo[:, q, :]), c_rows[:, q, :], c_hi[:, q, :], ALU.subtract).then_inc(lo_ready, 1)

            def y_low(it, q, p):
                dve.wait_ge(y_hi, it * 8 + (4 * q + p + 1))
                y = Y[HD:P, q, 2 * p:2 * p + 2, :].rearrange("p h n -> p (h n)")
                dve.tensor_tensor(r(y), psY[(2 + p) % 3][HD:P, :], y, ALU.subtract).then_inc(y_ready, 1)

            def slot(it, k, first, last):
                q, hh = divmod(k, 8)
                if k < 16:
                    dve.wait_ge(sim_ready, it * 16 + (k + 1))
                    dve.tensor_reduce(neg_max[:, k % E_RING, :], psS[k % S_RING][:, :].rearrange("p (i j) -> p i j", i=2), AX.X,
                                      ALU.max, negate=True).then_inc(max_ready, 1)
                    if hh - 1 in Y_AT and not (last and q == 1):
                        y_low(it + q, 1 - q, Y_AT.index(hh - 1))
                    if hh == 0 and not (first and q == 0):
                        y_low(it, q, 3)
                t = k - 1
                if (not first or t >= 0) and t < 16:
                    dve.wait_ge(exp_done, it * 16 + (t + 1))
                    dve.reciprocal(inv_sum[:, t % E_RING, :], row_sum[:, t % E_RING, :]).then_inc(ri_ready, 1)
                a = k - (ADD + 7)
                if a in (0, 8) or (a in (-8, -16) and not first):
                    qb = a // 8
                    dve.wait_ge(av_done, it * 8 + (4 * qb + 4))
                    i = it if qb >= 0 else it - 1
                    xr = rows(x1, qb % 2)[:, bass.ds(i, 1), :].rearrange("p i d -> p (i d)")
                    dve.scalar_tensor_tensor(xr, psU[0:HD, :], bout[:, :], xr, ALU.add, ALU.add)\
                       .then_inc(out_part, 1)
                    dve.wait_ge(out_part, it * 2 + (qb + 1))
                    dve.tensor_tensor(xr, xr, psU[HD:P, :], ALU.add).then_inc(out_read, 1)
                if k < 16:
                    if hh == 1 and not (last and q == 1):
                        split_lo(it + q, 1 - q, True)
                t = k - COPY
                if (not first or t >= 0) and t < 16 and t % 8 in DV:
                    if not first or t >= T_RING:
                        dve.wait_ge(av_done, it * 8 + (t - T_RING) // 2 + 1)
                    turn_out(dve, it, t, at_dve, dve.tensor_copy)
            split_lo(0, 0, False)
            for p in range(4):
                y_low(0, 0, p)
            run(dve, slot, ADD + 1)


def layernorm(nc, ctx, x, name, store=None):
    sb = lambda n, s: ctx.enter_context(nc.sbuf_tensor(name + n, s, F32))
    sem = lambda n: ctx.enter_context(nc.semaphore(name + n))
    stats = sb("stats", [P, TT, 6])
    mv = sb("mv", [P, TT, 2])
    shift = sb("shift", [P, TT, 1])
    eps = sb("eps", [P, 1])
    own_d, std, ready, shift_ok = sem("own"), sem("std"), sem("eps_ready"), sem("shift_ready")
    done = {"act": sem("tiles_by_act"), "dve": sem("tiles_by_dve")}
    stored = sem("stored")
    by = ["act" if i % 8 in (1, 4, 6) else "dve" for i in range(TT)]
    with nc.Block() as block:
        @block.gpsimd
        def _(pool):
            pool.memset(eps[:, :], LN_EPS).then_inc(ready, 1)

        @block.scalar
        def _(act):
            act.wait_ge(ready, 1)
            act.wait_ge(std, 1)
            act.activation(mv[:, :, 1:2], mv[:, :, 1:2], ACT.Sqrt, bias=eps[:, :]).then_inc(std, 1)
            act.wait_ge(shift_ok, 1)
            for i in [i for i in range(TT) if by[i] == "act"]:
                act.activation(x[:, i, :], x[:, i, :], ACT.Identity, scale=mv[:, i, 1:2], bias=shift[:, i, :])\
                   .then_inc(done["act"], 1)

        @block.vector
        def _(dve):
            for i in range(TT + 1):
                if i < TT:
                    dve.bn_stats(stats[:, i, :], x[:, i, :]).then_inc(own_d, 1)
                if i:
                    dve.wait_ge(own_d, i)
                    ag = dve.bn_aggr(mv[:, i - 1, :], stats[:, i - 1, :])
            ag.then_inc(std, 1)
            dve.wait_ge(std, 2)
            dve.reciprocal(mv[:, :, 1:2], mv[:, :, 1:2]).then_inc(own_d, 1)
            dve.wait_ge(own_d, TT + 1)
            dve.scalar_tensor_tensor(shift[:, :, :], mv[:, :, 0:1], -1.0, mv[:, :, 1:2], ALU.mult, ALU.mult).then_inc(shift_ok, 1)
            for i in [i for i in range(TT) if by[i] == "dve"]:
                dve.tensor_scalar(x[:, i, :], x[:, i, :], mv[:, i, 0:1], mv[:, i, 1:2], ALU.subtract, ALU.mult)\
                   .then_inc(done["dve"], 1)

        @block.sync
        def _(sp):
            if store is not None:
                for i in range(0, TT, 4):
                    for e in done:
                        sp.wait_ge(done[e], by[:i + 4].count(e))
                    sp.dma_start(store[:, i:i + 4, :], x[:, i:i + 4, :]).then_inc(stored, 16)
                sp.wait_ge(stored, 16 * TT // 4)


NE, TOPK, CAP, HE, HSH = 64, 6, 128, 32, 64
EC = P // HE
NC = NE // EC
TB = BW
NTB = NT // TB


def expert_weights(nc, ctx):
    return {"down": ctx.enter_context(nc.sbuf_tensor("down", [P, NC, DM], F32)),
            "in": ctx.enter_context(nc.semaphore("expert_weights_in"))}


def load_expert_weights(sp, ew, dram):
    sp.dma_start(ew["down"][:, :, :], dram["w_down"].rearrange("e h c -> (e h) c").rearrange("(n p) c -> p n c", p=P))\
      .then_inc(ew["in"], 16)


def experts(nc, ctx, x2, ew, dram, ident):
    sb = lambda n, s: ctx.enter_context(nc.sbuf_tensor(n, s, F32))
    sem = lambda n: ctx.enter_context(nc.semaphore(n))
    r = lambda ap: ap.bitcast(F32R)
    RAW, PIECES = 4, 4 * KD
    up_h = sb("UH", [P, KD, 2, NE * HE])
    up_l = sb("UL", [P, KD, 2, NE * HE])
    xT_h = sb("XTH", [P, KD, NT])
    xT_l = sb("XTL", [P, KD, NT])
    weight_rows = sb("WTT", [P, NT])
    sh_up = sb("sh_up", [P, KD, 2 * HSH])
    sh_h = sb("sh_h", [P, KD, 2 * HSH])
    sh_l = sb("sh_l", [P, KD, 2 * HSH])
    sh_dn = sb("sh_dn", [HSH, DM])
    gate = sb("gate", [P, KD, NE])
    spreader = sb("spread", [P, NC, P])
    sp_ok = sem("spread_ready")
    small = ctx.enter_context(ExitStack())
    sbs = lambda n, s: small.enter_context(nc.sbuf_tensor(n, s, F32))
    scores_ = sbs("sc", [P, TT, NE])
    top8 = sbs("top", [P, TT, 8])
    chosen = sbs("gt", [P, TT, NE])
    ties_ranks = sbs("er", [P, 2 * TT * NE])
    ties, tie_rank = (ties_ranks[:, i * TT * NE:(i + 1) * TT * NE].rearrange("p (t e) -> p t e", e=NE) for i in range(2))
    weight_parts = ties_ranks[:, :].rearrange("p (t a e) -> p t a e", a=2, e=NE)
    not_first = sbs("seg", [P, TT, NE])
    n_above = sbs("cnt", [P, TT, 1])
    sum_inv = sbs("rcp", [P, TT, 1])
    n_ahead = sbs("car", [P, TT, NE])
    tri_ones = sbs("tri", [P, P])
    raw = sbs("up_raw", [P, RAW, NE // 4, 2 * HE])
    all_ones = sbs("on1", [P, P])

    psum_bank = lambda n: ctx.enter_context(nc.psum_tensor(n, [P, BW], F32))
    banks = [psum_bank(f"e{i}") for i in range(8)]

    loaded = sem("gate_in")
    consts = sem("route_consts")
    xt_ps = sem("x2_turned")
    xt_hi = sem("x2_hi")
    xt_lo = sem("x2_lo")
    logit = sem("logits_in_psum")
    score = sem("scores_ready")
    own_d = sem("dve_own5")
    sel_ok = sem("selection_ready")
    counts = sem("counts_in_psum")
    weights_ok = sem("routing_weights_ready")
    wt_ps = sem("routing_weights_turned")
    wt_ok = sem("routing_rows_ready")
    up_hi = sem("up_hi")
    up_lo = sem("up_lo")
    rcp_ok = sem("score_sums_inverted")
    normal = sem("scores_normal")
    sh_hi = sem("shared_hi")
    NT8 = KD * NBK
    raw_in = [sem(f"up_raw_in{i}") for i in range(RAW)]

    def raw_part(x, v):
        k, q = divmod(x, 4)
        n = NE // 4
        part = lambda u: r(u[:, k, v, q * n * HE:(q + 1) * n * HE].rearrange("p (e h) -> p e h", h=HE))
        return raw[:, x % RAW, :, v * HE:(v + 1) * HE], part

    with nc.Block() as block:
        @block.sync
        def _(sp):
            sp.dma_start(gate[:, :, :], dram["w_gate"].rearrange("(k p) e -> p k e", p=P)).then_inc(loaded, 16)
            sp.dma_start(sh_up[:, :, :], dram["w_shared_up"].rearrange("(k p) e -> p k e", p=P)).then_inc(loaded, 16)
            sp.dma_start(sh_dn[:, :], dram["w_shared_down"]).then_inc(loaded, 16)
            for x in range(PIECES):
                k, q = divmod(x, 4)
                if x >= RAW:
                    sp.wait_ge(up_lo, 2 * (x - RAW + 1))
                sp.dma_start(raw[:, x % RAW, :, :], dram["w_up"][q * NE // 4:(q + 1) * NE // 4, k * P:(k + 1) * P, :]
                             .rearrange("e p h -> p e h")).then_inc(raw_in[x % RAW], 16)

        @block.gpsimd
        def _(pool):
            pool.memset(tri_ones[:, :], 1.0).then_inc(consts, 1)
            pool.memset(not_first[:, :, :], 1.0).then_inc(consts, 1)
            pool.memset(all_ones[:, :], 1.0).then_inc(consts, 1)
            pool.wait_ge(consts, 3)
            pool.affine_select(out=r(tri_ones[:, :]), in_=tri_ones[:, :], compare_op=ALU.is_gt, fill=0.0, base=0,
                               pattern=[[1, P]], channel_multiplier=-1).then_inc(consts, 1)
            pool.memset(not_first[:, :, 0:1], 0.0).then_inc(consts, 1)
            pool.wait_ge(consts, 5)
            pool.memset(spreader[:, :, :], 0.0).then_inc(sp_ok, 1)
            for n, base in enumerate((0, -NE)):
                pool.wait_ge(sp_ok, n + 1)
                v = spreader[:, :, :].rearrange("p c (e h) -> p c e h", h=HE)
                pool.affine_select(out=r(v), in_=v, compare_op=ALU.not_equal, fill=1.0, base=base,
                                   pattern=[[-EC, NC], [-1, EC], [0, HE]], channel_multiplier=1).then_inc(sp_ok, 1)
            pool.wait_ge(sp_ok, 3)
            for x in range(PIECES):
                for v in range(2):
                    src, part = raw_part(x, v)
                    pool.wait_ge(up_hi, 2 * x + v + 1)
                    pool.tensor_tensor(part(up_l), src, part(up_h).bitcast(F32), ALU.subtract).then_inc(up_lo, 1)
            pool.wait_ge(up_lo, 2 * PIECES)
            pool.wait_ge(sel_ok, 1)
            pool.tensor_tensor(scores_[:, :, :], scores_[:, :, :], chosen[:, :, :], ALU.mult).then_inc(normal, 1)
            pool.wait_ge(rcp_ok, 1)
            pool.wait_ge(normal, 1)
            pool.tensor_tensor(scores_[:, :, :], scores_[:, :, :], sum_inv[:, :, :].broadcast_to((P, TT, NE)), ALU.mult)\
                .then_inc(normal, 1)

        @block.tensor
        def _(pe):
            pe.wait_ge(consts, 5)
            for j in range(NT8):
                k, n = divmod(j, NBK)
                if j >= 4:
                    pe.wait_ge(xt_lo, j - 3)
                for i in range(4):
                    mm = pe.transpose(banks[j % 4][:, i * P:(i + 1) * P], x2[:, 4 * n + i, k * P:(k + 1) * P], ident[:, :])
                mm.then_inc(xt_ps, 1)
            pe.wait_ge(xt_lo, NT8)
            pe.wait_ge(loaded, 48)
            for i in range(TT):
                for n, (k, x) in enumerate([(k, x) for k in range(KD) for x in (xT_h, xT_l)]):
                    mm = pe.matmul(banks[4 + i // 8][:, i % 8 * NE:(i % 8 + 1) * NE], x[:, k, i * P:(i + 1) * P],
                                   gate[:, k, :], start=n == 0, stop=n == 2 * KD - 1)
            mm.then_inc(logit, 1)
            pe.wait_ge(sel_ok, 1)
            flat = chosen[:, :, :].rearrange("p i e -> p (i e)")
            for m, a in enumerate((tri_ones, all_ones)):
                for n in range(2):
                    mm = pe.matmul(banks[2 * m + n][:, :], r(a[:, :]), r(flat[:, n * BW:(n + 1) * BW]), start=True, stop=True)
            mm.then_inc(counts, 1)
            pe.wait_ge(weights_ok, 1)
            for i in range(TT):
                mm = pe.transpose(banks[4 + i // 4][:, i % 4 * P:(i % 4 + 1) * P],
                                  weight_parts[:, i, :, :].rearrange("p a e -> p (a e)"), ident[:, :])
                if i % 4 == 3:
                    mm.then_inc(wt_ps, 1)

        @block.scalar
        def _(act):
            for j in range(NT8):
                k, n = divmod(j, NBK)
                act.wait_ge(xt_ps, j + 1)
                act.activation(r(xT_h[:, k, n * BW:(n + 1) * BW]), banks[j % 4][:, :], ACT.Copy).then_inc(xt_hi, 1)
            for x in range(PIECES):
                if x == RAW:
                    act.wait_ge(logit, 1)
                    for n in range(2):
                        act.activation(scores_[:, 8 * n:8 * n + 8, :].rearrange("p i e -> p (i e)"), banks[4 + n][:, :],
                                       ACT.Sigmoid).then_inc(score, 1)
                act.wait_ge(raw_in[x % RAW], 16 * (x // RAW + 1))
                for v in range(2):
                    src, part = raw_part(x, v)
                    act.activation(part(up_h), src, ACT.Copy).then_inc(up_hi, 1)
            act.wait_ge(loaded, 48)
            act.activation(r(sh_h[:, :, :]), sh_up[:, :, :], ACT.Copy).then_inc(sh_hi, 1)
        @block.vector
        def _(dve):
            own = 0

            def link(ins):
                nonlocal own
                own += 1
                ins.then_inc(own_d, 1)
                dve.wait_ge(own_d, own)

            for j in range(NT8):
                k, n = divmod(j, NBK)
                dve.wait_ge(xt_hi, j + 1)
                c = slice(n * BW, (n + 1) * BW)
                dve.tensor_tensor(r(xT_l[:, k, c]), banks[j % 4][:, :], xT_h[:, k, c], ALU.subtract).then_inc(xt_lo, 1)
            dve.wait_ge(score, 2)
            for i in range(TT):
                mx = dve.max(top8[:, i, :], scores_[:, i, :])
            link(mx)
            edge = top8[:, :, TOPK - 1:TOPK].broadcast_to((P, TT, NE))
            dve.tensor_tensor(r(chosen[:, :, :]), scores_[:, :, :], edge, ALU.is_gt)
            dve.tensor_reduce(sum_inv[:, :, :], top8[:, :, 0:TOPK], AX.X, ALU.add)
            link(dve.tensor_tensor(ties[:, :, :], scores_[:, :, :], edge, ALU.is_equal))
            flat = lambda x: x[:, :, :].rearrange("p i e -> p (i e)")
            dve.wait_ge(consts, 5)
            dve.tensor_tensor_scan(flat(tie_rank), flat(not_first), flat(ties), 0.0, ALU.mult, ALU.add)
            link(dve.tensor_reduce(n_above[:, :, 0:1], chosen[:, :, :], AX.X, ALU.add))
            link(dve.tensor_tensor(tie_rank[:, :, :], tie_rank[:, :, :], n_above[:, :, 0:1].broadcast_to((P, TT, NE)), ALU.add))
            link(dve.scalar_tensor_tensor(flat(ties), flat(tie_rank), float(TOPK), flat(ties), ALU.is_le, ALU.mult))
            dve.tensor_tensor(r(chosen[:, :, :]), chosen[:, :, :], ties[:, :, :], ALU.add).then_inc(sel_ok, 1)
            dve.wait_ge(sel_ok, 1)
            dve.reciprocal(sum_inv[:, :, :], sum_inv[:, :, :]).then_inc(rcp_ok, 1)
            dve.wait_ge(counts, 1)
            link(dve.memset(n_ahead[:, 0, :], 0.0))
            for i in range(1, TT):
                link(dve.tensor_tensor(n_ahead[:, i, :], n_ahead[:, i - 1, :],
                                       banks[2 + (i - 1) // 8][:, (i - 1) % 8 * NE:((i - 1) % 8 + 1) * NE], ALU.add))
            for n in range(2):
                c = n_ahead[:, 8 * n:8 * n + 8, :].rearrange("p i e -> p (i e)")
                last = dve.tensor_tensor(c, c, banks[n][:, :], ALU.add)
            link(last)
            dve.wait_ge(normal, 2)
            link(dve.scalar_tensor_tensor(flat(scores_), flat(n_ahead), float(CAP), flat(scores_), ALU.is_lt, ALU.mult))
            link(dve.tensor_copy(r(weight_parts[:, :, 0, :]), scores_[:, :, :]))
            dve.tensor_tensor(r(weight_parts[:, :, 1, :]), scores_[:, :, :], weight_parts[:, :, 0, :], ALU.subtract)\
                .then_inc(weights_ok, 1)
            for n in range(4):
                dve.wait_ge(wt_ps, n + 1)
                dve.tensor_copy(r(weight_rows[:, n * BW:(n + 1) * BW]), banks[4 + n][:, :]).then_inc(wt_ok, 1)
            dve.wait_ge(sh_hi, 1)
            link(dve.tensor_tensor(r(sh_l[:, :, :]), sh_up[:, :, :], sh_h[:, :, :], ALU.subtract))
    small.close()

    silu = sb("SG", [P, 2, TB])
    hidden = sb("HT", [P, 2, TB])
    hid_h = sb("HH", [P, 3, TB])
    hid_l = sb("HL", [P, 3, TB])
    N1 = NC + 1
    second = sb("down_parts", [P, 2, N1, DM])
    down_part = lambda a, c: second[0:rows(c), a, c, :]
    dh_ok = sem("down_hi_ready")
    dl_ok = sem("down_lo_ready")
    g_ps = sem("gates_in_psum")
    v_ps = sem("values_in_psum")
    w_ps = sem("weights_in_psum")
    sg_ok = sem("silu_ready")
    product_ok = sem("hidden_unweighted")
    weighted_ok = sem("hidden_weighted")
    h_hi = sem("hidden_hi")
    h_ok = sem("hidden_ready")
    added = sem("chunks_added")
    o_read = sem("block_outputs_read")
    rows = lambda c: P if c < NC else HSH

    def before(c, ring=2, n=N1):
        return c - ring if c >= ring else max(x for x in range(n) if x % ring == c % ring) - n

    def blocks(eng, body):
        body(0, True, False)
        with eng.Fori(1, NTB - 1) as tb:
            body(tb, False, False)
        body(NTB - 1, False, True)

    with nc.Block() as block:
        @block.gpsimd
        def _(pool):
            pool.wait_ge(ew["in"], 16)
            for c in range(N1):
                src = ew["down"][:, c, :] if c < NC else sh_dn[:, :]
                pool.tensor_copy(r(down_part(0, c)), src).then_inc(dh_ok, 1)
                pool.wait_ge(dh_ok, c + 1)
                pool.tensor_tensor(r(down_part(1, c)), src, down_part(0, c), ALU.subtract).then_inc(dl_ok, 1)

        @block.tensor
        def _(pe):
            def up(tb, c, first):
                tok = bass.ds(tb * TB, TB)
                rhs = [x[:, k, tok] for k in range(KD) for x in (xT_h, xT_h, xT_l)]
                for v, s in ((0, g_ps), (1, v_ps)) if c < NC else ((0, g_ps),):
                    if not first or c >= 2:
                        pe.wait_ge((sg_ok, product_ok)[v or c == 0], tb * N1 + (before(c) + 1))
                    if c < NC:
                        lhs = [x[:, k, v, c * P:(c + 1) * P] for k in range(KD) for x in (up_h, up_l, up_h)]
                    else:
                        lhs = [x[:, k, :] for k in range(KD) for x in (sh_h, sh_l, sh_h)]
                    for n, (a, b) in enumerate(zip(lhs, rhs)):
                        mm = pe.matmul(banks[2 * (c % 2) + v][:, :], r(a), r(b), start=n == 0, stop=n == 3 * KD - 1)
                    mm.then_inc(s, 1)
                if c < NC:
                    if not first or c >= 2:
                        pe.wait_ge(weighted_ok, tb * NC + (before(c, 2, NC) + 1))
                    pe.matmul(banks[4 + c % 2][:, :], r(spreader[:, c, :]), r(weight_rows[:, tok]), start=True, stop=True)\
                      .then_inc(w_ps, 1)

            def down(tb, c, first):
                if first:
                    pe.wait_ge(dl_ok, c + 1)
                pe.wait_ge(h_ok, tb * N1 + (c + 1))
                if c == 0 and not first:
                    pe.wait_ge(o_read, tb)
                for i in range(TB // P):
                    for n, (h, w) in enumerate(((hid_h, 0), (hid_l, 0), (hid_h, 1))):
                        mm = pe.matmul(banks[6 + i // 2][:, i % 2 * DM:(i % 2 + 1) * DM],
                                       r(h[0:rows(c), c % 3, i * P:(i + 1) * P]), r(down_part(w, c)),
                                       start=c == 0 and n == 0 and i % 2 == 0, stop=c == NC and n == 2 and i % 2 == 1)
                mm.then_inc(added, 1)

            up(0, 0, True)
            up(0, 1, True)

            def body(tb, first, last):
                for c in range(N1):
                    if c + 2 < N1:
                        up(tb, c + 2, first)
                    elif not last:
                        up(tb + 1, c + 2 - N1, False)
                    down(tb, c, first)
            blocks(pe, body)

        @block.scalar
        def _(act):
            def high(tb, c, first):
                k = c % N1
                if k < NC:
                    act.wait_ge(weighted_ok, tb * NC + (c + 1))
                else:
                    act.wait_ge(product_ok, tb * N1 + (c + 1))
                if not first or c >= 3:
                    act.wait_ge(added, tb * N1 + ((before(k, 3) if c >= 0 else c - 3) + 1))
                act.activation(r(hid_h[0:rows(k), k % 3, :]), hidden[0:rows(k), k % 2, :], ACT.Copy).then_inc(h_hi, 1)

            def body(tb, first, last):
                for c in range(N1):
                    if c == 0 and not first:
                        high(tb, -1, False)
                    act.wait_ge(g_ps, tb * N1 + (c + 1))
                    if not first or c >= 2:
                        act.wait_ge(product_ok, tb * N1 + (before(c) + 1))
                    act.activation(silu[0:rows(c), c % 2, :], banks[2 * (c % 2)][P - rows(c):P, :], ACT.Silu).then_inc(sg_ok, 1)
                    if c:
                        high(tb, c - 1, first)
                if last:
                    high(tb, NC, False)
            blocks(act, body)

        @block.vector
        def _(dve):
            def low(tb, c):
                k = c % N1
                dve.wait_ge(h_hi, tb * N1 + (c + 1))
                dve.tensor_tensor(r(hid_l[0:rows(k), k % 3, :]), hidden[0:rows(k), k % 2, :], hid_h[0:rows(k), k % 3, :],
                                  ALU.subtract).then_inc(h_ok, 1)

            def add_block(tb, before_it):
                dve.wait_ge(added, tb * N1 + (0 if before_it else N1))
                for b in range(2):
                    x = x2[:, bass.ds(tb * 4 + (2 * b - 4 * before_it), 2), :].rearrange("p i d -> p (i d)")
                    o = dve.tensor_tensor(x, x, banks[6 + b][:, :], ALU.add)
                o.then_inc(o_read, 1)

            def body(tb, first, last):
                for c in range(N1):
                    if c == 0 and not first:
                        low(tb, -1)
                    dve.wait_ge(sg_ok, tb * N1 + (c + 1))
                    if c < NC:
                        dve.wait_ge(v_ps, tb * NC + (c + 1))
                    if not first or c >= 2:
                        dve.wait_ge(h_ok, tb * N1 + (before(c) + 1))
                    h = hidden[0:rows(c), c % 2, :]
                    dve.tensor_tensor(h, silu[0:rows(c), c % 2, :], banks[2 * (c % 2) + (c < NC)][0:rows(c), :], ALU.mult)\
                       .then_inc(product_ok, 1)
                    dve.wait_ge(product_ok, tb * N1 + (c + 1))
                    if c < NC:
                        dve.wait_ge(w_ps, tb * NC + (c + 1))
                        dve.tensor_tensor(h, h, banks[4 + c % 2][:, :], ALU.mult).then_inc(weighted_ok, 1)
                    if c:
                        low(tb, c - 1)
                    if c == 1 and not first:
                        add_block(tb, True)
                if last:
                    low(tb, NC)
                    add_block(tb, False)
            blocks(dve, body)


def decoder_layer(nc, tensors, out):
    of = lambda prefix: {n[len(prefix):]: a for n, a in tensors.items() if n.startswith(prefix)}
    with ExitStack() as ctx:
        ident = ctx.enter_context(nc.sbuf_tensor("ident", [P, P], F32))
        ones = ctx.enter_context(nc.sbuf_tensor("ones", [P, P], F32))
        x1 = ctx.enter_context(nc.sbuf_tensor("x1", [P, TT, DM], F32))
        memory(nc, dict(of("L0_attn_"), x=tensors["x"]), x1, ident, ones)
        ew = expert_weights(nc, ctx)
        with ExitStack() as c:
            cross_attention(nc, c, x1, dict(of("L0_xattn_"), ctx=tensors["ctx_2048"]), ident,
                            lambda sp: load_expert_weights(sp, ew, of("L0_ffn_")))
        with ExitStack() as c:
            layernorm(nc, c, x1, "ln2")
        with ExitStack() as c:
            experts(nc, c, x1, ew, of("L0_ffn_"), ident)
        with ExitStack() as c:
            layernorm(nc, c, x1, "ln3", out.rearrange("b s d -> (b s) d").rearrange("(i p) d -> p i d", p=P))


_INS = ["x", "ctx_2048", "L0_attn_Wk", "L0_attn_Wv", "L0_attn_Wq", "L0_attn_fast_lambda", "L0_attn_slow_lambda",
        "L0_attn_Waf", "L0_attn_baf", "L0_attn_Was", "L0_attn_bas", "L0_attn_nm_w1", "L0_attn_nm_b1",
        "L0_attn_nm_w2", "L0_attn_nm_b2", "L0_attn_ir_w1", "L0_attn_ir_b1", "L0_attn_ir_w2", "L0_attn_ir_b2",
        "L0_attn_pw_w", "L0_attn_pw_b", "L0_attn_Wo", "L0_attn_norm_w", "L0_xattn_Wq", "L0_xattn_Wkv",
        "L0_xattn_Wout", "L0_xattn_bout", "L0_ffn_w_gate", "L0_ffn_w_shared_up", "L0_ffn_w_shared_down",
        "L0_ffn_w_up", "L0_ffn_w_down"]


def kernel(**inputs):
    import numpy as _np
    import concourse.bacc as _bacc
    from concourse import mybir as _mybir
    from concourse.bass_utils import run_bass_kernel_spmd as _run

    nc = _bacc.Bacc("TRN2", target_bir_lowering=False, num_devices=1)
    arrays, tensors = {}, {}
    for name in _INS:
        a = _np.ascontiguousarray(inputs[name])
        arrays[f"in_{name}_dram"] = a
        tensors[name] = nc.dram_tensor(f"in_{name}_dram", a.shape, _mybir.dt.from_np(a.dtype), kind="ExternalInput").ap()
    out = nc.dram_tensor("out_0_dram", (NB, NS, DM), _mybir.dt.float32, kind="ExternalOutput").ap()
    decoder_layer(nc, tensors, out)
    r = _run(nc, [arrays], core_ids=[0])
    return r.results[0]["out_0_dram"]
```
